# Optimizing a Trainium2 kernel written in Bass

```python
import numpy as np
import jax
import jax.numpy as jnp

def _softmax(x, axis=-1):
    return jax.nn.softmax(x, axis=axis)

def _gelu(x):
    return jax.nn.gelu(x, approximate=True)

def _silu(x):
    return jax.nn.silu(x)

def _sigmoid(x):
    return jax.nn.sigmoid(x)

def _layernorm(x, axis=-1, eps=1e-05):
    m = jnp.mean(x, axis=axis, keepdims=True)
    v = jnp.var(x, axis=axis, keepdims=True)
    return (x - m) / jnp.sqrt(v + eps)

def _scatter_add(tgt, idx, src, axis=0):
    return tgt.at[idx].add(src)

def _segment_sum(src, seg, n):
    return jax.ops.segment_sum(src, seg, n)
kernel_name = 'mk_perceiver_d1_seqx_r8_f3d151'

def setup_inputs(seed: int=0):
    np.random.seed(seed)
    _w = jnp.asarray

    def _rec_inputs():
        import jax
        import jax.numpy as jnp
        _rk = jax.random.key(seed)
        x = -0.0002928 + 1 * jax.random.normal(jax.random.fold_in(_rk, 1), (32, 32, 256), jnp.float32)
        _lenS = 32 - jax.random.randint(jax.random.fold_in(_rk, 7), (32,), 0, max(1, 32 // 4) + 1, jnp.int32)
        _lenS2 = 257 - jax.random.randint(jax.random.fold_in(_rk, 8), (32,), 0, max(1, 257 // 4) + 1, jnp.int32)
        _ctx_512P = jax.random.normal(jax.random.fold_in(_rk, 11), (32, 16, 64), jnp.float32)
        _ctx_512c = jax.random.dirichlet(jax.random.fold_in(_rk, 511), 0.3 * jnp.ones((16,), jnp.float32), (32, 257))
        _ctx_512t = jnp.einsum('bsk,bkd->bsd', _ctx_512c, _ctx_512P)
        _ctx_512t = _ctx_512t * jax.lax.rsqrt(jnp.mean(jnp.square(_ctx_512t)) + 1e-12) * 0.953939
        ctx_512 = 0.000227908 + 0.99994 * (_ctx_512t + 0.3 * jax.random.normal(jax.random.fold_in(_rk, 611), (32, 257, 64), jnp.float32))
        return (x, ctx_512)
    x, ctx_512 = _rec_inputs()

    def _L0_xattn_setup():
        import jax, jax.numpy as jnp
        import numpy as np
        B, S, L = (2, 128, 128)
        DIM_Q, H, K, D_C, D_CQ, R = (256, 16, 128, 64, 192, 64)

        def _rope_tables(seq_len, dim, dtype):
            inv_freq = 1.0 / 10000.0 ** (jnp.arange(0, dim, 2, dtype=dtype) / dim)
            t = jnp.arange(seq_len, dtype=dtype)
            freqs = t[:, None] * inv_freq[None, :]
            sin = jnp.repeat(jnp.sin(freqs), 2, axis=-1)
            cos = jnp.repeat(jnp.cos(freqs), 2, axis=-1)
            return (sin, cos)

        def _rotate_half(x):
            h = x.shape[-1] // 2
            return jnp.concatenate([-x[..., h:], x[..., :h]], axis=-1)
        key = jax.random.key(seed)
        ks = jax.random.split(key, 8)
        s_in = 1.0 / np.sqrt(DIM_Q)
        s_k = 1.0 / np.sqrt(K)
        s_cq = 1.0 / np.sqrt(D_CQ)
        s_c = 1.0 / np.sqrt(D_C)
        return {'hidden_q': jax.random.normal(ks[0], (B, S, DIM_Q), jnp.float32), 'kv_c': jax.random.normal(ks[1], (B, L, D_C), jnp.float32), 'Wq': jax.random.normal(ks[2], (H * K, DIM_Q), jnp.float32) * s_in, 'w_kc_q': jax.random.normal(ks[3], (H, K, D_CQ), jnp.float32) * s_k, 'w_kc_kv': jax.random.normal(ks[4], (H, K, D_C), jnp.float32) * s_k, 'W_qr': jax.random.normal(ks[5], (H, D_CQ, R), jnp.float32) * s_cq / np.sqrt(R), 'W_kr': jax.random.normal(ks[6], (H, D_C, R), jnp.float32) * s_c, 'Wo': jax.random.normal(ks[7], (DIM_Q, H * K), jnp.float32) * s_k}
    _L0_xattn_all = _L0_xattn_setup()
    _L0_xattn_in = {k: v for k, v in _L0_xattn_all.items() if k in ('Wq', 'w_kc_q', 'w_kc_kv', 'W_qr', 'W_kr', 'Wo')}
    del _L0_xattn_all

    def _L0_attn_setup():
        import jax, jax.numpy as jnp
        import numpy as np
        BLOCK = 32
        NUM_HEADS = 16
        HEAD_DIM = 128
        FP4_GRID = jnp.array([0.0, 0.5, 1.0, 1.5, 2.0, 3.0, 4.0, 6.0], dtype=jnp.float32)

        def quantize_to_mxfp4(w, block_size=BLOCK):
            D, F = w.shape
            blocks = w.reshape(D // block_size, block_size, F)
            amax = jnp.max(jnp.abs(blocks), axis=1)
            e = jnp.floor(jnp.log2(jnp.maximum(amax, 1e-12) / 6.0))
            scale = jnp.exp2(e)
            v = blocks / scale[:, None, :]
            idx = jnp.argmin(jnp.abs(jnp.abs(v)[..., None] - FP4_GRID), axis=-1)
            codes = jnp.sign(v) * FP4_GRID[idx]
            return (codes.reshape(D, F).astype(jnp.float32), scale.astype(jnp.float32))

        def _mxfp4_matmul(x, codes, scales, block_size=BLOCK):
            w = codes * jnp.repeat(scales, block_size, axis=0)
            return x @ w
        key = jax.random.key(seed)
        ks = jax.random.split(key, 9)
        B, S, D = (2, 256, 256)
        feat = NUM_HEADS * HEAD_DIM
        x = jax.random.normal(ks[0], (B, S, D), dtype=jnp.float32)

        def make_w(k, din, dout):
            w = jax.random.normal(k, (din, dout), dtype=jnp.float32) * (1.0 / np.sqrt(din))
            return quantize_to_mxfp4(w, BLOCK)
        wq_codes, wq_scales = make_w(ks[1], D, feat)
        wk_codes, wk_scales = make_w(ks[2], D, feat)
        wv_codes, wv_scales = make_w(ks[3], D, feat)
        wo_codes, wo_scales = make_w(ks[4], feat, D)
        bq = jnp.zeros((feat,), jnp.float32)
        bk = jnp.zeros((feat,), jnp.float32)
        bv = jnp.zeros((feat,), jnp.float32)
        bo = jnp.zeros((D,), jnp.float32)
        return {'x': x, 'wq_codes': wq_codes, 'wq_scales': wq_scales, 'bq': bq, 'wk_codes': wk_codes, 'wk_scales': wk_scales, 'bk': bk, 'wv_codes': wv_codes, 'wv_scales': wv_scales, 'bv': bv, 'wo_codes': wo_codes, 'wo_scales': wo_scales, 'bo': bo}
    _L0_attn_all = _L0_attn_setup()
    _L0_attn_in = {k: v for k, v in _L0_attn_all.items() if k in ('wq_codes', 'wq_scales', 'bq', 'wk_codes', 'wk_scales', 'bk', 'wv_codes', 'wv_scales', 'bv', 'wo_codes', 'wo_scales', 'bo')}
    del _L0_attn_all

    def _L0_ffn_setup():
        import jax, jax.numpy as jnp
        import numpy as np
        TOP_K = 8
        CAPACITY = 128
        key = jax.random.key(seed)
        k1, k2, k3, k4 = jax.random.split(key, 4)
        B, S, H, E, I = (2, 128, 256, 64, 96)
        hidden_states = jax.random.normal(k1, (B, S, H), dtype=jnp.float32)
        router_weight = jax.random.normal(k2, (E, H), dtype=jnp.float32) * 0.02
        gate_up_proj = jax.random.normal(k3, (E, H, 2 * I), dtype=jnp.float32) * 0.02
        down_proj = jax.random.normal(k4, (E, I, H), dtype=jnp.float32) * 0.02
        return {'hidden_states': hidden_states, 'router_weight': router_weight, 'gate_up_proj': gate_up_proj, 'down_proj': down_proj}
    _L0_ffn_all = _L0_ffn_setup()
    _L0_ffn_in = {k: v for k, v in _L0_ffn_all.items() if k in ('router_weight', 'gate_up_proj', 'down_proj')}
    del _L0_ffn_all
    return {'x': x, 'ctx_512': ctx_512, 'L0_xattn_Wq': _L0_xattn_in['Wq'], 'L0_xattn_w_kc_q': _L0_xattn_in['w_kc_q'], 'L0_xattn_w_kc_kv': _L0_xattn_in['w_kc_kv'], 'L0_xattn_W_qr': _L0_xattn_in['W_qr'], 'L0_xattn_W_kr': _L0_xattn_in['W_kr'], 'L0_xattn_Wo': _L0_xattn_in['Wo'], 'L0_attn_wq_codes': _L0_attn_in['wq_codes'], 'L0_attn_wq_scales': _L0_attn_in['wq_scales'], 'L0_attn_bq': _L0_attn_in['bq'], 'L0_attn_wk_codes': _L0_attn_in['wk_codes'], 'L0_attn_wk_scales': _L0_attn_in['wk_scales'], 'L0_attn_bk': _L0_attn_in['bk'], 'L0_attn_wv_codes': _L0_attn_in['wv_codes'], 'L0_attn_wv_scales': _L0_attn_in['wv_scales'], 'L0_attn_bv': _L0_attn_in['bv'], 'L0_attn_wo_codes': _L0_attn_in['wo_codes'], 'L0_attn_wo_scales': _L0_attn_in['wo_scales'], 'L0_attn_bo': _L0_attn_in['bo'], 'L0_ffn_router_weight': _L0_ffn_in['router_weight'], 'L0_ffn_gate_up_proj': _L0_ffn_in['gate_up_proj'], 'L0_ffn_down_proj': _L0_ffn_in['down_proj']}

def reference(x, ctx_512, L0_xattn_Wq, L0_xattn_w_kc_q, L0_xattn_w_kc_kv, L0_xattn_W_qr, L0_xattn_W_kr, L0_xattn_Wo, L0_attn_wq_codes, L0_attn_wq_scales, L0_attn_bq, L0_attn_wk_codes, L0_attn_wk_scales, L0_attn_bk, L0_attn_wv_codes, L0_attn_wv_scales, L0_attn_bv, L0_attn_wo_codes, L0_attn_wo_scales, L0_attn_bo, L0_ffn_router_weight, L0_ffn_gate_up_proj, L0_ffn_down_proj):
    import jax
    import jax.numpy as jnp

    def _L0_xattn_ref(hidden_q, kv_c, Wq, w_kc_q, w_kc_kv, W_qr, W_kr, Wo):
        import jax, jax.numpy as jnp
        import numpy as np
        B, S, L = (2, 128, 128)
        DIM_Q, H, K, D_C, D_CQ, R = (256, 16, 128, 64, 192, 64)

        def _rope_tables(seq_len, dim, dtype):
            inv_freq = 1.0 / 10000.0 ** (jnp.arange(0, dim, 2, dtype=dtype) / dim)
            t = jnp.arange(seq_len, dtype=dtype)
            freqs = t[:, None] * inv_freq[None, :]
            sin = jnp.repeat(jnp.sin(freqs), 2, axis=-1)
            cos = jnp.repeat(jnp.cos(freqs), 2, axis=-1)
            return (sin, cos)

        def _rotate_half(x):
            h = x.shape[-1] // 2
            return jnp.concatenate([-x[..., h:], x[..., :h]], axis=-1)
        b, s, _ = hidden_q.shape
        l = kv_c.shape[1]
        q_hk = (hidden_q @ Wq.T).reshape(b, s, H, K)
        q_big = jnp.einsum('bshk,hkq->bshq', q_hk, w_kc_q)
        sin, cos = _rope_tables(l, D_C, kv_c.dtype)
        kv_rope = kv_c * cos[None] + _rotate_half(kv_c) * sin[None]
        q_r = jnp.einsum('bshq,hqr->bhsr', q_big, W_qr)
        k_r = jnp.einsum('bld,hdr->bhlr', kv_rope, W_kr)
        scores = jnp.einsum('bhsr,bhlr->bhsl', q_r, k_r)
        attn = jax.nn.softmax(scores, axis=-1)
        ctx_c = jnp.einsum('bhsl,bld->bhsd', attn, kv_rope)
        ctx_lat = jnp.einsum('bhsd,hkd->bshk', ctx_c, w_kc_kv)
        out = ctx_lat.reshape(b, s, H * K) @ Wo.T
        return out

    def _L0_attn_ref(x, wq_codes, wq_scales, bq, wk_codes, wk_scales, bk, wv_codes, wv_scales, bv, wo_codes, wo_scales, bo):
        import jax, jax.numpy as jnp
        import numpy as np
        BLOCK = 32
        NUM_HEADS = 16
        HEAD_DIM = 128
        FP4_GRID = jnp.array([0.0, 0.5, 1.0, 1.5, 2.0, 3.0, 4.0, 6.0], dtype=jnp.float32)

        def quantize_to_mxfp4(w, block_size=BLOCK):
            D, F = w.shape
            blocks = w.reshape(D // block_size, block_size, F)
            amax = jnp.max(jnp.abs(blocks), axis=1)
            e = jnp.floor(jnp.log2(jnp.maximum(amax, 1e-12) / 6.0))
            scale = jnp.exp2(e)
            v = blocks / scale[:, None, :]
            idx = jnp.argmin(jnp.abs(jnp.abs(v)[..., None] - FP4_GRID), axis=-1)
            codes = jnp.sign(v) * FP4_GRID[idx]
            return (codes.reshape(D, F).astype(jnp.float32), scale.astype(jnp.float32))

        def _mxfp4_matmul(x, codes, scales, block_size=BLOCK):
            w = codes * jnp.repeat(scales, block_size, axis=0)
            return x @ w
        B, S, D = x.shape
        q = _mxfp4_matmul(x, wq_codes, wq_scales) + bq
        k = _mxfp4_matmul(x, wk_codes, wk_scales) + bk
        v = _mxfp4_matmul(x, wv_codes, wv_scales) + bv
        q = q.reshape(B, S, NUM_HEADS, HEAD_DIM)
        k = k.reshape(B, S, NUM_HEADS, HEAD_DIM)
        v = v.reshape(B, S, NUM_HEADS, HEAD_DIM)
        scores = jnp.einsum('bqhd,bkhd->bhqk', q, k) / jnp.sqrt(jnp.float32(HEAD_DIM))
        attn = jax.nn.softmax(scores, axis=-1)
        out = jnp.einsum('bhqk,bkhd->bqhd', attn, v).reshape(B, S, NUM_HEADS * HEAD_DIM)
        return _mxfp4_matmul(out, wo_codes, wo_scales) + bo

    def _L0_ffn_ref(hidden_states, router_weight, gate_up_proj, down_proj):
        import jax, jax.numpy as jnp
        import numpy as np
        TOP_K = 8
        CAPACITY = 128
        B, S, H = hidden_states.shape
        E = router_weight.shape[0]
        K, C = (TOP_K, CAPACITY)
        x = hidden_states.reshape(-1, H)
        logits = x @ router_weight.T
        probs = jax.nn.softmax(logits, axis=-1)
        topw, topi = jax.lax.top_k(probs, K)
        topw = topw / jnp.sum(topw, axis=-1, keepdims=True)
        flat_e = topi.reshape(-1)
        oh = jax.nn.one_hot(flat_e, E, dtype=jnp.int32)
        pos = jnp.take_along_axis(jnp.cumsum(oh, axis=0), flat_e[:, None], axis=1)[:, 0] - 1
        x_rep = jnp.repeat(x, K, axis=0)
        xe = jnp.zeros((E, C, H), x.dtype).at[flat_e, pos].set(x_rep, mode='drop')
        gu = jnp.einsum('ech,ehf->ecf', xe, gate_up_proj)
        g, u = jnp.split(gu, 2, axis=-1)
        h = jax.nn.silu(g) * u
        ye = jnp.einsum('eci,eih->ech', h, down_proj)
        valid = pos < C
        y_flat = jnp.where(valid[:, None], ye[flat_e, jnp.minimum(pos, C - 1)], 0.0)
        y = jnp.sum(y_flat.reshape(-1, K, H) * topw.reshape(-1, K)[..., None], axis=1)
        return y.reshape(B, S, H)
    x = x + _L0_xattn_ref(_layernorm(x, axis=-1), ctx_512, L0_xattn_Wq, L0_xattn_w_kc_q, L0_xattn_w_kc_kv, L0_xattn_W_qr, L0_xattn_W_kr, L0_xattn_Wo)
    x = x + _L0_attn_ref(_layernorm(x, axis=-1), L0_attn_wq_codes, L0_attn_wq_scales, L0_attn_bq, L0_attn_wk_codes, L0_attn_wk_scales, L0_attn_bk, L0_attn_wv_codes, L0_attn_wv_scales, L0_attn_bv, L0_attn_wo_codes, L0_attn_wo_scales, L0_attn_bo)
    x = x + _L0_ffn_ref(_layernorm(x, axis=-1), L0_ffn_router_weight, L0_ffn_gate_up_proj, L0_ffn_down_proj)
    return x

_drawn_inputs = setup_inputs


def setup_inputs(seed=0):
    import zlib

    import numpy as np

    out = dict(_drawn_inputs(seed))
    spreads = {'L0_attn_bq': (0.0, 0.8),
     'L0_attn_bk': (0.0, 0.8),
     'L0_attn_bv': (0.0, 0.1),
     'L0_attn_bo': (0.0, 0.1)}
    factors = {'L0_attn_wq_scales': 4.77,
     'L0_attn_wk_scales': 4.783,
     'L0_ffn_router_weight': 8.0,
     'L0_ffn_gate_up_proj': 8.0,
     'L0_ffn_down_proj': 8.0}
    for name, (base, spread) in spreads.items():
        noise = np.random.default_rng([zlib.crc32(name.encode()), seed]).standard_normal(out[name].shape)
        drawn = base * np.exp(spread * noise) if base else spread * noise
        out[name] = jnp.asarray(drawn.astype(out[name].dtype))
    for name, factor in factors.items():
        out[name] = (out[name] * factor).astype(out[name].dtype)
    return out
```

```python
import concourse.bass as bass
from concourse import mybir
from contextlib import ExitStack

B, S, D = 32, 32, 256
NL, DC, DQ, R = 257, 64, 192, 64
H, HD = 16, 128
F = H * HD
E, I, TOPK, CAP = 64, 96, 8, 128

P = 128
T = B * S // P
BT = P // S
DCH = D // P
HP = H // 2
ROWS = BT * H * S // P
RB = ROWS // BT
QC = DQ // 2
GH = 4
GROUPS = H // GH
NOSLOT = E * CAP

XS = ["hT", "qa", "qb", "kt0", "kt1", "cT0", "kt2", "cT1", "kt3", "cT2", "cT3", "out"]
SS = ["hT", "q0", "q1", "q2", "q3", "k0", "k1", "k2", "k3", "sc", "v0", "v1", "v2", "v3",
      "pv0", "pv1", "pv2", "pv3", "wo", "rT", "log", "pos"]
BEHIND = {0: ["k0", "k1"], 1: ["k2", "k3"], 2: ["sc"], 3: ["v0"], 4: ["v1"], 5: ["v2"], 6: ["v3"],
          7: ["pv0"], 8: ["pv1"], 9: ["pv2"], 10: ["pv3"], 11: ["wo"], 13: ["rT"], 15: ["log"], 18: ["pos"]}
X_AT = {2: ["kt1"], 6: ["cT0", "kt2"], 10: ["cT1", "kt3"], 14: ["cT2"], 18: ["cT3"], 19: ["out"]}
STEPS = ROWS + 4
NEWTON = 3
NLINKS = 5 + 3 * NEWTON
XLINKS = 2 * NLINKS + 2 * BT
SLINKS = NLINKS + 16
NB = 8
FREE = 1


def build(nc, x, ctx_in, Wq, kcq, kckv, Wqr, Wkr, Wo_x, codes, scales, bq, bk, bv, bo, rw, gup, dnp,
          rope_cos, rope_sin, out):
    f32, bf16, u32 = mybir.dt.float32, mybir.dt.bfloat16, mybir.dt.uint32
    ALU, ACT, AX = mybir.AluOpType, mybir.ActivationFunctionType, mybir.AxisListType

    ctx = ExitStack()
    with ctx:
        def sb(name, shape, dt=f32):
            return ctx.enter_context(nc.sbuf_tensor(name, shape, dt))

        def sem(name):
            return ctx.enter_context(nc.semaphore(name))

        bank = [ctx.enter_context(nc.psum_tensor(f"bank{n}", [P, 512], f32)) for n in range(8)]
        XE = nc.dram_tensor("expert_rows", [E * CAP, D], f32, kind="Internal").ap()
        YE = nc.dram_tensor("expert_out", [E * CAP + 1, D], f32, kind="Internal").ap()

        ident = sb("ident", [P, P])
        before = sb("before", [P, P], bf16)
        ones16 = sb("ones16", [P, P], bf16)
        iota_i = sb("iota_i", [P, E], mybir.dt.int32)
        iota_e = sb("iota_e", [P, E])
        slot0 = sb("slot0", [P, E])
        X = sb("X", [P, T, D])
        M = sb("M", [P, DCH, H * DC])
        N = sb("N", [P, HP, D])
        W = sb("W", [P, 8, 2048])
        bqk = sb("bqk", [P, 2, H])
        bvT = sb("bvT", [P, H])
        bo_row = sb("bo_row", [1, D])
        obias = sb("obias", [P, D])
        onerow = sb("onerow", [1, P])
        rwT = sb("rwT", [P, DCH, E])
        cosT = sb("cosT", [P, 3, DC])
        sinT = sb("sinT", [P, 3, DC])

        C = sb("C", [P, BT, 3, DC])
        Ct = sb("Ct", [P, BT, 3, DC])
        Cr = sb("Cr", [P, BT, 3, 2, DC])
        KT = sb("KT", [P, 2, NL])
        h1 = sb("h1", [P, D])
        h1T = sb("h1T", [P, DCH, P])
        qT = sb("qT", [P, BT, HP, S])
        pr = sb("pr", [P, 2 * RB, NL])
        pT = sb("pT", [P, 2, 2, P])
        nmax = sb("nmax", [P, 2 * RB])
        rsum = sb("rsum", [P, 2 * RB])
        rinv = sb("rinv", [P, 2 * RB])
        On = sb("On", [P, 2, RB, DC])
        cT = sb("cT", [P, HP, P])
        st1 = sb("st1", [P, 6])
        mv1 = sb("mv1", [P, 2])
        rs1 = sb("rs1", [P, 2])
        rwr = h1[0:E, :]

        SPACE = 4 * 2048 + 2 * 256 + 512 + 2 * 512
        space = sb("space", [P, SPACE])
        at = [0]

        def cut(n, parts=P):
            a = at[0]
            at[0] += n
            assert at[0] <= SPACE
            return space[0:parts, a:a + n]

        fWq = [cut(GH * D).rearrange("p (h d) -> p h d", h=GH) for _ in range(2)]
        fkq = [cut(GH * DQ).rearrange("p (h d) -> p h d", h=GH) for _ in range(2)]
        fqr = [cut(GH * 2 * R, QC).rearrange("p (h c d) -> p h c d", h=GH, c=2) for _ in range(2)]
        fkr = [cut(GH * R, DC).rearrange("p (h d) -> p h d", h=GH) for _ in range(2)]
        fkv = [cut(GH * DC).rearrange("p (h d) -> p h d", h=GH) for _ in range(2)]
        fWo = [cut(DCH * GH * HD).rearrange("p (c h d) -> p c h d", c=DCH, h=GH) for _ in range(2)]
        fqrT = cut(GH * 2 * QC, R).rearrange("p (h c d) -> p h c d", h=GH, c=2)
        fkrT = cut(GH * DC, R).rearrange("p (h d) -> p h d", h=GH)
        fWoT = cut(GH * D).rearrange("p (h d) -> p h d", h=GH)
        fkqT = qT[0:QC].rearrange("p b c s -> p (b c s)").rearrange("p (h c d) -> p h c d", h=GH, c=2)
        cflat = cT[:, :, :].rearrange("p a b -> p (a b)")
        fG = cflat[0:QC, 0:GH * 2 * DC].rearrange("p (h c d) -> p h c d", h=GH, c=2)
        fQ = cflat[:, 512:512 + GH * DC].rearrange("p (h d) -> p h d", h=GH)
        at[0] = 0
        qS = cut(H * P).rearrange("p (h t) -> p h t", h=H)
        kS = cut(H * P).rearrange("p (h t) -> p h t", h=H)
        V = cut(F)
        oT = cut(H * P).rearrange("p (h t) -> p h t", h=H)
        h2T = cut(DCH * P).rearrange("p (c t) -> p c t", c=DCH)
        h3T = cut(DCH * P).rearrange("p (c t) -> p c t", c=DCH)
        sS = cut(H * S).rearrange("p (h t) -> p h t", h=H)
        oh = cut(TOPK * E).rearrange("p (k e) -> p k e", k=TOPK)
        oh2 = cut(TOPK * E).rearrange("p (k e) -> p k e", k=TOPK)
        diag = sb("diag", [P, H, P])
        h2 = sb("h2", [P, D])
        h3 = sb("h3", [P, D])
        st2 = sb("st2", [P, 6])
        mv2 = sb("mv2", [P, 2])
        rs2 = sb("rs2", [P, 2])
        smax = sb("smax", [P, H])
        ssum = sb("ssum", [P, H])
        sinv = sb("sinv", [P, H])
        lg = sb("lg", [P, E])
        top = sb("top", [P, TOPK])
        topi = sb("topi", [P, TOPK], u32)
        topf = sb("topf", [P, TOPK])
        ntop = sb("ntop", [P, 1])
        etop = sb("etop", [P, TOPK])
        esum = sb("esum", [P, 1])
        einv = sb("einv", [P, 1])
        mask = sb("mask", [P, E], bf16)
        count = sb("count", [P, E], bf16)
        sv = sb("sv", [P, E])
        sv2 = sb("sv2", [P, E])
        slotf = sb("slotf", [P, TOPK])
        slot = sb("slot", [P, TOPK], u32)
        slots = sb("slots", [P, T, TOPK], u32)
        wts = sb("wts", [P, T, TOPK])

        ring = sb("ring", [P, NB * (DCH * 2 * I + D)])
        gu = ring[:, 0:NB * DCH * 2 * I].rearrange("p (n c f) -> p n c f", n=NB, c=DCH)
        dn = ring[0:I, NB * DCH * 2 * I:].rearrange("p (n d) -> p n d", n=NB)
        scl = ring[:, 0:4096].rearrange("p (n f) -> p n f", n=2)
        Wf = W[:, :, :].rearrange("p u f -> p (u f)")
        xe = Wf[:, 0:2048].rearrange("p (n d) -> p n d", n=NB)
        xeT = Wf[:, 2048:2560].rearrange("p (n c t) -> p n c t", n=2, c=DCH)
        sg = Wf[0:I, 2560:2816].rearrange("p (n t) -> p n t", n=2)
        hh = Wf[0:I, 2816:3072].rearrange("p (n t) -> p n t", n=2)
        ye = Wf[:, 3072:4096].rearrange("p (n d) -> p n d", n=4)
        got = Wf[:, 4096:8192].rearrange("p (n k d) -> p n k d", n=2, k=TOPK)
        gslot = sb("gslot", [P, 2, TOPK], u32)

        x_in, tab_in, rw_in, bias_in, ctx_ld, zero_out = (sem(n) for n in (
            "x_in", "tables_in", "router_in", "biases_in", "context_in", "zero_out"))
        fold_in = [sem("fold_in0"), sem("fold_in1")]
        w_in = [sem("w_in0"), sem("w_in1")]
        ew_in = [sem(f"expert_weights_in{n}") for n in range(NB)]
        xe_in = [sem(f"expert_rows_in{n}") for n in range(NB)]
        ye_out = [sem(f"expert_out{n}") for n in range(4)]
        got_in = [sem("gathered0"), sem("gathered1")]
        scat, h3_free, stored = sem("scattered"), sem("h3_free"), sem("stored")
        consts, iotas, zeroed, pool_link, rw_t, rwT_ready, ob_mm, ob_ready, w_done = (sem(n) for n in (
            "consts", "iotas", "zeroed", "pool_link", "router_transposed", "rwT_ready", "obias_summed",
            "obias_ready", "w_dequantised"))
        f_t, f_ta, f_td, f_g, f_gd, f_n, f_na, f_q, f_qd, f_m, f_md = (sem(n) for n in (
            "f_transposed", "f_act_copied", "f_dve_copied", "f_G", "f_G_copied", "f_N", "f_N_copied",
            "f_Q", "f_Q_copied", "f_M", "f_M_copied"))
        xf = [sem("x_filled0"), sem("x_filled1")]
        xd = [sem("x_drained0"), sem("x_drained1")]
        x_link, h1_ready, rope_link, roped, scored, maxed, expd, transposed, pt_ready, summed, last_ready, on_ready = (
            sem(n) for n in ("x_link", "h1_ready", "rope_link", "roped", "scored", "maxed", "expd", "transposed",
                             "pt_ready", "summed", "last_ready", "on_ready"))
        sf = [sem("s_filled0"), sem("s_filled1")]
        sd = [sem("s_drained0"), sem("s_drained1")]
        s_link, h2_ready, shifted, s_expd, diag_ready, h3_ready, top_ready, e_ready, mask_ready, slot_ready = (
            sem(n) for n in ("s_link", "h2_ready", "shifted", "s_expd", "diag_ready", "h3_ready", "top_ready",
                             "e_ready", "mask_ready", "slot_ready"))
        e_t, e_tc, e_gu, e_silu, e_h, e_dn, e_ye = (sem(n) for n in (
            "e_transposed", "e_xT_ready", "e_gate_up", "e_silu", "e_hidden", "e_down", "e_out_ready"))
        gs_ready, y_link, y_ready = (sem(n) for n in ("gather_slots_ready", "y_link", "y_ready"))

        passed = sem("passed")

        def alone(e):
            e.sem_inc(passed, 1)

        block = ctx.enter_context(nc.Block())
        XBANK = (bank[4], bank[5])
        SBANK = (bank[6], bank[7])

        def xpos(name, i, more=1):
            n = XS.index(name)
            return n % 2, i * (len(XS) // 2) + n // 2 + more

        def spos(name, j, more=1):
            n = SS.index(name)
            return n % 2, j * (len(SS) // 2) + n // 2 + more

        def wait_pos(e, sems, pos):
            e.wait_ge(sems[pos[0]], pos[1] + (FREE if sems in (xd, sd) else 0))

        @block.sync
        def _(e):
            e.dma_start(X[:, :, :], x.rearrange("(t p) d -> p t d", p=P)).then_inc(x_in, 16)
            e.sem_inc(f_m, FREE)
            with e.Fori(0, GROUPS // 2) as j:
                for half in range(2):
                    g = j * 2 + half
                    e.wait_ge(f_m, j * 2 + FREE)
                    hs = bass.ds(g * GH, GH)
                    fs = bass.ds(g * (GH * HD), GH * HD)
                    for c in range(DCH):
                        e.dma_start(fWo[half][:, c], Wo_x[c * P:(c + 1) * P, fs].rearrange("p (h k) -> p h k", h=GH)).then_inc(fold_in[half], 16)
                        e.dma_start(fqr[half][:, :, c], Wqr[hs, c * QC:(c + 1) * QC, :].rearrange("h q r -> q h r")).then_inc(fold_in[half], 16)
                    e.dma_start(fkq[half], kcq[hs].rearrange("h k q -> k h q")).then_inc(fold_in[half], 16)
                    e.dma_start(fkr[half], Wkr[hs].rearrange("h d r -> d h r")).then_inc(fold_in[half], 16)
                    e.dma_start(fWq[half], Wq[fs, :].rearrange("(h k) d -> k h d", h=GH)).then_inc(fold_in[half], 16)
                    e.dma_start(fkv[half], kckv[hs].rearrange("h k d -> k h d")).then_inc(fold_in[half], 16)

            def load_context(i):
                bs = bass.ds(i * BT, BT)
                for c in range(2):
                    e.dma_start(C[:, :, c, :], ctx_in[bs, c * P:(c + 1) * P, :].rearrange("b p d -> p b d")).then_inc(ctx_ld, 16)
                e.dma_start(C[:, :, 2, :], ctx_in[bs, 2 * P, :].unsqueeze(0).to_broadcast([P, BT, DC])).then_inc(ctx_ld, 16)

            load_context(0)
            for u in range(8):
                if u >= 2:
                    e.wait_ge(w_done, u - 1)
                w, c = u // 2, u % 2
                if w < 3:
                    e.dma_start(W[:, u], codes[w][c * P:(c + 1) * P, :]).then_inc(w_in[u % 2], 16)
                    for q in range(4):
                        e.dma_start(scl[32 * q:32 * q + 32, u % 2],
                                    scales[w][4 * c + q:4 * c + q + 1, :].to_broadcast([32, F])).then_inc(w_in[u % 2], 16)
                else:
                    hs = slice(8 * c, 8 * c + 8)
                    e.dma_start(W[:, u].rearrange("p (h d) -> p h d", h=8),
                                codes[w].rearrange("(h p) d -> p h d", p=P)[:, hs]).then_inc(w_in[u % 2], 16)
                    for q in range(4):
                        e.dma_start(scl[32 * q:32 * q + 32, u % 2].rearrange("p (h d) -> p h d", h=8),
                                    scales[w].rearrange("(h q) d -> q h d", q=4)[q:q + 1, hs].to_broadcast([32, 8, D])
                                    ).then_inc(w_in[u % 2], 16)
            e.wait_ge(w_done, 8)

            def load_expert(ex, n):
                e.dma_start(gu[:, n], gup[bass.ds(ex, 1)].rearrange("o (c p) f -> p (o c) f", p=P)).then_inc(ew_in[n], 16)
                e.dma_start(dn[:, n], dnp[bass.ds(ex, 1)].rearrange("o i d -> i (o d)")).then_inc(ew_in[n], 16)

            def load_rows(ex, n):
                e.dma_start(xe[:, n], XE[bass.ds(ex * CAP, CAP), :]).then_inc(xe_in[n], 16)

            for n in range(NB):
                load_expert(n, n)
            with e.Fori(1, T) as i:
                e.wait_ge(roped, i * 2)
                load_context(i)
            e.wait_ge(h3_free, T + FREE)
            for n in range(NB):
                load_rows(n, n)
            with e.Fori(1, E // NB) as j:
                for n in range(NB):
                    e.wait_ge(e_dn, j * NB + (n + 1 - NB))
                    load_expert(j * NB + n, n)
                    load_rows(j * NB + n, n)
            with e.Fori(0, T) as t:
                e.wait_ge(y_ready, t + 1)
                e.dma_start(out[bass.ds(t * P, P), :], X[:, bass.ds(t, 1), :].rearrange("p o d -> p (o d)")).then_inc(stored, 16)
            e.wait_ge(stored, 16 * T)

        @block.gpsimd
        def _(e):
            links = [0]

            def link(ins):
                links[0] += 1
                ins.then_inc(pool_link, 1)
                e.wait_ge(pool_link, links[0])

            link(e.memset(ident[:, :], 0.0))
            e.affine_select(out=ident[:, :], in_=ident[:, :], compare_op=ALU.not_equal, fill=1.0, base=0,
                            pattern=[[-1, P]], channel_multiplier=1).then_inc(consts, 1)
            link(e.memset(ones16[:, :], 1.0))
            e.affine_select(out=before[:, :], in_=ones16[:, :], compare_op=ALU.is_gt, fill=0.0, base=0,
                            pattern=[[1, P]], channel_multiplier=-1).then_inc(consts, 1)
            e.memset(onerow[:, :], 1.0).then_inc(consts, 1)
            link(e.iota(iota_i[:, :], pattern=[[1, E]], base=0, channel_multiplier=0))
            link(e.tensor_copy(iota_e[:, :], iota_i[:, :]))
            e.tensor_scalar(slot0[:, :], iota_e[:, :], float(CAP), float(-NOSLOT), ALU.mult, ALU.add).then_inc(iotas, 1)
            e.wait_ge(tab_in, 16 * 2)

            def rope(i):
                e.wait_ge(ctx_ld, i * 48 + 48)
                half = DC // 2
                e.tensor_tensor(Ct[:, :, :, 0:half], C[:, :, :, half:DC],
                                sinT[:, :, 0:half].unsqueeze(1).to_broadcast([P, BT, 3, half]), ALU.mult).then_inc(rope_link, 1)
                e.tensor_tensor(Ct[:, :, :, half:DC], C[:, :, :, 0:half],
                                sinT[:, :, half:DC].unsqueeze(1).to_broadcast([P, BT, 3, half]), ALU.mult).then_inc(rope_link, 1)
                e.wait_ge(rope_link, i * 3 + 2)
                e.tensor_tensor(C[:, :, :, :], C[:, :, :, :],
                                cosT[:, :, :].unsqueeze(1).to_broadcast([P, BT, 3, DC]), ALU.mult).then_inc(rope_link, 1)
                e.wait_ge(rope_link, i * 3 + 3)
                e.wait_ge(summed, i * ROWS)
                e.wait_ge(last_ready, i * BT)
                for d in range(2):
                    e.tensor_tensor(Cr[:, :, :, d, :], C[:, :, :, :], Ct[:, :, :, :], ALU.add).then_inc(roped, 1)
                e.wait_ge(roped, i * 2 + 2)

            def last_rows(i, b):
                e.wait_ge(expd, i * ROWS + RB * (b + 1))
                if b >= 2:
                    wait_pos(e, xf, xpos(f"cT{b - 2}", i))
                else:
                    e.wait_ge(xf[1], i * (len(XS) // 2))
                e.tensor_tensor(On[:, b % 2], Cr[:, b, 2, 0, :].unsqueeze(1).to_broadcast([P, RB, DC]),
                                pr[:, RB * (b % 2):RB * (b % 2) + RB, NL - 1:NL].to_broadcast([P, RB, DC]),
                                ALU.mult).then_inc(last_ready, 1)

            def scatter(j):
                e.wait_ge(slot_ready, j + 1)
                alone(e)
                for k in range(TOPK):
                    e.indirect_dma_start(XE[:, :], bass.IndirectOffsetOnAxis(ap=slot[:, k:k + 1], axis=0), h3[:, :], None,
                                         bounds_check=E * CAP - 1, oob_is_err=False).then_inc(scat, 16)
                e.wait_ge(scat, j * (16 * TOPK) + 16 * TOPK)
                e.sem_inc(h3_free, 1)

            def dequantise(u):
                e.wait_ge(w_in[u % 2], 80 * (u // 2 + 1))
                e.tensor_tensor(W[:, u], W[:, u], scl[:, u % 2], ALU.mult).then_inc(w_done, 1)

            rope(0)
            for u in range(4):
                dequantise(u)
            for b in range(BT):
                last_rows(0, b)
            for u in range(4, 8):
                dequantise(u)
            e.wait_ge(zero_out, 32)
            with e.Fori(0, T - 1) as j:
                rope(j + 1)
                for b in range(BT):
                    last_rows(j + 1, b)
                scatter(j)
            scatter(T - 1)
            with e.Fori(0, E // NB) as j:
                for n in range(NB):
                    e.wait_ge(e_ye, j * NB + n + 1)
                    alone(e)
                    e.dma_start(YE[bass.ds(j * (NB * CAP) + n * CAP, CAP), :], ye[:, n % 4]).then_inc(ye_out[n % 4], 16)
            for n in range(4):
                e.wait_ge(ye_out[n], 16 * E // 4)
            with e.Fori(0, T // 2) as j:
                for n in range(2):
                    e.wait_ge(gs_ready, j * 2 + n + 1)
                    alone(e)
                    for k in range(TOPK):
                        e.indirect_dma_start(got[:, n, k], None, YE[:, :],
                                             bass.IndirectOffsetOnAxis(ap=gslot[:, n, k:k + 1], axis=0),
                                             bounds_check=E * CAP, oob_is_err=False).then_inc(got_in[n], 16)

        @block.scalar
        def _(e):
            e.dma_start(cosT[:, :, :], rope_cos).then_inc(tab_in, 16)
            e.dma_start(sinT[:, :, :], rope_sin).then_inc(tab_in, 16)
            e.dma_start(rwr, rw).then_inc(rw_in, 16)
            with nc.allow_non_contiguous_dma(reason="biases of 2048 elements"):
                for n, bias in enumerate((bq, bk)):
                    e.dma_start(bqk[:, n, :], bias.rearrange("(h p) -> p h", p=P)).then_inc(bias_in, 16)
                e.dma_start(bvT[:, :], bv.rearrange("(h p) -> p h", p=P)).then_inc(bias_in, 16)
            e.dma_start(bo_row[:, :], bo.unsqueeze(0)).then_inc(bias_in, 16)
            e.wait_ge(zeroed, 1)
            e.dma_start(XE.rearrange("(p a) d -> p (a d)", p=P).rearrange("p (a n) -> p a n", a=8),
                        diag[:, :, :].rearrange("p h t -> p (h t)").unsqueeze(1).to_broadcast([P, 8, H * P])).then_inc(zero_out, 16)
            e.dma_start(YE[E * CAP:E * CAP + 1, :], diag[0:1, 0:2, :].rearrange("p h t -> p (h t)")).then_inc(zero_out, 16)

            with e.Fori(0, GROUPS // 2) as j:
                for half in range(2):
                    g = j * 2 + half
                    e.wait_ge(f_t, g + 1)
                    for p in range(2):
                        e.copy(fkqT[:, 2 * p:2 * p + 2], bank[p][0:QC, :].rearrange("p (h c d) -> p h c d", h=2, c=2)).then_inc(f_ta, 1)
                        e.copy(fWoT[:, 2 * p:2 * p + 2], bank[5 + p][:, :].rearrange("p (h d) -> p h d", h=2)).then_inc(f_ta, 1)
                    e.wait_ge(f_n, g + 1)
                    e.copy(N[:, bass.ds(g * 2, 2), :], bank[0][:, :].rearrange("p (c d) -> p c d", c=2)).then_inc(f_na, 1)

            def x_use(name, i):
                bk_, need = xpos(name, i)
                src = XBANK[bk_]
                e.wait_ge(xf[bk_], need)
                if name == "hT":
                    dst, s = h1T[:, :, :], src[:, 0:D].rearrange("p (c t) -> p c t", c=DCH)
                elif name in ("qa", "qb"):
                    a = 4 * (name == "qb")
                    dst = qT[:, :, a:a + 4, :].rearrange("p b c s -> p c b s")
                    s = src[:, :].rearrange("p (c b s) -> p c b s", c=4, b=BT)
                elif name[:2] == "kt":
                    dst, s = KT[:, int(name[2]) % 2, :], src[:, 0:NL]
                else:
                    b = int(name[2])
                    dst, s = cT[:, :, S * b:S * b + S], src[:, 0:D].rearrange("p (c t) -> p c t", c=HP)
                e.copy(dst, s).then_inc(xd[bk_], 1)

            def exp_row(i, r):
                e.wait_ge(maxed, i * ROWS + r + 1)
                if r % RB == 0:
                    b = r // RB
                    e.wait_ge(on_ready, i * BT + b - 1 if b else i * BT)
                s = r % (2 * RB)
                e.activation(pr[:, s, :], bank[r % 2][:, 0:NL], ACT.Exp, bias=nmax[:, s:s + 1],
                             accum_out=rsum[:, s:s + 1]).then_inc(expd, 1)

            def copy_row(i, r):
                e.wait_ge(transposed, i * ROWS + r + 1)
                if r >= 2:
                    e.wait_ge(summed, i * ROWS + r - 1)
                e.copy(pT[:, r % 2], bank[2][:, 0:2 * P].rearrange("p (c t) -> p c t", c=2)).then_inc(pt_ready, 1)

            def s_use(name, j):
                bk_, need = spos(name, j)
                src = SBANK[bk_]
                if name in ("hT", "rT"):
                    e.wait_ge(sf[bk_], need)
                    e.copy(h2T if name == "hT" else h3T, src[:, 0:D].rearrange("p (c t) -> p c t", c=DCH)).then_inc(sd[bk_], 1)
                elif name[0] == "v":
                    e.wait_ge(sf[bk_], need)
                    e.copy(V[:, 512 * int(name[1]):512 * int(name[1]) + 512], src[:, :]).then_inc(sd[bk_], 1)
                elif name[:2] == "pv":
                    e.wait_ge(sf[bk_], need)
                    g = int(name[2])
                    e.copy(oT[:, 4 * g:4 * g + 4, :], src[:, :].rearrange("p (h t) -> p h t", h=4)).then_inc(sd[bk_], 1)
                elif name == "sc":
                    e.wait_ge(shifted, j + 1)
                    e.activation(sS, sS, ACT.Exp, scale=float(HD) ** -0.5).then_inc(s_expd, 1)
                elif name == "log":
                    e.wait_ge(top_ready, j + 1)
                    e.activation(etop[:, :], top[:, :], ACT.Exp, bias=ntop[:, :], accum_out=esum[:, :]).then_inc(e_ready, 1)

            def tile(i, j):
                if j is not None:
                    s_use("hT", j)
                if i is not None:
                    for name in ("hT", "qa", "qb", "kt0"):
                        x_use(name, i)
                for r in range(STEPS):
                    if i is not None:
                        if r < ROWS:
                            exp_row(i, r)
                        if 1 <= r <= ROWS:
                            copy_row(i, r - 1)
                        for name in X_AT.get(r, ()):
                            if name != "out":
                                x_use(name, i)
                    if j is not None:
                        for name in BEHIND.get(r, ()):
                            s_use(name, j)

            tile(0, None)
            with e.Fori(0, T - 1) as j:
                tile(j + 1, j)
            tile(None, T - 1)

            def expert_copy(ex, n):
                e.wait_ge(e_t, ex + 1)
                e.copy(xeT[:, n % 2], bank[n % 2][:, 0:D].rearrange("p (c t) -> p c t", c=DCH)).then_inc(e_tc, 1)

            def experts(j, last):
                for n in range(NB):
                    if not (last and n == NB - 1):
                        expert_copy(j * NB + n + 1, n + 1)
                    e.wait_ge(e_gu, j * NB + n + 1)
                    e.activation(sg[:, n % 2], bank[2 + n % 2][0:I, 0:P], ACT.Silu).then_inc(e_silu, 1)

            expert_copy(0, 0)
            with e.Fori(0, E // NB - 1) as j:
                experts(j, False)
            experts(E // NB - 1, True)

        @block.vector
        def _(e):
            e.memset(diag[:, :, :], 0.0).then_inc(zeroed, 1)
            e.memset(count[:, :], 0.0).then_inc(zeroed, 1)
            e.wait_ge(rw_t, 1)
            e.tensor_copy(rwT[:, :, :], bank[7][:, 0:DCH * E].rearrange("p (c n) -> p c n", c=DCH)).then_inc(rwT_ready, 1)

            with e.Fori(0, GROUPS // 2) as j:
                for half in range(2):
                    g = j * 2 + half
                    e.wait_ge(f_t, g + 1)
                    for p in range(2):
                        e.tensor_copy(fqrT[:, 2 * p:2 * p + 2], bank[2 + p][0:R, 0:4 * QC].rearrange("p (h c d) -> p h c d", h=2, c=2)).then_inc(f_td, 1)
                    e.tensor_copy(fkrT, bank[4][0:R, 0:GH * DC].rearrange("p (h d) -> p h d", h=GH)).then_inc(f_td, 1)
                    e.wait_ge(f_g, g + 1)
                    e.tensor_copy(fG, bank[7][0:QC, :].rearrange("p (h c d) -> p h c d", h=GH, c=2)).then_inc(f_gd, 1)
                    e.wait_ge(f_q, g + 1)
                    e.tensor_copy(fQ, bank[1][:, 0:GH * DC].rearrange("p (h d) -> p h d", h=GH)).then_inc(f_qd, 1)
                    e.wait_ge(f_m, g + 1 + FREE)
                    e.tensor_copy(M[:, :, bass.ds(g * (GH * DC), GH * DC)], bank[2][:, :].rearrange("p (c n) -> p c n", c=DCH)).then_inc(f_md, 1)

            done = {}

            def link(ins, which, base):
                done[which] = done.get(which, 0) + 1
                s, n = (x_link, XLINKS) if which == "x" else (s_link, SLINKS)
                ins.then_inc(s, 1)
                e.wait_ge(s, base * n + done[which])

            def norm(dst, t, which, base, st, mv, rs, ready):
                src = X[:, bass.ds(t, 1), :].rearrange("p o d -> p (o d)")
                alone(e)
                link(e.bn_stats(st[:, :], src), which, base)
                alone(e)
                link(e.bn_aggr(mv[:, :], st[:, :]), which, base)
                var = mv[:, 1:2]
                link(e.tensor_scalar(var, var, 1e-5, None, ALU.add), which, base)
                link(e.tensor_scalar(rs[:, 1:2].bitcast(u32), var.bitcast(u32), 1, None, ALU.logical_shift_right), which, base)
                link(e.tensor_scalar(rs[:, 0:1].bitcast(u32), rs[:, 1:2].bitcast(u32), -1.0, float(0x5f3759df), ALU.mult, ALU.add), which, base)
                for _ in range(NEWTON):
                    link(e.scalar_tensor_tensor(rs[:, 1:2], rs[:, 0:1], rs[:, 0:1], var, ALU.mult, ALU.mult), which, base)
                    link(e.tensor_scalar(rs[:, 1:2], rs[:, 1:2], -0.5, 1.5, ALU.mult, ALU.add), which, base)
                    link(e.tensor_tensor(rs[:, 0:1], rs[:, 0:1], rs[:, 1:2], ALU.mult), which, base)
                e.tensor_scalar(dst[:, :], src, mv[:, 0:1], rs[:, 0:1], ALU.subtract, ALU.mult).then_inc(ready, 1)

            def max_row(i, r):
                e.wait_ge(scored, i * ROWS + r + 1)
                s = r % (2 * RB)
                e.tensor_reduce(nmax[:, s:s + 1], bank[r % 2][:, 0:NL], AX.X, ALU.max, negate=True).then_inc(maxed, 1)

            def normalise(i, b):
                e.wait_ge(summed, i * ROWS + RB * (b + 1))
                e.wait_ge(last_ready, i * BT + b + 1)
                link(e.tensor_tensor(On[:, b % 2], bank[3][:, 0:RB * DC].rearrange("p (r d) -> p r d", r=RB),
                                     On[:, b % 2], ALU.add), "x", i)
                s = RB * (b % 2)
                link(e.reciprocal(rinv[:, s:s + RB], rsum[:, s:s + RB]), "x", i)
                e.tensor_tensor(On[:, b % 2], On[:, b % 2], rinv[:, s:s + RB].unsqueeze(2).to_broadcast([P, RB, DC]),
                                ALU.mult).then_inc(on_ready, 1)

            def x_out(i):
                bk_, need = xpos("out", i)
                e.wait_ge(xf[bk_], need)
                src = X[:, bass.ds(i, 1), :].rearrange("p o d -> p (o d)")
                e.tensor_tensor(src, src, XBANK[bk_][:, 0:D], ALU.add).then_inc(xd[bk_], 1)
                e.wait_ge(xd[bk_], need + FREE)
                norm(h2, i, "x", i, st1, mv1, rs1, h2_ready)

            def softmax(j):
                e.wait_ge(s_expd, j + 1)
                link(e.tensor_reduce(ssum[:, :], sS, AX.X, ALU.add), "s", j)
                link(e.reciprocal(sinv[:, :], ssum[:, :]), "s", j)
                link(e.tensor_tensor(sS, sS, sinv[:, :].unsqueeze(2).to_broadcast([P, H, S]), ALU.mult), "s", j)
                for q in range(4):
                    qs = slice(32 * q, 32 * q + 32)
                    e.transpose(diag[qs, :, qs], sS[qs]).then_inc(diag_ready, 1)

            def s_use(name, j):
                bk_, need = spos(name, j)
                src = SBANK[bk_]
                if name[0] in "qk":
                    e.wait_ge(sf[bk_], need)
                    g, w = int(name[1]), int(name[0] == "k")
                    e.tensor_tensor((qS, kS)[w][:, 4 * g:4 * g + 4, :], src[:, :].rearrange("p (h t) -> p h t", h=4),
                                    bqk[:, w, 4 * g:4 * g + 4].unsqueeze(2).to_broadcast([P, 4, P]), ALU.add).then_inc(sd[bk_], 1)
                elif name == "sc":
                    e.wait_ge(sf[bk_], need)
                    s3 = src[:, :].rearrange("p (h t) -> p h t", h=H)
                    link(e.tensor_reduce(smax[:, :], s3, AX.X, ALU.max), "s", j)
                    e.tensor_tensor(sS, s3, smax[:, :].unsqueeze(2).to_broadcast([P, H, S]), ALU.subtract).then_inc(sd[bk_], 1)
                    e.wait_ge(sd[bk_], need + FREE)
                    e.nop().then_inc(shifted, 1)
                elif name == "wo":
                    e.wait_ge(sf[bk_], need)
                    src2 = X[:, bass.ds(j, 1), :].rearrange("p o d -> p (o d)")
                    e.tensor_tensor(src2, src2, src[:, 0:D], ALU.add).then_inc(sd[bk_], 1)
                    e.wait_ge(sd[bk_], need + FREE)
                    link(e.tensor_tensor(src2, src2, obias[:, :], ALU.add), "s", j)
                    e.wait_ge(h3_free, j + FREE)
                    norm(h3, j, "s", j, st2, mv2, rs2, h3_ready)
                elif name == "log":
                    e.wait_ge(sf[bk_], need)
                    e.tensor_copy(lg[:, :], src[:, 0:E]).then_inc(sd[bk_], 1)
                    e.wait_ge(sd[bk_], need + FREE)
                    alone(e)
                    link(e.max(top[:, :], lg[:, :]), "s", j)
                    e.tensor_scalar(ntop[:, :], top[:, 0:1], -1.0, None, ALU.mult).then_inc(top_ready, 1)
                    link(e.max_index(topi[:, :], top[:, :], lg[:, :]), "s", j)
                    link(e.tensor_copy(topf[:, :], topi[:, :]), "s", j)
                    link(e.tensor_tensor(oh, iota_e[:, :].unsqueeze(1).to_broadcast([P, TOPK, E]),
                                         topf[:, :].unsqueeze(2).to_broadcast([P, TOPK, E]), ALU.is_equal), "s", j)
                    with nc.allow_low_precision(reason="zeros and ones"):
                        e.tensor_reduce(mask[:, :], oh.rearrange("p k e -> p e k"), AX.X, ALU.add).then_inc(mask_ready, 1)
                    e.wait_ge(mask_ready, j + 1)
                    e.wait_ge(e_ready, j + 1)
                    link(e.reciprocal(einv[:, :], esum[:, :]), "s", j)
                    link(e.tensor_scalar(wts[:, bass.ds(j, 1), :].rearrange("p o k -> p (o k)"), etop[:, :], einv[:, :], None, ALU.mult), "s", j)
                elif name == "pos":
                    e.wait_ge(sf[bk_], need)
                    link(e.tensor_tensor(sv[:, :], src[:, 0:E], slot0[:, :], ALU.add), "s", j)
                    e.scalar_tensor_tensor(sv2[:, :], src[:, 0:E], float(CAP), sv[:, :], ALU.is_lt, ALU.mult).then_inc(sd[bk_], 1)
                    e.wait_ge(sd[bk_], need + FREE)
                    link(e.tensor_tensor(count[:, :], count[:, :], mask[:, :], ALU.add), "s", j)
                    link(e.tensor_tensor(oh2, oh, sv2[:, :].unsqueeze(1).to_broadcast([P, TOPK, E]), ALU.mult), "s", j)
                    link(e.tensor_reduce(slotf[:, :], oh2, AX.X, ALU.add), "s", j)
                    link(e.tensor_scalar(slots[:, bass.ds(j, 1), :].rearrange("p o k -> p (o k)"), slotf[:, :], float(NOSLOT), None, ALU.add), "s", j)
                    e.tensor_scalar(slot[:, :], slotf[:, :], float(NOSLOT), None, ALU.add).then_inc(slot_ready, 1)

            def tile(i, j):
                done.clear()
                if i is not None:
                    norm(h1, i, "x", i, st1, mv1, rs1, h1_ready)
                if j is not None:
                    for name in ("q0", "q1", "q2", "q3"):
                        s_use(name, j)
                for r in range(STEPS):
                    if i is not None:
                        if r < ROWS:
                            max_row(i, r)
                        if r % RB == 1 and r > RB:
                            normalise(i, r // RB - 1)
                        if "out" in X_AT.get(r, ()):
                            x_out(i)
                    if j is not None:
                        for name in BEHIND.get(r, ()):
                            s_use(name, j)
                            if name == "v0":
                                softmax(j)
                assert i is None or done["x"] == XLINKS, done
                assert j is None or done["s"] == SLINKS, done

            e.sem_inc(h3_free, FREE)
            e.wait_ge(x_in, 16)
            e.wait_ge(iotas, 1)
            e.wait_ge(zeroed, 2)
            tile(0, None)
            e.wait_ge(ob_mm, 1)
            e.tensor_copy(obias[:, :], bank[7][:, 0:D]).then_inc(ob_ready, 1)
            e.wait_ge(ob_ready, 1)
            e.wait_ge(bias_in, 64)
            e.wait_ge(zero_out, 32)
            with e.Fori(0, T - 1) as j:
                tile(j + 1, j)
            tile(None, T - 1)

            def experts(j, first):
                for n in range(NB):
                    e.wait_ge(e_silu, j * NB + n + 1)
                    e.tensor_tensor(hh[:, n % 2], sg[:, n % 2], bank[2 + n % 2][0:I, P:2 * P], ALU.mult).then_inc(e_h, 1)
                    if not (first and n == 0):
                        m = (n - 1) % NB
                        e.wait_ge(e_dn, j * NB + n)
                        e.wait_ge(ye_out[m % 4], j * 32 + (16 * (m // 4) if n else -16))
                        e.tensor_copy(ye[:, m % 4], bank[4 + m % 2][:, 0:D]).then_inc(e_ye, 1)

            experts(0, True)
            with e.Fori(1, E // NB) as j:
                experts(j, False)
            e.wait_ge(e_dn, E)
            e.wait_ge(ye_out[3], 16 * (E // 4 - 1))
            e.tensor_copy(ye[:, 3], bank[4 + (NB - 1) % 2][:, 0:D]).then_inc(e_ye, 1)
            def gather_slots(t, n):
                e.tensor_copy(gslot[:, n], slots[:, bass.ds(t, 1), :].rearrange("p o k -> p (o k)")).then_inc(gs_ready, 1)

            def combine(t, n, m):
                e.wait_ge(got_in[n], m * (16 * TOPK) + 16 * TOPK)
                acc = X[:, bass.ds(t, 1), :].rearrange("p o d -> p (o d)")
                for k in range(TOPK):
                    ins = e.scalar_tensor_tensor(acc, got[:, n, k], wts[:, bass.ds(t, 1), k:k + 1].rearrange("p o k -> p (o k)"),
                                                 acc, ALU.mult, ALU.add)
                    if k < TOPK - 1:
                        ins.then_inc(y_link, 1)
                        e.wait_ge(y_link, t * (TOPK - 1) + k + 1)
                    else:
                        ins.then_inc(y_ready, 1)

            gather_slots(0, 0)
            gather_slots(1, 1)
            with e.Fori(0, T // 2 - 1) as j:
                for n in range(2):
                    combine(j * 2 + n, n, j)
                    gather_slots(j * 2 + n + 2, n)
            for n in range(2):
                combine(T - 2 + n, n, T // 2 - 1)

        @block.tensor
        def _(e):
            for s in (f_na, f_md, xd[0], xd[1], sd[0], sd[1]):
                e.sem_inc(s, FREE)
            e.wait_ge(consts, 3)
            e.wait_ge(rw_in, 16)
            for c in range(DCH):
                ins = e.transpose(bank[7][:, c * E:(c + 1) * E], rwr[:, c * P:(c + 1) * P], ident[0:E, 0:E])
            ins.then_inc(rw_t, 1)
            e.wait_ge(rwT_ready, 1)

            with e.Fori(0, GROUPS // 2) as j:
                for half in range(2):
                    g = j * 2 + half
                    e.wait_ge(fold_in[half], j * 128 + 128)
                    e.wait_ge(f_na, g + FREE)
                    e.wait_ge(f_md, g + FREE)
                    for h in range(GH):
                        p, o = h // 2, 256 * (h % 2)
                        for c in range(2):
                            e.transpose(bank[p][0:QC, o + c * P:o + (c + 1) * P], fkq[half][:, h, c * QC:(c + 1) * QC], ident[:, :])
                            e.transpose(bank[2 + p][0:R, (2 * (h % 2) + c) * QC:(2 * (h % 2) + c + 1) * QC], fqr[half][:, h, c, :], ident[0:QC, 0:QC])
                            e.transpose(bank[5 + p][:, o + c * P:o + (c + 1) * P], fWo[half][:, c, h, :], ident[:, :])
                        ins = e.transpose(bank[4][0:R, h * DC:(h + 1) * DC], fkr[half][:, h, :], ident[0:DC, 0:DC])
                    ins.then_inc(f_t, 1)
                    e.wait_ge(f_td, g * 3 + 3)
                    for h in range(GH):
                        for c in range(2):
                            ins = e.matmul(bank[7][0:QC, (2 * h + c) * DC:(2 * h + c + 1) * DC], fqrT[:, h, c, :], fkrT[:, h, :], start=True, stop=True)
                    ins.then_inc(f_g, 1)
                    e.wait_ge(f_ta, g * 4 + 4)
                    for h in range(GH):
                        q = DC * (h % 2)
                        ins = e.matmul(bank[0][q:q + DC, (h // 2) * D:(h // 2 + 1) * D], fkv[half][:, h, :], fWoT[:, h, :], start=True, stop=True)
                    ins.then_inc(f_n, 1)
                    e.wait_ge(f_gd, g + 1)
                    for h in range(GH):
                        for c in range(2):
                            ins = e.matmul(bank[1][:, h * DC:(h + 1) * DC], fkqT[:, h, c, :], fG[:, h, c, :], start=c == 0, stop=c == 1)
                    ins.then_inc(f_q, 1)
                    e.wait_ge(f_qd, g + 1)
                    for h in range(GH):
                        for c in range(DCH):
                            ins = e.matmul(bank[2][:, c * 256 + h * DC:c * 256 + (h + 1) * DC], fWq[half][:, h, c * P:(c + 1) * P], fQ[:, h, :], start=True, stop=True)
                    ins.then_inc(f_m, 1)
            e.wait_ge(f_md, GROUPS + FREE)
            e.wait_ge(f_na, GROUPS + FREE)

            def x_use(name, i):
                bk_, need = xpos(name, i)
                dst = XBANK[bk_]
                e.wait_ge(xd[bk_], need - 1 + FREE)
                if name == "hT":
                    e.wait_ge(h1_ready, i + 1)
                    for c in range(DCH):
                        ins = e.transpose(dst[:, c * P:(c + 1) * P], h1[:, c * P:(c + 1) * P], ident[:, :])
                elif name in ("qa", "qb"):
                    wait_pos(e, xd, xpos("hT", i))
                    for n in range(4):
                        c = n + 4 * (name == "qb")
                        for k in range(DCH):
                            ins = e.matmul(dst[:, n * P:(n + 1) * P], M[:, k, c * P:(c + 1) * P], h1T[:, k, :], start=k == 0, stop=k == DCH - 1)
                elif name[:2] == "kt":
                    b = int(name[2])
                    e.wait_ge(roped, i * 2 + 2)
                    for c in range(2):
                        e.transpose(dst[:, c * P:(c + 1) * P], Cr[:, b, c].rearrange("p t d -> p (t d)"), ident[:, :])
                    ins = e.transpose(dst[:, 2 * P:NL], Cr[0:1, b, 2].rearrange("p t d -> p (t d)"), ident[0:1, 0:1])
                elif name[:2] == "cT":
                    b = int(name[2])
                    e.wait_ge(on_ready, i * BT + b + 1)
                    for g in range(2):
                        ins = e.transpose(dst[:, g * P:(g + 1) * P], On[:, b % 2, 2 * g:2 * g + 2, :].rearrange("p r d -> p (r d)"), ident[:, :])
                else:
                    wait_pos(e, xd, xpos("cT3", i))
                    for c in range(HP):
                        ins = e.matmul(dst[:, 0:D], cT[:, c, :], N[:, c, :], start=c == 0, stop=c == HP - 1)
                ins.then_inc(xf[bk_], 1)

            def score_row(i, r):
                b, g, q = r // RB, r % RB // 2, DC * (r % 2)
                if r % RB == 0:
                    wait_pos(e, xd, xpos(f"kt{b}", i))
                if r == 0:
                    wait_pos(e, xd, xpos("qb", i))
                e.wait_ge(expd, i * ROWS + r - 1 if r else i * ROWS)
                e.matmul(bank[r % 2][:, 0:NL], qT[q:q + DC, b, 4 * g:4 * g + 4, :], KT[q:q + DC, b % 2, :],
                         start=True, stop=True).then_inc(scored, 1)

            def transpose_row(i, r):
                e.wait_ge(expd, i * ROWS + r + 1)
                e.wait_ge(pt_ready, i * ROWS + r)
                for c in range(2):
                    ins = e.transpose(bank[2][:, c * P:(c + 1) * P], pr[:, r % (2 * RB), c * P:(c + 1) * P], ident[:, :])
                ins.then_inc(transposed, 1)

            def sum_row(i, r):
                b = r // RB
                e.wait_ge(pt_ready, i * ROWS + r + 1)
                if r % RB == 0:
                    e.wait_ge(on_ready, i * BT + b)
                o = DC * (r % RB)
                for c in range(2):
                    ins = e.matmul(bank[3][:, o:o + DC], pT[:, r % 2, c, :], Cr[:, b, c, 0, :], start=c == 0, stop=c == 1)
                ins.then_inc(summed, 1)

            def s_use(name, j):
                bk_, need = spos(name, j)
                dst = SBANK[bk_]
                e.wait_ge(sd[bk_], need - 1 + FREE)
                if name in ("hT", "rT"):
                    e.wait_ge(h2_ready if name == "hT" else h3_ready, j + 1)
                    src = h2 if name == "hT" else h3
                    for c in range(DCH):
                        ins = e.transpose(dst[:, c * P:(c + 1) * P], src[:, c * P:(c + 1) * P], ident[:, :])
                elif name[0] in "qk":
                    wait_pos(e, sd, spos("hT", j))
                    w = 2 * (name[0] == "k")
                    for n in range(4):
                        h = 4 * int(name[1]) + n
                        for k in range(DCH):
                            ins = e.matmul(dst[:, n * P:(n + 1) * P], W[:, w + k, h * HD:(h + 1) * HD], h2T[:, k, :], start=k == 0, stop=k == DCH - 1)
                elif name == "sc":
                    wait_pos(e, sd, spos("k3", j))
                    for h in range(H):
                        for q in range(4):
                            qs = slice(32 * q, 32 * q + 32)
                            ins = e.matmul(dst[qs, h * S:(h + 1) * S], qS[:, h, qs], kS[:, h, qs], start=True, stop=True, tile_position=(0, 32 * q))
                elif name[0] == "v":
                    o = 512 * int(name[1])
                    for k in range(DCH):
                        ins = e.matmul(dst[:, :], h2T[:, k, :], W[:, 4 + k, o:o + 512], start=k == 0, stop=k == DCH - 1)
                elif name[:2] == "pv":
                    e.wait_ge(diag_ready, j * 4 + 4)
                    wait_pos(e, sd, spos("v3", j))
                    for n in range(4):
                        h = 4 * int(name[2]) + n
                        ins = e.matmul(dst[:, n * P:(n + 1) * P], V[:, h * HD:(h + 1) * HD], diag[:, h, :], start=True, stop=True)
                elif name == "wo":
                    wait_pos(e, sd, spos("pv3", j))
                    for h in range(H):
                        ins = e.matmul(dst[:, 0:D], oT[:, h, :], W[:, 6 + h // 8, (h % 8) * D:(h % 8 + 1) * D], start=h == 0, stop=h == H - 1)
                elif name == "log":
                    wait_pos(e, sd, spos("rT", j))
                    for k in range(DCH):
                        ins = e.matmul(dst[:, 0:E], h3T[:, k, :], rwT[:, k, :], start=k == 0, stop=k == DCH - 1)
                elif name == "pos":
                    e.wait_ge(mask_ready, j + 1)
                    e.matmul(dst[:, 0:E], before[:, :], mask[:, :], start=True, stop=False)
                    ins = e.matmul(dst[:, 0:E], ones16[:, :], count[:, :], start=False, stop=True)
                ins.then_inc(sf[bk_], 1)

            def tile(i, j):
                if j is not None:
                    s_use("hT", j)
                if i is not None:
                    x_use("hT", i)
                if j is not None:
                    s_use("q0", j)
                    s_use("q1", j)
                if i is not None:
                    for name in ("qa", "qb", "kt0"):
                        x_use(name, i)
                if j is not None:
                    s_use("q2", j)
                    s_use("q3", j)
                for r in range(STEPS):
                    if i is not None:
                        if r < ROWS:
                            score_row(i, r)
                        if 1 <= r <= ROWS:
                            transpose_row(i, r - 1)
                        if 2 <= r <= ROWS + 1:
                            sum_row(i, r - 2)
                        for name in X_AT.get(r, ()):
                            x_use(name, i)
                    if j is not None:
                        for name in BEHIND.get(r, ()):
                            s_use(name, j)

            tile(0, None)
            e.wait_ge(w_done, 8)
            e.wait_ge(bias_in, 64)
            e.matmul(bank[7][:, 0:D], onerow[:, :], bo_row[:, :], start=True, stop=False)
            for h in range(H):
                ins = e.matmul(bank[7][:, 0:D], bvT[:, h:h + 1].to_broadcast([P, P]), W[:, 6 + h // 8, (h % 8) * D:(h % 8 + 1) * D],
                               start=False, stop=h == H - 1)
            ins.then_inc(ob_mm, 1)
            e.wait_ge(ob_ready, 1)
            with e.Fori(0, T - 1) as j:
                tile(j + 1, j)
            tile(None, T - 1)

            def expert_t(j, n):
                e.wait_ge(xe_in[n], j * 16 + 16)
                for c in range(DCH):
                    ins = e.transpose(bank[n % 2][:, c * P:(c + 1) * P], xe[:, n, c * P:(c + 1) * P], ident[:, :])
                ins.then_inc(e_t, 1)

            def expert_gate_up(j, n):
                e.wait_ge(ew_in[n], j * 32 + 32)
                e.wait_ge(e_tc, j * NB + n + 1)
                for half in range(2):
                    for c in range(DCH):
                        ins = e.matmul(bank[2 + n % 2][0:I, half * P:(half + 1) * P], gu[:, n, c, half * I:(half + 1) * I], xeT[:, n % 2, c, :],
                                       start=c == 0, stop=c == DCH - 1)
                ins.then_inc(e_gu, 1)

            def expert_down(j, n, before_that):
                e.wait_ge(e_h, before_that + 1)
                if not isinstance(before_that, int) or before_that >= 2:
                    e.wait_ge(e_ye, before_that - 1)
                e.matmul(bank[4 + n % 2][:, 0:D], hh[:, n % 2], dn[:, n], start=True, stop=True).then_inc(e_dn, 1)

            def experts(j, first, last):
                for n in range(NB):
                    if n < NB - 1:
                        expert_t(j, n + 1)
                    elif not last:
                        expert_t(j + 1, 0)
                    expert_gate_up(j, n)
                    if not (first and n == 0):
                        expert_down(j, (n - 1) % NB, j * NB + n - 1)

            expert_t(0, 0)
            experts(0, True, False)
            with e.Fori(1, E // NB - 1) as j:
                experts(j, False, False)
            experts(E // NB - 1, False, True)
            expert_down(E // NB - 1, NB - 1, E - 1)


_NAMES = ["x", "ctx_512", "L0_xattn_Wq", "L0_xattn_w_kc_q", "L0_xattn_w_kc_kv", "L0_xattn_W_qr", "L0_xattn_W_kr",
          "L0_xattn_Wo", "L0_attn_wq_codes", "L0_attn_wk_codes", "L0_attn_wv_codes", "L0_attn_wo_codes",
          "L0_attn_wq_scales", "L0_attn_wk_scales", "L0_attn_wv_scales", "L0_attn_wo_scales", "L0_attn_bq",
          "L0_attn_bk", "L0_attn_bv", "L0_attn_bo", "L0_ffn_router_weight", "L0_ffn_gate_up_proj", "L0_ffn_down_proj"]


def rope_tables():
    import numpy as np
    inv = (np.float32(1.0) / np.float32(10000.0) ** (np.arange(0, DC, 2, dtype=np.float32) / np.float32(DC))).astype(np.float32)
    f = np.arange(NL, dtype=np.float32)[:, None] * inv[None, :]
    sin, cos = (np.repeat(t.astype(np.float32), 2, axis=-1) for t in (np.sin(f), np.cos(f)))
    sin = np.concatenate([-sin[:, :DC // 2], sin[:, DC // 2:]], axis=-1)
    lay = lambda t: np.ascontiguousarray(np.stack([t[:P], t[P:2 * P], np.repeat(t[2 * P:], P, axis=0)], axis=1))
    return lay(cos), lay(sin)


def kernel(**inputs):
    import numpy as np
    import concourse.bacc as bacc
    from concourse.bass_utils import run_bass_kernel_spmd

    nc = bacc.Bacc("TRN2", target_bir_lowering=False, num_devices=1)
    arrays, aps = {}, {}

    def give(name, a):
        arrays[name + "_dram"] = a
        aps[name] = nc.dram_tensor(name + "_dram", a.shape, mybir.dt.from_np(a.dtype), kind="ExternalInput").ap()

    for name in _NAMES:
        a = np.ascontiguousarray(inputs[name])
        give(name, a.reshape(B * S, D) if name == "x" else a)
    cos, sin = rope_tables()
    give("rope_cos", cos)
    give("rope_sin", sin)
    out = nc.dram_tensor("out_dram", [B * S, D], mybir.dt.float32, kind="ExternalOutput").ap()
    v = [aps[n] for n in _NAMES]
    build(nc, *v[:8], v[8:12], v[12:16], *v[16:], aps["rope_cos"], aps["rope_sin"], out)
    r = run_bass_kernel_spmd(nc, [arrays], core_ids=[0])
    return r.results[0]["out_dram"].reshape(B, S, D)
```

```python
import concourse.bass as bass
from concourse import mybir
from contextlib import ExitStack

B, S, D = 32, 32, 256
NL, DC, DQ, R = 257, 64, 192, 64
H, HD = 16, 128
F = H * HD
E, I, TOPK, CAP = 64, 96, 8, 128

P = 128
T = B * S // P
BT = P // S
DCH = D // P
HP = H // 2
ROWS = BT * H * S // P
RB = ROWS // BT
QC = DQ // 2
GH = 4
GROUPS = H // GH
NOSLOT = E * CAP
ROW = D + E + 1
YROWS = (T + 1) * P
NY = 2
FC = 2

XS = ["hT", "qa", "qb", "kt0", "kt1", "cT0", "kt2", "cT1", "kt3", "cT2", "cT3", "out"]
SS = ["hT", "q0", "q1", "q2", "q3", "k0", "k1", "rT", "k2", "k3", "sc", "log", "v0", "v1", "v2", "pos", "v3",
      "pv0", "pv1", "pv2", "pv3", "wo"]
ROUTER = ("rT", "log", "pos")
BEHIND = {0: ["hT"], 1: ["q0", "q1"], 2: ["q2", "q3"], 3: ["k0", "k1"], 4: ["rT", "k2", "k3"], 5: ["sc", "log"],
          6: ["v0"], 7: ["v1"], 8: ["v2"], 9: ["pos", "v3"], 11: ["pv0"], 12: ["pv1"], 13: ["pv2"], 14: ["pv3"],
          15: ["wo0"], 16: ["wo1"], 17: ["wo2"], 18: ["wo3"]}
WS = 16.0
X_AT = {2: ["kt1"], 6: ["cT0", "kt2"], 10: ["cT1", "kt3"], 14: ["cT2"], 18: ["cT3"], 19: ["out"]}
STEPS = ROWS + 4
NEWTON = 3
NLINKS = 5 + 3 * NEWTON
XLINKS = NLINKS + 2 * BT
SLINKS = NLINKS + 5
RLINKS = 11
NB = 8
FREE = 1


def build(nc, x, ctx_in, Wq, kcq, kckv, Wqr, Wkr, Wo_x, codes, scales, bq, bk, bv, bo, rw, gup, dnp,
          rope_cos, rope_sin, out):
    f32, bf16, f16, u32 = mybir.dt.float32, mybir.dt.bfloat16, mybir.dt.float16, mybir.dt.uint32
    ALU, ACT, AX = mybir.AluOpType, mybir.ActivationFunctionType, mybir.AxisListType

    ctx = ExitStack()
    with ctx:
        def sb(name, shape, dt=f32):
            return ctx.enter_context(nc.sbuf_tensor(name, shape, dt))

        def sem(name):
            return ctx.enter_context(nc.semaphore(name))

        bank = [ctx.enter_context(nc.psum_tensor(f"bank{n}", [P, 512], f32)) for n in range(8)]
        XE = nc.dram_tensor("expert_rows", [E * CAP, ROW], f32, kind="Internal").ap()
        Y = [nc.dram_tensor(f"expert_sums{n}", [YROWS, D], f32, kind="Internal").ap() for n in range(NY)]

        ident = sb("ident", [P, P])
        before = sb("before", [P, P], bf16)
        ones16 = sb("ones16", [P, P], bf16)
        iota_i = sb("iota_i", [P, E], mybir.dt.int32)
        iota_e = sb("iota_e", [P, E])
        spare_i = sb("spare_i", [P, 1], mybir.dt.int32)
        slot0 = sb("slot0", [P, E])
        X = sb("X", [P, T + 1, D])
        M = sb("M", [P, DCH, H * DC])
        N = sb("N", [P, HP, D])
        Wh = sb("Wh", [P, 8, 2048], f16)
        Wl = sb("Wl", [P, 8, 2048], f16)
        bqk = sb("bqk", [P, 2, H])
        bvT = sb("bvT", [P, H])
        bvh = sb("bvh", [P, H], f16)
        bvl = sb("bvl", [P, H], f16)
        obias = sb("obias", [P, D])
        rwT = sb("rwT", [P, DCH, E])
        cosT = sb("cosT", [P, 3, DC])
        sinT = sb("sinT", [P, 3, DC])

        C = sb("C", [P, BT, 3, DC])
        Ct = sb("Ct", [P, BT, 3, DC])
        Cr = sb("Cr", [P, BT, 3, 2, DC])
        KT = sb("KT", [P, 2, NL])
        h1 = sb("h1", [P, D])
        h1T = sb("h1T", [P, DCH, P])
        qT = sb("qT", [P, BT, HP, S])
        pr = sb("pr", [P, 2 * RB, NL])
        pT = sb("pT", [P, 2, 2, P])
        nmax = sb("nmax", [P, 2 * RB])
        rsum = sb("rsum", [P, 2 * RB])
        rinv = sb("rinv", [P, 2 * RB])
        On = sb("On", [P, 2, RB, DC])
        cT = sb("cT", [P, HP, P])
        st1 = sb("st1", [P, 6])
        mv1 = sb("mv1", [P, 2])
        st0 = sb("st0", [P, T + 1, 6])
        mv0 = sb("mv0", [P, T + 1, 2])
        rs0 = sb("rs0", [P, 2, T + 1])
        rs1 = sb("rs1", [P, 2])
        rwr = h1[0:E, :]

        SPACE = 4 * 2048 + 2 * 256 + 2 * 512 + 2 * 512
        space = sb("space", [P, SPACE])
        at = [0]

        def cut(n, parts=P):
            a = at[0]
            at[0] += n
            assert at[0] <= SPACE
            return space[0:parts, a:a + n]

        fWq = [cut(GH * D).rearrange("p (h d) -> p h d", h=GH) for _ in range(2)]
        fkq = [cut(GH * DQ).rearrange("p (h d) -> p h d", h=GH) for _ in range(2)]
        fqr = [cut(GH * 2 * R, QC).rearrange("p (h c d) -> p h c d", h=GH, c=2) for _ in range(2)]
        fkr = [cut(GH * R, DC).rearrange("p (h d) -> p h d", h=GH) for _ in range(2)]
        fkv = [cut(GH * DC).rearrange("p (h d) -> p h d", h=GH) for _ in range(2)]
        fWo = [cut(DCH * GH * HD).rearrange("p (c h d) -> p c h d", c=DCH, h=GH) for _ in range(2)]
        fqrT = cut(GH * 2 * QC, R).rearrange("p (h c d) -> p h c d", h=GH, c=2)
        fkrT = cut(GH * DC, R).rearrange("p (h d) -> p h d", h=GH)
        fWoT = cut(GH * D).rearrange("p (h d) -> p h d", h=GH)
        fkqT = qT[0:QC].rearrange("p b c s -> p (b c s)").rearrange("p (h c d) -> p h c d", h=GH, c=2)
        cflat = cT[:, :, :].rearrange("p a b -> p (a b)")
        fG = cflat[0:QC, 0:GH * 2 * DC].rearrange("p (h c d) -> p h c d", h=GH, c=2)
        fQ = cflat[:, 512:512 + GH * DC].rearrange("p (h d) -> p h d", h=GH)
        at[0] = 0
        qS = cut(H * P).rearrange("p (h t) -> p h t", h=H)
        kS = cut(H * P).rearrange("p (h t) -> p h t", h=H)
        V = cut(F)
        oTh, oTl = (cut(H * P // 2).bitcast(f16).rearrange("p (h t) -> p h t", h=H) for _ in range(2))
        h2h, h2l = (cut(DCH * P // 2).bitcast(f16).rearrange("p (c t) -> p c t", c=DCH) for _ in range(2))
        h3T = cut(DCH * P).rearrange("p (c t) -> p c t", c=DCH)
        sS = cut(H * S).rearrange("p (h t) -> p h t", h=H)
        sT = cut(H * S).rearrange("p (h t) -> p h t", h=H)
        oh = cut(TOPK * E).rearrange("p (k e) -> p k e", k=TOPK)
        oh2 = cut(TOPK * E).rearrange("p (k e) -> p k e", k=TOPK)
        diag = sb("diag", [P, H, P])
        h2 = sb("h2", [P, D])
        h3 = sb("h3", [P, ROW])
        st2 = sb("st2", [P, 6])
        mv2 = sb("mv2", [P, 2])
        rs2 = sb("rs2", [P, 2])
        smax = sb("smax", [P, H])
        ssum = sb("ssum", [P, H])
        sinv = sb("sinv", [P, H])
        lg = sb("lg", [P, E])
        top = sb("top", [P, TOPK])
        topi = sb("topi", [P, TOPK], u32)
        topf = sb("topf", [P, TOPK])
        ntop = sb("ntop", [P, 1])
        etop = sb("etop", [P, TOPK])
        esum = sb("esum", [P, 1])
        einv = sb("einv", [P, 1])
        mask = sb("mask", [P, E], bf16)
        count = sb("count", [P, E], bf16)
        sv = sb("sv", [P, E])
        sv2 = sb("sv2", [P, E])
        slotf = sb("slotf", [P, TOPK])
        slot = sb("slot", [P, TOPK], u32)

        ring = sb("ring", [P, NB * (DCH * 2 * I + D)])
        gu = ring[:, 0:NB * DCH * 2 * I].rearrange("p (n c f) -> p n c f", n=NB, c=DCH)
        dn = ring[0:I, NB * DCH * 2 * I:].rearrange("p (n d) -> p n d", n=NB)
        parts = [t.rearrange("p (n f) -> p n f", n=2) for t in (
            ring[:, 0:2048], ring[:, 2048:4096], pr[:, :, :].rearrange("p a b -> p (a b)")[:, 0:2048],
            diag[:, :, :].rearrange("p a b -> p (a b)"))]
        Wf = Wh[:, :, :].rearrange("p u f -> p (u f)").bitcast(f32)
        xeT = Wf[:, 0:512].rearrange("p (n c t) -> p n c t", n=2, c=DCH)
        sg = Wf[0:I, 512:768].rearrange("p (n t) -> p n t", n=2)
        hh = Wf[0:I, 768:1024].rearrange("p (n t) -> p n t", n=2)
        ye = Wf[:, 1024:2048].rearrange("p (n d) -> p n d", n=4)
        xe = Wf[:, 2048:2048 + NB * ROW].rearrange("p (n d) -> p n d", n=NB)
        ysum = Wl[:, :, :].rearrange("p u f -> p (u f)").bitcast(f32)[:, 0:NY * T * D].rearrange("p (y t d) -> p y t d", y=NY, t=T)
        etok = sb("etok", [P, 4], u32)

        x_in, tab_in, rw_in, bias_in, ctx_ld, zero_out = (sem(n) for n in (
            "x_in", "tables_in", "router_in", "biases_in", "context_in", "zero_out"))
        fold_in = [sem("fold_in0"), sem("fold_in1")]
        w_in = [sem(f"w_in{n}") for n in range(4)]
        ew_in = [sem(f"expert_weights_in{n}") for n in range(NB)]
        xe_in = [sem(f"expert_rows_in{n}") for n in range(NB)]
        ye_out = [sem(f"expert_out{n}") for n in range(4)]
        sums_in = [sem(f"sums_in{n}") for n in range(T // FC)]
        scat, h3_free, stored = sem("scattered"), sem("h3_free"), sem("stored")
        consts, iotas, zeroed, pool_link, rw_t, rwT_ready, ob_mm, ob_ready, w_done = (sem(n) for n in (
            "consts", "iotas", "zeroed", "pool_link", "router_transposed", "rwT_ready", "obias_summed",
            "obias_ready", "w_done"))
        w_mul, w_high, bv_split = sem("w_dequantised"), sem("w_high"), sem("bv_split")
        f_t, f_ta, f_td, f_g, f_gd, f_n, f_na, f_q, f_qd, f_m, f_md = (sem(n) for n in (
            "f_transposed", "f_act_copied", "f_dve_copied", "f_G", "f_G_copied", "f_N", "f_N_copied",
            "f_Q", "f_Q_copied", "f_M", "f_M_copied"))
        xf = [sem("x_filled0"), sem("x_filled1")]
        xd = [sem("x_drained0"), sem("x_drained1")]
        x_link, r_link, n_link, sT_ready, h1_ready, rope_link, roped, scored, maxed, expd, transposed, pt_ready, summed, last_ready, on_ready = (
            sem(n) for n in ("x_link", "r_link", "n_link", "sT_ready", "h1_ready", "rope_link", "roped", "scored", "maxed", "expd", "transposed",
                             "pt_ready", "summed", "last_ready", "on_ready"))
        sf = [sem("s_filled0"), sem("s_filled1")]
        sd = [sem("s_drained0"), sem("s_drained1")]
        s_high, s_link, h2_ready, shifted, s_expd, diag_ready, h3_ready, top_ready, e_ready, mask_ready, slot_ready = (
            sem(n) for n in ("s_high", "s_link", "h2_ready", "shifted", "s_expd", "diag_ready", "h3_ready", "top_ready",
                             "e_ready", "mask_ready", "slot_ready"))
        e_t, e_tc, e_gu, e_silu, e_h, e_dn, e_ye = (sem(n) for n in (
            "e_transposed", "e_xT_ready", "e_gate_up", "e_silu", "e_hidden", "e_down", "e_out_ready"))
        y_link, y_ready = sem("y_link"), sem("y_ready")

        passed = sem("passed")

        def alone(e):
            e.sem_inc(passed, 1)

        block = ctx.enter_context(nc.Block())
        XBANK = (bank[4], bank[5])
        SBANK = (bank[6], bank[7])

        def xpos(name, i, more=1):
            n = XS.index(name)
            return n % 2, i * (len(XS) // 2) + n // 2 + more

        def spos(name, j, more=1):
            n = SS.index(name[:2] if name[:2] == "wo" else name)
            if name in ROUTER:
                j = j + 1
            return n % 2, j * (len(SS) // 2) + n // 2 + more

        def wait_pos(e, sems, pos):
            e.wait_ge(sems[pos[0]], pos[1] + (FREE if sems in (xd, sd) else 0))

        def part_of(w, g, n):
            return w[:, :, :].rearrange("p u (a f) -> p (u a) f", a=2)[:, bass.ds(g * 4 + n, 1), :].rearrange("p o f -> p (o f)")

        @block.sync
        def _(e):
            e.dma_start(X[:, 0:T, :], x.rearrange("(t p) d -> p t d", p=P)).then_inc(x_in, 16)
            def load_fold(g):
                half = g % 2
                if g >= 2:
                    e.wait_ge(f_m, g - 1)
                hs = slice(g * GH, g * GH + GH)
                fs = slice(g * GH * HD, (g + 1) * GH * HD)
                for c in range(DCH):
                    e.dma_start(fWo[half][:, c], Wo_x[c * P:(c + 1) * P, fs].rearrange("p (h k) -> p h k", h=GH)).then_inc(fold_in[half], 16)
                    e.dma_start(fqr[half][:, :, c], Wqr[hs, c * QC:(c + 1) * QC, :].rearrange("h q r -> q h r")).then_inc(fold_in[half], 16)
                e.dma_start(fkq[half], kcq[hs].rearrange("h k q -> k h q")).then_inc(fold_in[half], 16)
                e.dma_start(fkr[half], Wkr[hs].rearrange("h d r -> d h r")).then_inc(fold_in[half], 16)
                e.dma_start(fWq[half], Wq[fs, :].rearrange("(h k) d -> k h d", h=GH)).then_inc(fold_in[half], 16)
                e.dma_start(fkv[half], kckv[hs].rearrange("h k d -> k h d")).then_inc(fold_in[half], 16)

            def load_part(u):
                if u >= 4:
                    e.wait_ge(w_done, u - 3)
                w, c, o = u // 4, u % 4 // 2, 1024 * (u % 2)
                to = parts[u % 4]
                if w < 3:
                    e.dma_start(to[:, 0], codes[w][c * P:(c + 1) * P, o:o + 1024]).then_inc(w_in[u % 4], 16)
                    for q in range(4):
                        e.dma_start(to[32 * q:32 * q + 32, 1],
                                    scales[w][4 * c + q:4 * c + q + 1, o:o + 1024].to_broadcast([32, 1024])).then_inc(w_in[u % 4], 16)
                else:
                    hs = slice(4 * (u % 4), 4 * (u % 4) + 4)
                    e.dma_start(to[:, 0].rearrange("p (h d) -> p h d", h=4),
                                codes[w].rearrange("(h p) d -> p h d", p=P)[:, hs]).then_inc(w_in[u % 4], 16)
                    for q in range(4):
                        e.dma_start(to[32 * q:32 * q + 32, 1].rearrange("p (h d) -> p h d", h=4),
                                    scales[w].rearrange("(h q) d -> q h d", q=4)[q:q + 1, hs].to_broadcast([32, 4, D])
                                    ).then_inc(w_in[u % 4], 16)

            def load_context(i):
                bs = bass.ds(i * BT, BT)
                for c in range(2):
                    e.dma_start(C[:, :, c, :], ctx_in[bs, c * P:(c + 1) * P, :].rearrange("b p d -> p b d")).then_inc(ctx_ld, 16)
                e.dma_start(C[:, :, 2, :], ctx_in[bs, 2 * P, :].unsqueeze(0).to_broadcast([P, BT, DC])).then_inc(ctx_ld, 16)

            load_fold(0)
            load_context(0)
            load_fold(1)
            for u in range(8):
                load_part(u)
            load_fold(2)
            load_fold(3)
            for u in range(8, 16):
                load_part(u)
            e.wait_ge(w_done, 16)

            def load_expert(ex, n):
                e.dma_start(gu[:, n], gup[bass.ds(ex, 1)].rearrange("o (c p) f -> p (o c) f", p=P)).then_inc(ew_in[n], 16)
                e.dma_start(dn[:, n], dnp[bass.ds(ex, 1)].rearrange("o i d -> i (o d)")).then_inc(ew_in[n], 16)

            def load_rows(ex, n):
                e.dma_start(xe[:, n], XE[bass.ds(ex * CAP, CAP), :]).then_inc(xe_in[n], 16)

            for n in range(NB):
                load_expert(n, n)
            with e.Fori(1, T) as i:
                e.wait_ge(roped, i * 2)
                load_context(i)
            e.wait_ge(h3_free, T + FREE)
            for n in range(NB):
                load_rows(n, n)
            with e.Fori(1, E // NB) as j:
                for n in range(NB):
                    e.wait_ge(e_ye, j * NB + (n + 1 - NB))
                    load_expert(j * NB + n, n)
                    load_rows(j * NB + n, n)
            for n in range(4):
                e.wait_ge(ye_out[n], 16 * E // 4)
            for c in range(T // FC):
                for y in range(NY):
                    e.dma_start(ysum[:, y, FC * c:FC * c + FC, :],
                                Y[y][FC * c * P:FC * (c + 1) * P, :].rearrange("(t p) d -> p t d", p=P)).then_inc(sums_in[c], 16)
            for c in range(T // FC):
                e.wait_ge(y_ready, c + 1)
                e.dma_start(out[FC * c * P:FC * (c + 1) * P, :].rearrange("(t p) d -> p t d", p=P),
                            X[:, FC * c:FC * c + FC, :]).then_inc(stored, 16)
            e.wait_ge(stored, 16 * (T // FC))

        @block.gpsimd
        def _(e):
            links = [0]

            def link(ins):
                links[0] += 1
                ins.then_inc(pool_link, 1)
                e.wait_ge(pool_link, links[0])

            link(e.memset(ident[:, :], 0.0))
            e.affine_select(out=ident[:, :], in_=ident[:, :], compare_op=ALU.not_equal, fill=1.0, base=0,
                            pattern=[[-1, P]], channel_multiplier=1).then_inc(consts, 1)
            link(e.memset(ones16[:, :], 1.0))
            e.affine_select(out=before[:, :], in_=ones16[:, :], compare_op=ALU.is_gt, fill=0.0, base=0,
                            pattern=[[1, P]], channel_multiplier=-1).then_inc(consts, 1)
            link(e.iota(iota_i[:, :], pattern=[[1, E]], base=0, channel_multiplier=0))
            link(e.tensor_copy(iota_e[:, :], iota_i[:, :]))
            e.tensor_scalar(slot0[:, :], iota_e[:, :], float(CAP), float(-NOSLOT), ALU.mult, ALU.add).then_inc(iotas, 1)
            link(e.iota(spare_i[:, :], pattern=[[0, 1]], base=B * S, channel_multiplier=1))
            link(e.memset(h3[:, 0:D + E], 0.0))
            e.tensor_copy(h3[:, D + E:ROW], spare_i[:, :]).then_inc(iotas, 1)
            e.wait_ge(tab_in, 16 * 2)

            def rope(i):
                e.wait_ge(ctx_ld, i * 48 + 48)
                half = DC // 2
                e.tensor_tensor(Ct[:, :, :, 0:half], C[:, :, :, half:DC],
                                sinT[:, :, 0:half].unsqueeze(1).to_broadcast([P, BT, 3, half]), ALU.mult).then_inc(rope_link, 1)
                e.tensor_tensor(Ct[:, :, :, half:DC], C[:, :, :, 0:half],
                                sinT[:, :, half:DC].unsqueeze(1).to_broadcast([P, BT, 3, half]), ALU.mult).then_inc(rope_link, 1)
                e.wait_ge(rope_link, i * 3 + 2)
                e.tensor_tensor(C[:, :, :, :], C[:, :, :, :],
                                cosT[:, :, :].unsqueeze(1).to_broadcast([P, BT, 3, DC]), ALU.mult).then_inc(rope_link, 1)
                e.wait_ge(rope_link, i * 3 + 3)
                e.wait_ge(summed, i * ROWS)
                e.wait_ge(last_ready, i * BT)
                for d in range(2):
                    e.tensor_tensor(Cr[:, :, :, d, :], C[:, :, :, :], Ct[:, :, :, :], ALU.add).then_inc(roped, 1)
                e.wait_ge(roped, i * 2 + 2)

            def last_rows(i, b):
                e.wait_ge(expd, i * ROWS + RB * (b + 1))
                if b >= 2:
                    wait_pos(e, xf, xpos(f"cT{b - 2}", i))
                else:
                    e.wait_ge(xf[1], i * (len(XS) // 2))
                e.tensor_tensor(On[:, b % 2], Cr[:, b, 2, 0, :].unsqueeze(1).to_broadcast([P, RB, DC]),
                                pr[:, RB * (b % 2):RB * (b % 2) + RB, NL - 1:NL].to_broadcast([P, RB, DC]),
                                ALU.mult).then_inc(last_ready, 1)

            def scatter(j, first, last):
                if first == 0:
                    e.wait_ge(slot_ready, j + 1)
                    alone(e)
                for k in range(first, last):
                    e.indirect_dma_start(XE[:, :], bass.IndirectOffsetOnAxis(ap=slot[:, k:k + 1], axis=0), h3[:, :], None,
                                         bounds_check=E * CAP - 1, oob_is_err=False).then_inc(scat, 16)

            def scattered(j):
                e.wait_ge(scat, j * (16 * TOPK) + 16 * TOPK)
                e.sem_inc(h3_free, 1)

            rope(0)
            with e.Fori(0, 4) as g:
                for n in range(4):
                    e.wait_ge(w_high, g * 4 + n + 1)
                    e.tensor_tensor(part_of(Wl, g, n), parts[n][:, 0], part_of(Wh, g, n), ALU.subtract).then_inc(w_done, 1)
            for b in range(BT):
                last_rows(0, b)
            e.wait_ge(zero_out, 16 * (1 + NY))
            def tile(i, m):
                rope(i)
                for b in range(BT):
                    last_rows(i, b)
                    if b in (1, 2) and m is not None:
                        scatter(m, TOPK // 2 * (b - 1), TOPK // 2 * b)
                if m is not None:
                    scattered(m)

            tile(1, None)
            with e.Fori(1, T - 1) as j:
                tile(j + 1, j - 1)
            for m in (T - 2, T - 1):
                scatter(m, 0, TOPK)
                scattered(m)

            def add_out(j, first):
                for n in range(NB):
                    e.wait_ge(e_ye, j * NB + n + 1)
                    if not first or n >= NY:
                        e.wait_ge(ye_out[(n - NY) % 4], j * (16 * NB // 4) + 16 * ((n - NY) // 4 + 1))
                    alone(e)
                    e.indirect_dma_start(Y[n % NY][:, :], bass.IndirectOffsetOnAxis(ap=etok[:, n % 4:n % 4 + 1], axis=0), ye[:, n % 4], None,
                                         bounds_check=YROWS - 1, oob_is_err=False, compute_op=ALU.add).then_inc(ye_out[n % 4], 16)

            add_out(0, True)
            with e.Fori(1, E // NB) as j:
                add_out(j, False)

        @block.scalar
        def _(e):
            e.dma_start(cosT[:, :, :], rope_cos).then_inc(tab_in, 16)
            e.dma_start(sinT[:, :, :], rope_sin).then_inc(tab_in, 16)
            e.dma_start(rwr, rw).then_inc(rw_in, 16)
            with nc.allow_non_contiguous_dma(reason="biases of 2048 elements"):
                for n, bias in enumerate((bq, bk)):
                    e.dma_start(bqk[:, n, :], bias.rearrange("(h p) -> p h", p=P)).then_inc(bias_in, 16)
                e.dma_start(bvT[:, :], bv.rearrange("(h p) -> p h", p=P)).then_inc(bias_in, 16)
            e.dma_start(obias[:, :], bo.unsqueeze(0).to_broadcast([P, D])).then_inc(bias_in, 16)
            with e.Fori(0, GROUPS // 2) as j:
                for half in range(2):
                    g = j * 2 + half
                    e.wait_ge(f_t, g + 1)
                    for p in range(2):
                        e.copy(fkqT[:, 2 * p:2 * p + 2], bank[p][0:QC, :].rearrange("p (h c d) -> p h c d", h=2, c=2)).then_inc(f_ta, 1)
                        e.copy(fWoT[:, 2 * p:2 * p + 2], bank[5 + p][:, :].rearrange("p (h d) -> p h d", h=2)).then_inc(f_ta, 1)
                    e.wait_ge(f_n, g + 1)
                    e.copy(N[:, bass.ds(g * 2, 2), :], bank[0][:, :].rearrange("p (c d) -> p c d", c=2)).then_inc(f_na, 1)
                    for n in range(4):
                        e.wait_ge(w_mul, g * 4 + n + 1)
                        e.copy(part_of(Wh, g, n), parts[n][:, 0]).then_inc(w_high, 1)

            e.wait_ge(iotas, 2)
            e.dma_start(XE.rearrange("(e c) d -> c e d", c=CAP), h3[:, :].unsqueeze(1).to_broadcast([P, E, ROW])).then_inc(zero_out, 16)
            for n in range(NY):
                e.dma_start(Y[n].rearrange("(a p) d -> p a d", p=P), h3[:, 0:D].unsqueeze(1).to_broadcast([P, YROWS // P, D])).then_inc(zero_out, 16)

            def x_use(name, i):
                bk_, need = xpos(name, i)
                src = XBANK[bk_]
                e.wait_ge(xf[bk_], need)
                if name == "hT":
                    dst, s = h1T[:, :, :], src[:, 0:D].rearrange("p (c t) -> p c t", c=DCH)
                elif name in ("qa", "qb"):
                    a = 4 * (name == "qb")
                    dst = qT[:, :, a:a + 4, :].rearrange("p b c s -> p c b s")
                    s = src[:, :].rearrange("p (c b s) -> p c b s", c=4, b=BT)
                elif name[:2] == "kt":
                    dst, s = KT[:, int(name[2]) % 2, :], src[:, 0:NL]
                else:
                    b = int(name[2])
                    dst, s = cT[:, :, S * b:S * b + S], src[:, 0:D].rearrange("p (c t) -> p c t", c=HP)
                e.copy(dst, s).then_inc(xd[bk_], 1)

            def exp_row(i, r):
                e.wait_ge(maxed, i * ROWS + r + 1)
                if r % RB == 0:
                    b = r // RB
                    e.wait_ge(on_ready, i * BT + b - 1 if b else i * BT)
                s = r % (2 * RB)
                e.activation(pr[:, s, :], bank[r % 2][:, 0:NL], ACT.Exp, bias=nmax[:, s:s + 1],
                             accum_out=rsum[:, s:s + 1]).then_inc(expd, 1)

            def copy_row(i, r):
                e.wait_ge(transposed, i * ROWS + r + 1)
                if r >= 2:
                    e.wait_ge(summed, i * ROWS + r - 1)
                e.copy(pT[:, r % 2], bank[2][:, 0:2 * P].rearrange("p (c t) -> p c t", c=2)).then_inc(pt_ready, 1)

            def s_use(name, j):
                bk_, need = spos(name, j)
                src = SBANK[bk_]
                if name == "rT":
                    e.wait_ge(sf[bk_], need)
                    e.copy(h3T, src[:, 0:D].rearrange("p (c t) -> p c t", c=DCH)).then_inc(sd[bk_], 1)
                elif name == "hT":
                    e.wait_ge(sf[bk_], need)
                    e.copy(h2h, src[:, 0:D].rearrange("p (c t) -> p c t", c=DCH)).then_inc(s_high, 1)
                elif name[0] == "v":
                    e.wait_ge(sf[bk_], need)
                    e.mul(V[:, 512 * int(name[1]):512 * int(name[1]) + 512], src[:, :], 1.0 / WS).then_inc(sd[bk_], 1)
                elif name[:2] == "pv":
                    e.wait_ge(sf[bk_], need)
                    g = int(name[2])
                    e.copy(oTh[:, 4 * g:4 * g + 4, :], src[:, :].rearrange("p (h t) -> p h t", h=4)).then_inc(s_high, 1)
                elif name == "sc":
                    e.wait_ge(shifted, j + 1)
                    e.activation(sS, sS, ACT.Exp, scale=float(HD) ** -0.5).then_inc(s_expd, 1)
                elif name == "log":
                    e.wait_ge(top_ready, j + 1)
                    e.activation(etop[:, :], top[:, :], ACT.Exp, bias=ntop[:, :], accum_out=esum[:, :]).then_inc(e_ready, 1)
                    e.activation(h3[:, D:D + E], lg[:, :], ACT.Exp, bias=ntop[:, :]).then_inc(e_ready, 1)

            def spread(j, q):
                e.wait_ge(sT_ready, j + 1)
                qs = slice(32 * q, 32 * q + 32)
                e.copy(diag[qs, :, qs], sT[qs]).then_inc(diag_ready, 1)

            def tile(i, j, m):
                if i is not None:
                    for name in ("hT", "qa", "qb", "kt0"):
                        x_use(name, i)

                def uses(names):
                    for name in names:
                        if (m if name in ROUTER else j) is not None:
                            s_use(name, m if name in ROUTER else j)

                for r in range(STEPS):
                    if i is not None:
                        if r < ROWS:
                            exp_row(i, r)
                        if 1 <= r <= ROWS:
                            copy_row(i, r - 1)
                        for name in X_AT.get(r, ()):
                            if name != "out":
                                x_use(name, i)
                    uses(BEHIND.get(r, ()))
                    if j is not None and r in (8, 9):
                        for q in (0, 1) if r == 8 else (2, 3):
                            spread(j, q)

            tile(0, None, None)
            e.wait_ge(zeroed, 3)
            tile(1, 0, None)
            with e.Fori(1, T - 1) as j:
                tile(j + 1, j, j - 1)
            tile(None, T - 1, T - 2)
            tile(None, None, T - 1)

            def expert_copy(ex, n):
                e.wait_ge(e_t, ex + 1)
                e.copy(xeT[:, n % 2], bank[n % 2][:, 0:D].rearrange("p (c t) -> p c t", c=DCH)).then_inc(e_tc, 1)

            def experts(j, last):
                for n in range(NB):
                    if not (last and n == NB - 1):
                        expert_copy(j * NB + n + 1, n + 1)
                    e.wait_ge(e_gu, j * NB + n + 1)
                    e.activation(sg[:, n % 2], bank[2 + n % 2][0:I, 0:P], ACT.Silu).then_inc(e_silu, 1)

            expert_copy(0, 0)
            with e.Fori(0, E // NB - 1) as j:
                experts(j, False)
            experts(E // NB - 1, True)

        @block.vector
        def _(e):
            e.memset(count[:, :], 0.0).then_inc(zeroed, 1)
            e.memset(X[:, T, :], 0.0).then_inc(zeroed, 1)
            e.wait_ge(rw_t, 1)
            e.tensor_copy(rwT[:, :, :], bank[7][:, 0:DCH * E].rearrange("p (c n) -> p c n", c=DCH)).then_inc(rwT_ready, 1)

            done = {}
            LINKS = {"x": (x_link, XLINKS), "s": (s_link, SLINKS), "r": (r_link, RLINKS), "n": (n_link, 0)}

            def link(ins, which, base):
                done[which] = done.get(which, 0) + 1
                s, n = LINKS[which]
                ins.then_inc(s, 1)
                e.wait_ge(s, base * n + done[which])

            def root(var, y, t, which, base):
                link(e.tensor_scalar(var, var, 1e-5, None, ALU.add), which, base)
                link(e.tensor_scalar(t.bitcast(u32), var.bitcast(u32), 1, None, ALU.logical_shift_right), which, base)
                link(e.tensor_scalar(y.bitcast(u32), t.bitcast(u32), -1.0, float(0x5f3759df), ALU.mult, ALU.add), which, base)
                for _ in range(NEWTON):
                    link(e.tensor_tensor(t, y, y, ALU.mult), which, base)
                    link(e.scalar_tensor_tensor(t, t, -0.5, var, ALU.mult, ALU.mult), which, base)
                    link(e.scalar_tensor_tensor(y, t, 1.5, y, ALU.add, ALU.mult), which, base)

            e.wait_ge(x_in, 16)
            e.wait_ge(zeroed, 2)
            for t in range(T + 1):
                e.bn_stats(st0[:, t, :], X[:, t, :]).then_inc(n_link, 1)
            e.wait_ge(n_link, T + 1)
            for t in range(T + 1):
                e.bn_aggr(mv0[:, t, :], st0[:, t, :]).then_inc(n_link, 1)
            e.wait_ge(n_link, 2 * T + 2)
            done["n"] = 2 * T + 2
            root(mv0[:, :, 1], rs0[:, 0, :], rs0[:, 1, :], "n", 0)
            with e.Fori(0, GROUPS // 2) as j:
                for half in range(2):
                    g = j * 2 + half
                    e.wait_ge(f_t, g + 1)
                    for p in range(2):
                        e.tensor_copy(fqrT[:, 2 * p:2 * p + 2], bank[2 + p][0:R, 0:4 * QC].rearrange("p (h c d) -> p h c d", h=2, c=2)).then_inc(f_td, 1)
                    e.tensor_copy(fkrT, bank[4][0:R, 0:GH * DC].rearrange("p (h d) -> p h d", h=GH)).then_inc(f_td, 1)
                    e.wait_ge(f_g, g + 1)
                    e.tensor_copy(fG, bank[7][0:QC, :].rearrange("p (h c d) -> p h c d", h=GH, c=2)).then_inc(f_gd, 1)
                    e.wait_ge(f_q, g + 1)
                    e.tensor_copy(fQ, bank[1][:, 0:GH * DC].rearrange("p (h d) -> p h d", h=GH)).then_inc(f_qd, 1)
                    for n in range(4):
                        e.wait_ge(w_in[n], g * 80 + 80)
                        e.scalar_tensor_tensor(parts[n][:, 0], parts[n][:, 0], WS, parts[n][:, 1], ALU.mult, ALU.mult).then_inc(w_mul, 1)
                    e.wait_ge(f_m, g + 1)
                    e.tensor_copy(M[:, :, bass.ds(g * (GH * DC), GH * DC)], bank[2][:, :].rearrange("p (c n) -> p c n", c=DCH)).then_inc(f_md, 1)

            def norm(dst, t, which, base, st, mv, rs, ready):
                src = X[:, bass.ds(t, 1), :].rearrange("p o d -> p (o d)")
                alone(e)
                link(e.bn_stats(st[:, :], src), which, base)
                alone(e)
                link(e.bn_aggr(mv[:, :], st[:, :]), which, base)
                root(mv[:, 1:2], rs[:, 0:1], rs[:, 1:2], which, base)
                e.tensor_scalar(dst[:, 0:D], src, mv[:, 0:1], rs[:, 0:1], ALU.subtract, ALU.mult).then_inc(ready, 1)

            def max_row(i, r):
                e.wait_ge(scored, i * ROWS + r + 1)
                s = r % (2 * RB)
                e.tensor_reduce(nmax[:, s:s + 1], bank[r % 2][:, 0:NL], AX.X, ALU.max, negate=True).then_inc(maxed, 1)

            def normalise(i, b):
                e.wait_ge(summed, i * ROWS + RB * (b + 1))
                e.wait_ge(last_ready, i * BT + b + 1)
                link(e.tensor_tensor(On[:, b % 2], bank[3][:, 0:RB * DC].rearrange("p (r d) -> p r d", r=RB),
                                     On[:, b % 2], ALU.add), "x", i)
                s = RB * (b % 2)
                link(e.reciprocal(rinv[:, s:s + RB], rsum[:, s:s + RB]), "x", i)
                e.tensor_tensor(On[:, b % 2], On[:, b % 2], rinv[:, s:s + RB].unsqueeze(2).to_broadcast([P, RB, DC]),
                                ALU.mult).then_inc(on_ready, 1)

            def x_out(i):
                bk_, need = xpos("out", i)
                e.wait_ge(xf[bk_], need)
                src = X[:, bass.ds(i, 1), :].rearrange("p o d -> p (o d)")
                e.tensor_tensor(src, src, XBANK[bk_][:, 0:D], ALU.add).then_inc(xd[bk_], 1)
                e.wait_ge(xd[bk_], need + FREE)
                norm(h2, i, "x", i, st1, mv1, rs1, h2_ready)

            def softmax_sum(j):
                e.wait_ge(s_expd, j + 1)
                link(e.tensor_reduce(ssum[:, :], sS, AX.X, ALU.add), "s", j)
                link(e.reciprocal(sinv[:, :], ssum[:, :]), "s", j)

            def softmax_end(j):
                link(e.tensor_tensor(sS, sS, sinv[:, :].unsqueeze(2).to_broadcast([P, H, S]), ALU.mult), "s", j)
                e.transpose(sT, sS).then_inc(sT_ready, 1)

            def s_use(name, j):
                bk_, need = spos(name, j)
                src = SBANK[bk_]
                if name[0] in "qk":
                    e.wait_ge(sf[bk_], need)
                    g, w = int(name[1]), int(name[0] == "k")
                    e.scalar_tensor_tensor((qS, kS)[w][:, 4 * g:4 * g + 4, :], src[:, :].rearrange("p (h t) -> p h t", h=4), 1.0 / WS,
                                           bqk[:, w, 4 * g:4 * g + 4].unsqueeze(2).to_broadcast([P, 4, P]), ALU.mult, ALU.add).then_inc(sd[bk_], 1)
                elif name == "sc":
                    e.wait_ge(sf[bk_], need)
                    s3 = src[:, :].rearrange("p (h t) -> p h t", h=H)
                    link(e.tensor_reduce(smax[:, :], s3, AX.X, ALU.max), "s", j)
                    e.tensor_tensor(sS, s3, smax[:, :].unsqueeze(2).to_broadcast([P, H, S]), ALU.subtract).then_inc(sd[bk_], 1)
                    e.wait_ge(sd[bk_], need + FREE)
                    e.nop().then_inc(shifted, 1)
                elif name == "hT":
                    e.wait_ge(s_high, j * 5 + 1)
                    e.tensor_tensor(h2l, src[:, 0:D].rearrange("p (c t) -> p c t", c=DCH), h2h, ALU.subtract).then_inc(sd[bk_], 1)
                elif name[:2] == "pv":
                    g = int(name[2])
                    e.wait_ge(s_high, j * 5 + g + 2)
                    e.tensor_tensor(oTl[:, 4 * g:4 * g + 4, :], src[:, :].rearrange("p (h t) -> p h t", h=4),
                                    oTh[:, 4 * g:4 * g + 4, :], ALU.subtract).then_inc(sd[bk_], 1)
                elif name == "log":
                    e.wait_ge(sf[bk_], need)
                    e.tensor_copy(lg[:, :], src[:, 0:E]).then_inc(sd[bk_], 1)
                    e.wait_ge(sd[bk_], need + FREE)
                    alone(e)
                    link(e.max(top[:, :], lg[:, :]), "r", j)
                    e.tensor_scalar(ntop[:, :], top[:, 0:1], -1.0, None, ALU.mult).then_inc(top_ready, 1)
                    link(e.max_index(topi[:, :], top[:, :], lg[:, :]), "r", j)
                elif name == "pos":
                    e.wait_ge(sf[bk_], need)
                    link(e.tensor_tensor(sv[:, :], src[:, 0:E], slot0[:, :], ALU.add), "r", j)
                    e.scalar_tensor_tensor(sv2[:, :], src[:, 0:E], float(CAP), sv[:, :], ALU.is_lt, ALU.mult).then_inc(sd[bk_], 1)
                    e.wait_ge(sd[bk_], need + FREE)
                    link(e.tensor_tensor(count[:, :], count[:, :], mask[:, :], ALU.add), "r", j)

            def chosen(j):
                link(e.tensor_copy(topf[:, :], topi[:, :]), "r", j)
                link(e.tensor_tensor(oh, iota_e[:, :].unsqueeze(1).to_broadcast([P, TOPK, E]),
                                     topf[:, :].unsqueeze(2).to_broadcast([P, TOPK, E]), ALU.is_equal), "r", j)
                with nc.allow_low_precision(reason="zeros and ones"):
                    e.tensor_reduce(mask[:, :], oh.rearrange("p k e -> p e k"), AX.X, ALU.add).then_inc(mask_ready, 1)
                e.wait_ge(mask_ready, j + 1)

            def weigh(j):
                e.wait_ge(e_ready, j * 2 + 2)
                link(e.reciprocal(einv[:, :], esum[:, :]), "r", j)
                link(e.tensor_scalar(h3[:, D:D + E], h3[:, D:D + E], einv[:, :], None, ALU.mult), "r", j)
                link(e.tensor_scalar(h3[:, D + E:ROW], h3[:, D + E:ROW], float(P), None, ALU.add), "r", j)

            def place(j):
                link(e.tensor_tensor(oh2, oh, sv2[:, :].unsqueeze(1).to_broadcast([P, TOPK, E]), ALU.mult), "r", j)
                link(e.tensor_reduce(slotf[:, :], oh2, AX.X, ALU.add), "r", j)
                e.tensor_scalar(slot[:, :], slotf[:, :], float(NOSLOT), None, ALU.add).then_inc(slot_ready, 1)

            def self_out(j):
                bk_, need = spos("wo", j)
                src = SBANK[bk_]
                e.wait_ge(sf[bk_], need)
                src2 = X[:, bass.ds(j, 1), :].rearrange("p o d -> p (o d)")
                e.scalar_tensor_tensor(src2, src[:, 0:D], 1.0 / WS, src2, ALU.mult, ALU.add).then_inc(sd[bk_], 1)
                e.wait_ge(sd[bk_], need + FREE)
                link(e.tensor_tensor(src2, src2, obias[:, :], ALU.add), "s", j)
                e.wait_ge(h3_free, j + FREE)
                norm(h3, j, "s", j, st2, mv2, rs2, h3_ready)

            def next_h1(i):
                e.tensor_scalar(h1[:, :], X[:, bass.ds(i, 1), :].rearrange("p o d -> p (o d)"),
                                mv0[:, bass.ds(i, 1), 0:1].rearrange("p o d -> p (o d)"), rs0[:, 0, bass.ds(i, 1)],
                                ALU.subtract, ALU.mult).then_inc(h1_ready, 1)

            def tile(i, j, m):
                done.clear()
                def uses(names):
                    for name in names:
                        if (m if name in ROUTER else j) is not None:
                            s_use(name, m if name in ROUTER else j)

                for r in range(STEPS):
                    if i is not None:
                        if r < ROWS:
                            max_row(i, r)
                        if r % RB == 1 and r > RB:
                            normalise(i, r // RB - 1)
                        if "out" in X_AT.get(r, ()):
                            x_out(i)
                        if r == 10:
                            next_h1(i + 1)
                    uses(BEHIND.get(r, ()))
                    if j is not None and r == 6:
                        softmax_sum(j)
                    if j is not None and r == 7:
                        softmax_end(j)
                    if m is not None and r == 7:
                        chosen(m)
                    if m is not None and r == 8:
                        weigh(m)
                    if m is not None and r == 10:
                        place(m)
                if j is not None:
                    self_out(j)
                assert i is None or done["x"] == XLINKS, done
                assert j is None or done["s"] == SLINKS, done
                assert m is None or done["r"] == RLINKS, done

            e.sem_inc(h3_free, FREE)
            e.wait_ge(iotas, 2)
            e.wait_ge(w_done, 16)
            e.memset(diag[:, :, :], 0.0).then_inc(zeroed, 1)
            e.wait_ge(bias_in, 64)
            e.tensor_copy(bvh[:, :], bvT[:, :]).then_inc(bv_split, 1)
            e.wait_ge(bv_split, 1)
            e.tensor_tensor(bvl[:, :], bvT[:, :], bvh[:, :], ALU.subtract).then_inc(bv_split, 1)
            next_h1(0)
            tile(0, None, None)
            e.wait_ge(zero_out, 16 * (1 + NY))
            e.tensor_scalar(h3[:, D + E:ROW], h3[:, D + E:ROW], float(-(B * S + P)), None, ALU.add).then_inc(zeroed, 1)
            e.wait_ge(zeroed, 4)
            e.wait_ge(ob_mm, 1)
            e.scalar_tensor_tensor(obias[:, :], bank[7][:, 0:D], 1.0 / WS, obias[:, :], ALU.mult, ALU.add).then_inc(ob_ready, 1)
            e.wait_ge(ob_ready, 1)
            tile(1, 0, None)
            with e.Fori(1, T - 1) as j:
                tile(j + 1, j, j - 1)
            tile(None, T - 1, T - 2)
            tile(None, None, T - 1)

            def experts(j, first):
                for n in range(NB):
                    e.wait_ge(e_silu, j * NB + n + 1)
                    e.tensor_tensor(hh[:, n % 2], sg[:, n % 2], bank[2 + n % 2][0:I, P:2 * P], ALU.mult).then_inc(e_h, 1)
                    if not (first and n == 0):
                        m = (n - 1) % NB
                        e.wait_ge(e_dn, j * NB + n)
                        if not first or m >= 4:
                            e.wait_ge(ye_out[m % 4], j * 32 + (16 * (m // 4) if n else -16))
                        weighted(m, j * NB + n - 1)

            def weighted(m, ex):
                e.tensor_copy(etok[:, m % 4:m % 4 + 1], xe[:, m, D + E:ROW])
                e.tensor_scalar(ye[:, m % 4], bank[4 + m % 2][:, 0:D], xe[:, m, bass.ds(ex + D, 1)], None, ALU.mult).then_inc(e_ye, 1)

            experts(0, True)
            with e.Fori(1, E // NB) as j:
                experts(j, False)
            e.wait_ge(e_dn, E)
            e.wait_ge(ye_out[3], 16 * (E // 4 - 1))
            weighted(NB - 1, E - 1)
            for c in range(T // FC):
                e.wait_ge(sums_in[c], 16 * NY)
                for y in range(NY):
                    ins = e.tensor_tensor(X[:, FC * c:FC * c + FC, :], X[:, FC * c:FC * c + FC, :], ysum[:, y, FC * c:FC * c + FC, :], ALU.add)
                    if y < NY - 1:
                        ins.then_inc(y_link, 1)
                        e.wait_ge(y_link, c * (NY - 1) + y + 1)
                ins.then_inc(y_ready, 1)

        @block.tensor
        def _(e):
            for s in (f_na, f_md, xd[0], xd[1], sd[0], sd[1]):
                e.sem_inc(s, FREE)
            e.wait_ge(consts, 2)
            e.wait_ge(rw_in, 16)
            for c in range(DCH):
                ins = e.transpose(bank[7][:, c * E:(c + 1) * E], rwr[:, c * P:(c + 1) * P], ident[0:E, 0:E])
            ins.then_inc(rw_t, 1)
            e.wait_ge(rwT_ready, 1)

            with e.Fori(0, GROUPS // 2) as j:
                for half in range(2):
                    g = j * 2 + half
                    e.wait_ge(fold_in[half], j * 128 + 128)
                    e.wait_ge(f_na, g + FREE)
                    e.wait_ge(f_md, g + FREE)
                    for h in range(GH):
                        p, o = h // 2, 256 * (h % 2)
                        for c in range(2):
                            e.transpose(bank[p][0:QC, o + c * P:o + (c + 1) * P], fkq[half][:, h, c * QC:(c + 1) * QC], ident[:, :])
                            e.transpose(bank[2 + p][0:R, (2 * (h % 2) + c) * QC:(2 * (h % 2) + c + 1) * QC], fqr[half][:, h, c, :], ident[0:QC, 0:QC])
                            e.transpose(bank[5 + p][:, o + c * P:o + (c + 1) * P], fWo[half][:, c, h, :], ident[:, :])
                        ins = e.transpose(bank[4][0:R, h * DC:(h + 1) * DC], fkr[half][:, h, :], ident[0:DC, 0:DC])
                    ins.then_inc(f_t, 1)
                    e.wait_ge(f_td, g * 3 + 3)
                    for h in range(GH):
                        for c in range(2):
                            ins = e.matmul(bank[7][0:QC, (2 * h + c) * DC:(2 * h + c + 1) * DC], fqrT[:, h, c, :], fkrT[:, h, :], start=True, stop=True)
                    ins.then_inc(f_g, 1)
                    e.wait_ge(f_ta, g * 4 + 4)
                    for h in range(GH):
                        q = DC * (h % 2)
                        ins = e.matmul(bank[0][q:q + DC, (h // 2) * D:(h // 2 + 1) * D], fkv[half][:, h, :], fWoT[:, h, :], start=True, stop=True)
                    ins.then_inc(f_n, 1)
                    e.wait_ge(f_gd, g + 1)
                    for h in range(GH):
                        for c in range(2):
                            ins = e.matmul(bank[1][:, h * DC:(h + 1) * DC], fkqT[:, h, c, :], fG[:, h, c, :], start=c == 0, stop=c == 1)
                    ins.then_inc(f_q, 1)
                    e.wait_ge(f_qd, g + 1)
                    for h in range(GH):
                        for c in range(DCH):
                            ins = e.matmul(bank[2][:, c * 256 + h * DC:c * 256 + (h + 1) * DC], fWq[half][:, h, c * P:(c + 1) * P], fQ[:, h, :], start=True, stop=True)
                    ins.then_inc(f_m, 1)
            e.wait_ge(f_md, GROUPS + FREE)
            e.wait_ge(f_na, GROUPS + FREE)

            def split(dst, terms, first=True, last=True):
                for n, (ah, al, bh, bl) in enumerate(terms):
                    e.matmul(dst, ah, bh, start=first and n == 0, stop=False)
                    e.matmul(dst, ah, bl, start=False, stop=False)
                    ins = e.matmul(dst, al, bh, start=False, stop=last and n == len(terms) - 1)
                return ins

            def x_use(name, i):
                bk_, need = xpos(name, i)
                dst = XBANK[bk_]
                e.wait_ge(xd[bk_], need - 1 + FREE)
                if name == "hT":
                    e.wait_ge(h1_ready, i + 1)
                    for c in range(DCH):
                        ins = e.transpose(dst[:, c * P:(c + 1) * P], h1[:, c * P:(c + 1) * P], ident[:, :])
                elif name in ("qa", "qb"):
                    wait_pos(e, xd, xpos("hT", i))
                    for n in range(4):
                        c = n + 4 * (name == "qb")
                        for k in range(DCH):
                            ins = e.matmul(dst[:, n * P:(n + 1) * P], M[:, k, c * P:(c + 1) * P], h1T[:, k, :], start=k == 0, stop=k == DCH - 1)
                elif name[:2] == "kt":
                    b = int(name[2])
                    e.wait_ge(roped, i * 2 + 2)
                    for c in range(2):
                        e.transpose(dst[:, c * P:(c + 1) * P], Cr[:, b, c].rearrange("p t d -> p (t d)"), ident[:, :])
                    ins = e.transpose(dst[:, 2 * P:NL], Cr[0:1, b, 2].rearrange("p t d -> p (t d)"), ident[0:1, 0:1])
                elif name[:2] == "cT":
                    b = int(name[2])
                    e.wait_ge(on_ready, i * BT + b + 1)
                    for g in range(2):
                        ins = e.transpose(dst[:, g * P:(g + 1) * P], On[:, b % 2, 2 * g:2 * g + 2, :].rearrange("p r d -> p (r d)"), ident[:, :])
                else:
                    wait_pos(e, xd, xpos("cT3", i))
                    for c in range(HP):
                        ins = e.matmul(dst[:, 0:D], cT[:, c, :], N[:, c, :], start=c == 0, stop=c == HP - 1)
                ins.then_inc(xf[bk_], 1)

            def score_row(i, r):
                b, g, q = r // RB, r % RB // 2, DC * (r % 2)
                if r % RB == 0:
                    wait_pos(e, xd, xpos(f"kt{b}", i))
                if r == 0:
                    wait_pos(e, xd, xpos("qb", i))
                e.wait_ge(expd, i * ROWS + r - 1 if r else i * ROWS)
                e.matmul(bank[r % 2][:, 0:NL], qT[q:q + DC, b, 4 * g:4 * g + 4, :], KT[q:q + DC, b % 2, :],
                         start=True, stop=True).then_inc(scored, 1)

            def transpose_row(i, r):
                e.wait_ge(expd, i * ROWS + r + 1)
                e.wait_ge(pt_ready, i * ROWS + r)
                for c in range(2):
                    ins = e.transpose(bank[2][:, c * P:(c + 1) * P], pr[:, r % (2 * RB), c * P:(c + 1) * P], ident[:, :])
                ins.then_inc(transposed, 1)

            def sum_row(i, r):
                b = r // RB
                e.wait_ge(pt_ready, i * ROWS + r + 1)
                if r % RB == 0:
                    e.wait_ge(on_ready, i * BT + b)
                o = DC * (r % RB)
                for c in range(2):
                    ins = e.matmul(bank[3][:, o:o + DC], pT[:, r % 2, c, :], Cr[:, b, c, 0, :], start=c == 0, stop=c == 1)
                ins.then_inc(summed, 1)

            def s_use(name, j):
                bk_, need = spos(name, j)
                dst = SBANK[bk_]
                if name not in ("wo1", "wo2", "wo3"):
                    e.wait_ge(sd[bk_], need - 1 + FREE)
                if name in ("hT", "rT"):
                    e.wait_ge(h2_ready if name == "hT" else h3_ready, j + 1)
                    src = h2 if name == "hT" else h3
                    for c in range(DCH):
                        ins = e.transpose(dst[:, c * P:(c + 1) * P], src[:, c * P:(c + 1) * P], ident[:, :])
                elif name[0] in "qk":
                    wait_pos(e, sd, spos("hT", j))
                    w = 2 * (name[0] == "k")
                    for n in range(4):
                        h = 4 * int(name[1]) + n
                        ins = split(dst[:, n * P:(n + 1) * P], [(Wh[:, w + k, h * HD:(h + 1) * HD], Wl[:, w + k, h * HD:(h + 1) * HD],
                                                                 h2h[:, k, :], h2l[:, k, :]) for k in range(DCH)])
                elif name == "sc":
                    wait_pos(e, sd, spos("k3", j))
                    for h in range(H):
                        for q in range(4):
                            qs = slice(32 * q, 32 * q + 32)
                            ins = e.matmul(dst[qs, h * S:(h + 1) * S], qS[:, h, qs], kS[:, h, qs], start=True, stop=True, tile_position=(0, 32 * q))
                elif name[0] == "v":
                    o = 512 * int(name[1])
                    ins = split(dst[:, :], [(h2h[:, k, :], h2l[:, k, :], Wh[:, 4 + k, o:o + 512], Wl[:, 4 + k, o:o + 512])
                                            for k in range(DCH)])
                elif name[:2] == "pv":
                    e.wait_ge(diag_ready, j * 4 + 4)
                    wait_pos(e, sd, spos("v3", j))
                    for n in range(4):
                        h = 4 * int(name[2]) + n
                        ins = e.matmul(dst[:, n * P:(n + 1) * P], V[:, h * HD:(h + 1) * HD], diag[:, h, :], start=True, stop=True)
                elif name[:2] == "wo":
                    if name == "wo0":
                        wait_pos(e, sd, spos("pv3", j))
                    a = 4 * int(name[2])
                    ins = split(dst[:, 0:D], [(oTh[:, h, :], oTl[:, h, :], Wh[:, 6 + h // 8, (h % 8) * D:(h % 8 + 1) * D],
                                               Wl[:, 6 + h // 8, (h % 8) * D:(h % 8 + 1) * D]) for h in range(a, a + 4)],
                                first=a == 0, last=a == 12)
                elif name == "log":
                    wait_pos(e, sd, spos("rT", j))
                    for k in range(DCH):
                        ins = e.matmul(dst[:, 0:E], h3T[:, k, :], rwT[:, k, :], start=k == 0, stop=k == DCH - 1)
                elif name == "pos":
                    e.wait_ge(mask_ready, j + 1)
                    e.matmul(dst[:, 0:E], before[:, :], mask[:, :], start=True, stop=False)
                    ins = e.matmul(dst[:, 0:E], ones16[:, :], count[:, :], start=False, stop=True)
                if name not in ("wo0", "wo1", "wo2"):
                    ins.then_inc(sf[bk_], 1)

            def skip(name, j):
                bk_, need = spos(name, j)
                e.wait_ge(sd[bk_], need - 1 + FREE)
                e.sem_inc(sf[bk_], 1)
                e.sem_inc(sd[bk_], 1)

            def tile(i, j, m):

                def uses(names):
                    for name in names:
                        if j is None and m is None:
                            continue
                        t = m if name in ROUTER else j
                        if t is not None:
                            s_use(name, t)
                        elif j is None:
                            if name not in ("wo0", "wo1", "wo2"):
                                skip(name, m + 1)
                        else:
                            skip(name, j - 1)

                if i is not None:
                    for name in ("hT", "qa", "qb", "kt0"):
                        x_use(name, i)
                for r in range(STEPS):
                    if i is not None:
                        if r < ROWS:
                            score_row(i, r)
                        if 1 <= r <= ROWS:
                            transpose_row(i, r - 1)
                        if 2 <= r <= ROWS + 1:
                            sum_row(i, r - 2)
                        for name in X_AT.get(r, ()):
                            x_use(name, i)
                    uses(BEHIND.get(r, ()))

            tile(0, None, None)
            e.wait_ge(w_done, 16)
            e.wait_ge(bv_split, 2)
            ins = split(bank[7][:, 0:D], [(bvh[:, h:h + 1].to_broadcast([P, P]), bvl[:, h:h + 1].to_broadcast([P, P]),
                                           Wh[:, 6 + h // 8, (h % 8) * D:(h % 8 + 1) * D],
                                           Wl[:, 6 + h // 8, (h % 8) * D:(h % 8 + 1) * D]) for h in range(H)])
            ins.then_inc(ob_mm, 1)
            e.wait_ge(ob_ready, 1)
            tile(1, 0, None)
            with e.Fori(1, T - 1) as j:
                tile(j + 1, j, j - 1)
            tile(None, T - 1, T - 2)
            tile(None, None, T - 1)

            def expert_t(j, n):
                e.wait_ge(xe_in[n], j * 16 + 16)
                for c in range(DCH):
                    ins = e.transpose(bank[n % 2][:, c * P:(c + 1) * P], xe[:, n, c * P:(c + 1) * P], ident[:, :])
                ins.then_inc(e_t, 1)

            def expert_gate_up(j, n):
                e.wait_ge(ew_in[n], j * 32 + 32)
                e.wait_ge(e_tc, j * NB + n + 1)
                for half in range(2):
                    for c in range(DCH):
                        ins = e.matmul(bank[2 + n % 2][0:I, half * P:(half + 1) * P], gu[:, n, c, half * I:(half + 1) * I], xeT[:, n % 2, c, :],
                                       start=c == 0, stop=c == DCH - 1)
                ins.then_inc(e_gu, 1)

            def expert_down(j, n, before_that):
                e.wait_ge(e_h, before_that + 1)
                if not isinstance(before_that, int) or before_that >= 2:
                    e.wait_ge(e_ye, before_that - 1)
                e.matmul(bank[4 + n % 2][:, 0:D], hh[:, n % 2], dn[:, n], start=True, stop=True).then_inc(e_dn, 1)

            def experts(j, first, last):
                for n in range(NB):
                    if n < NB - 1:
                        expert_t(j, n + 1)
                    elif not last:
                        expert_t(j + 1, 0)
                    expert_gate_up(j, n)
                    if not (first and n == 0):
                        expert_down(j, (n - 1) % NB, j * NB + n - 1)

            expert_t(0, 0)
            experts(0, True, False)
            with e.Fori(1, E // NB - 1) as j:
                experts(j, False, False)
            experts(E // NB - 1, False, True)
            expert_down(E // NB - 1, NB - 1, E - 1)


_NAMES = ["x", "ctx_512", "L0_xattn_Wq", "L0_xattn_w_kc_q", "L0_xattn_w_kc_kv", "L0_xattn_W_qr", "L0_xattn_W_kr",
          "L0_xattn_Wo", "L0_attn_wq_codes", "L0_attn_wk_codes", "L0_attn_wv_codes", "L0_attn_wo_codes",
          "L0_attn_wq_scales", "L0_attn_wk_scales", "L0_attn_wv_scales", "L0_attn_wo_scales", "L0_attn_bq",
          "L0_attn_bk", "L0_attn_bv", "L0_attn_bo", "L0_ffn_router_weight", "L0_ffn_gate_up_proj", "L0_ffn_down_proj"]


def rope_tables():
    import numpy as np
    inv = (np.float32(1.0) / np.float32(10000.0) ** (np.arange(0, DC, 2, dtype=np.float32) / np.float32(DC))).astype(np.float32)
    f = np.arange(NL, dtype=np.float32)[:, None] * inv[None, :]
    sin, cos = (np.repeat(t.astype(np.float32), 2, axis=-1) for t in (np.sin(f), np.cos(f)))
    sin = np.concatenate([-sin[:, :DC // 2], sin[:, DC // 2:]], axis=-1)
    lay = lambda t: np.ascontiguousarray(np.stack([t[:P], t[P:2 * P], np.repeat(t[2 * P:], P, axis=0)], axis=1))
    return lay(cos), lay(sin)


def kernel(**inputs):
    import numpy as np
    import concourse.bacc as bacc
    from concourse.bass_utils import run_bass_kernel_spmd

    nc = bacc.Bacc("TRN2", target_bir_lowering=False, num_devices=1)
    arrays, aps = {}, {}

    def give(name, a):
        arrays[name + "_dram"] = a
        aps[name] = nc.dram_tensor(name + "_dram", a.shape, mybir.dt.from_np(a.dtype), kind="ExternalInput").ap()

    for name in _NAMES:
        a = np.ascontiguousarray(inputs[name])
        give(name, a.reshape(B * S, D) if name == "x" else a)
    cos, sin = rope_tables()
    give("rope_cos", cos)
    give("rope_sin", sin)
    out = nc.dram_tensor("out_dram", [B * S, D], mybir.dt.float32, kind="ExternalOutput").ap()
    v = [aps[n] for n in _NAMES]
    build(nc, *v[:8], v[8:12], v[12:16], *v[16:], aps["rope_cos"], aps["rope_sin"], out)
    r = run_bass_kernel_spmd(nc, [arrays], core_ids=[0])
    return r.results[0]["out_dram"].reshape(B, S, D)
```

```python
import concourse.bass as bass
from concourse import mybir
from contextlib import ExitStack

B, S, D = 32, 32, 256
NL, DC, DQ, R = 257, 64, 192, 64
H, HD = 16, 128
F = H * HD
E, I, TOPK, CAP = 64, 96, 8, 128

P = 128
T = B * S // P
BT = P // S
DCH = D // P
HP = H // 2
ROWS = BT * H * S // P
RB = ROWS // BT
QC = DQ // 2
GH = 4
GROUPS = H // GH
NOSLOT = E * CAP
ROW = D + E + 1
YROWS = (T + 1) * P
NY = 2
FC = 2

XS = ["kt1", "kt2", "cT0", "kt3", "cT1", "cT2", "hT", "qa", "qb", "cT3", "kt0", "out"]
XSPLIT = ["kt1", "kt2", "kt3", "qa", "qb", "kt0"]
XNEXT = ("hT", "qa", "qb", "kt0")
X_AT = {2: ["kt1"], 6: ["kt2"], 7: ["cT0"], 10: ["kt3"], 11: ["cT1"], 15: ["cT2", "hT"], 16: ["qa"], 18: ["qb"],
        19: ["cT3", "kt0"], 20: ["out"]}
SS = ["wo", "hT", "q0", "q1", "q2", "q3", "k0", "rT", "k1", "k2", "log", "k3", "sc", "v0", "pos", "v1", "v2", "v3",
      "pv0", "pv1", "pv2", "pv3"]
BEFORE = ("wo", "rT", "log", "pos")
BEHIND = {0: ["wo0"], 1: ["wo1"], 2: ["wo2"], 3: ["hT", "wo3"], 4: ["q0"], 5: ["q1"], 6: ["q2", "q3"], 7: ["k0", "rT"],
          8: ["k1", "k2", "log"], 9: ["k3"], 10: ["sc"], 11: ["v0", "pos"], 12: ["v1"], 13: ["v2"], 14: ["v3"],
          15: ["pv0"], 16: ["pv1"], 17: ["pv2"], 18: ["pv3"]}
WS = 16.0
STEPS = ROWS + 5
PARTS = 16
FOLD_PARTS = (0, 0, 2, 3)
PART0 = [sum(FOLD_PARTS[:g]) for g in range(GROUPS + 1)]
TILE_PARTS = dict(zip((0, 2, 3, 5, 6, 8, 9, 11, 12, 14, 15), range(PART0[GROUPS], PARTS)))
NPB = 6
BUFFER = [u % 3 for u in range(PART0[GROUPS])]
BUFFER += [(PART0[GROUPS] % 3 + n) % NPB for n in range(PARTS - PART0[GROUPS])]
NEWTON = 3
NLINKS = 6 + 2 * NEWTON
XLINKS = 2 * BT
SLINKS = NLINKS + 4
RLINKS = NLINKS + 12
NB = 8
FREE = 1


def build(nc, x, ctx_in, Wq, kcq, kckv, Wqr, Wkr, Wo_x, codes, scales, bq, bk, bv, bo, rw, gup, dnp,
          rope_cos, rope_sin, out):
    f32, bf16, f16, u32 = mybir.dt.float32, mybir.dt.bfloat16, mybir.dt.float16, mybir.dt.uint32
    ALU, ACT, AX = mybir.AluOpType, mybir.ActivationFunctionType, mybir.AxisListType

    ctx = ExitStack()
    with ctx:
        def sb(name, shape, dt=f32):
            return ctx.enter_context(nc.sbuf_tensor(name, shape, dt))

        def sem(name):
            return ctx.enter_context(nc.semaphore(name))

        bank = [ctx.enter_context(nc.psum_tensor(f"bank{n}", [P, 512], f32)) for n in range(8)]
        XE = nc.dram_tensor("expert_rows", [E * CAP, ROW], f32, kind="Internal").ap()
        Y = [nc.dram_tensor(f"expert_sums{n}", [YROWS, D], f32, kind="Internal").ap() for n in range(NY)]

        ident = sb("ident", [P, P])
        before = sb("before", [P, P], bf16)
        ones16 = sb("ones16", [P, P], bf16)
        iota_i = sb("iota_i", [P, E], mybir.dt.int32)
        iota_e = sb("iota_e", [P, E])
        spare_i = sb("spare_i", [P, 1], mybir.dt.int32)
        slot0 = sb("slot0", [P, E])
        X = sb("X", [P, T, D])
        M = sb("M", [P, DCH, H * DC])
        N = sb("N", [P, HP, D])
        Wh = sb("Wh", [P, 8, 2048], f16)
        Wl = sb("Wl", [P, 8, 2048], f16)
        bqk = sb("bqk", [P, 2, H])
        bvT = sb("bvT", [P, H])
        bvh = sb("bvh", [P, H], f16)
        bvl = sb("bvl", [P, H], f16)
        obias = sb("obias", [P, D])
        rwT = sb("rwT", [P, DCH, E])
        cosT = sb("cosT", [P, 3, DC])
        sinT = sb("sinT", [P, 3, DC])

        C = sb("C", [P, BT, 3, DC])
        Ct = sb("Ct", [P, BT, 3, DC])
        Cr = sb("Cr", [P, BT, 3, 2, DC])
        KTh = sb("KTh", [P, 2, NL + 1], f16)
        KTl = sb("KTl", [P, 2, NL + 1], f16)
        h1 = sb("h1", [P, D])
        h1T = sb("h1T", [P, DCH, P])
        qspace = sb("qspace", [P, BT * HP * S])
        q2 = [qspace[:, n * (BT * HP * S // 2):(n + 1) * (BT * HP * S // 2)].bitcast(f16).rearrange("p (b c s) -> p b c s", b=BT, c=HP)
              for n in range(2)]
        pr = sb("pr", [P, 2 * RB, NL])
        pT = sb("pT", [P, 2, 2, P])
        nmax = sb("nmax", [P, 2 * RB])
        rsum = sb("rsum", [P, 2 * RB])
        rinv = sb("rinv", [P, 2 * RB])
        On = sb("On", [P, 2, RB, DC])
        cT = sb("cT", [P, HP, P])
        st1 = sb("st1", [P, 6])
        mv1 = sb("mv1", [P, 2])
        st0 = sb("st0", [P, T, 6])
        mv0 = sb("mv0", [P, T, 2])
        rs0 = sb("rs0", [P, 2, T])
        rs1 = sb("rs1", [P, 2])
        rwr = h1[0:E, :]

        SPACE = 4 * 2048 + 2 * 256 + 2 * 512 + 2 * 512
        space = sb("space", [P, SPACE])
        at = [0]

        def cut(n, parts=P):
            a = at[0]
            at[0] += n
            assert at[0] <= SPACE
            return space[0:parts, a:a + n]

        fWq = [cut(GH * D).rearrange("p (h d) -> p h d", h=GH) for _ in range(2)]
        fkq = [cut(GH * DQ).rearrange("p (h d) -> p h d", h=GH) for _ in range(2)]
        fqr = [cut(GH * 2 * R, QC).rearrange("p (h c d) -> p h c d", h=GH, c=2) for _ in range(2)]
        fkr = [cut(GH * R, DC).rearrange("p (h d) -> p h d", h=GH) for _ in range(2)]
        fkv = [cut(GH * DC).rearrange("p (h d) -> p h d", h=GH) for _ in range(2)]
        fWo = [cut(DCH * GH * HD).rearrange("p (c h d) -> p c h d", c=DCH, h=GH) for _ in range(2)]
        fqrT = cut(GH * 2 * QC, R).rearrange("p (h c d) -> p h c d", h=GH, c=2)
        fkrT = cut(GH * DC, R).rearrange("p (h d) -> p h d", h=GH)
        fWoT = cut(GH * D).rearrange("p (h d) -> p h d", h=GH)
        fkqT = qspace[0:QC, :].rearrange("p (h c d) -> p h c d", h=GH, c=2)
        cflat = cT[:, :, :].rearrange("p a b -> p (a b)")
        fG = cflat[0:QC, 0:GH * 2 * DC].rearrange("p (h c d) -> p h c d", h=GH, c=2)
        fQ = cflat[:, 512:512 + GH * DC].rearrange("p (h d) -> p h d", h=GH)
        at[0] = 0
        qS = cut(H * P).rearrange("p (h t) -> p h t", h=H)
        kS = cut(H * P).rearrange("p (h t) -> p h t", h=H)
        V = cut(F)
        oTh, oTl = (cut(H * P // 2).bitcast(f16).rearrange("p (h t) -> p h t", h=H) for _ in range(2))
        h2h, h2l = (cut(DCH * P // 2).bitcast(f16).rearrange("p (c t) -> p c t", c=DCH) for _ in range(2))
        h3T = cut(DCH * P).rearrange("p (c t) -> p c t", c=DCH)
        sS = cut(H * S).rearrange("p (h t) -> p h t", h=H)
        sT = cut(H * S).rearrange("p (h t) -> p h t", h=H)
        oh = cut(TOPK * E).rearrange("p (k e) -> p k e", k=TOPK)
        oh2 = cut(TOPK * E).rearrange("p (k e) -> p k e", k=TOPK)
        diag = sb("diag", [P, H, P])
        h2 = sb("h2", [P, D])
        h3 = sb("h3", [P, ROW])
        st2 = sb("st2", [P, 6])
        mv2 = sb("mv2", [P, 2])
        rs2 = sb("rs2", [P, 2])
        smax = sb("smax", [P, H])
        ssum = sb("ssum", [P, H])
        sinv = sb("sinv", [P, H])
        lg = sb("lg", [P, E])
        top = sb("top", [P, TOPK])
        topi = sb("topi", [P, TOPK], u32)
        topf = sb("topf", [P, TOPK])
        ntop = sb("ntop", [P, 1])
        etop = sb("etop", [P, TOPK])
        esum = sb("esum", [P, 1])
        einv = sb("einv", [P, 1])
        mask = sb("mask", [P, E], bf16)
        count = sb("count", [P, E], bf16)
        sv = sb("sv", [P, E])
        sv2 = sb("sv2", [P, E])
        slotf = sb("slotf", [P, TOPK])
        slot = sb("slot", [P, TOPK], u32)

        ring = sb("ring", [P, NB * (DCH * 2 * I + D)])
        gu = ring[:, 0:NB * DCH * 2 * I].rearrange("p (n c f) -> p n c f", n=NB, c=DCH)
        dn = ring[0:I, NB * DCH * 2 * I:].rearrange("p (n d) -> p n d", n=NB)
        parts = [t.rearrange("p (n f) -> p n f", n=2) for t in (
            ring[:, 0:2048], ring[:, 2048:4096],
            diag[:, :, :].rearrange("p a b -> p (a b)"), space[:, 0:2048], space[:, 2048:4096], space[:, 4096:6144])]
        Wf = Wh[:, :, :].rearrange("p u f -> p (u f)").bitcast(f32)
        xeT = Wf[:, 0:512].rearrange("p (n c t) -> p n c t", n=2, c=DCH)
        sg = Wf[0:I, 512:768].rearrange("p (n t) -> p n t", n=2)
        hh = Wf[0:I, 768:1024].rearrange("p (n t) -> p n t", n=2)
        ye = Wf[:, 1024:2048].rearrange("p (n d) -> p n d", n=4)
        xe = Wf[:, 2048:2048 + NB * ROW].rearrange("p (n d) -> p n d", n=NB)
        ysum = Wl[:, :, :].rearrange("p u f -> p (u f)").bitcast(f32)[:, 0:NY * T * D].rearrange("p (y t d) -> p y t d", y=NY, t=T)
        etok = sb("etok", [P, 4], u32)

        x_in, tab_in, rw_in, bias_in, ctx_ld, zero_out = (sem(n) for n in (
            "x_in", "tables_in", "router_in", "biases_in", "context_in", "zero_out"))
        rope_in = [sem("fold_rope_in0"), sem("fold_rope_in1")]
        fold_in = [sem("fold_in0"), sem("fold_in1")]
        rest_in = [sem("fold_rest_in0"), sem("fold_rest_in1")]
        w_in = [sem(f"w_in{n}") for n in range(NPB)]
        ew_in = [sem(f"expert_weights_in{n}") for n in range(NB)]
        xe_in = [sem(f"expert_rows_in{n}") for n in range(NB)]
        ye_out = [sem(f"expert_out{n}") for n in range(4)]
        sums_in = [sem(f"sums_in{n}") for n in range(T // FC)]
        scat, h3_free, stored = sem("scattered"), sem("h3_free"), sem("stored")
        consts, iotas, zeroed, pool_link, rw_t, rwT_ready, ob_mm, ob_ready, w_done = (sem(n) for n in (
            "consts", "iotas", "zeroed", "pool_link", "router_transposed", "rwT_ready", "obias_summed",
            "obias_ready", "w_done"))
        w_mul, w_high, bv_split = sem("w_dequantised"), sem("w_high"), sem("bv_split")
        f_a, f_b, f_ta, f_td, f_g, f_gd, f_n, f_na, f_q, f_qd, f_m, f_md = (sem(n) for n in (
            "f_rope_transposed", "f_transposed", "f_act_copied", "f_dve_copied", "f_G", "f_G_copied", "f_N", "f_N_copied",
            "f_Q", "f_Q_copied", "f_M", "f_M_copied"))
        xf = [sem("x_filled0"), sem("x_filled1")]
        xd = [sem("x_drained0"), sem("x_drained1")]
        x_high = sem("x_high")
        x_link, r_link, n_link, sT_ready, h1_ready, rope_link, roped, scored, maxed, expd, transposed, pt_ready, summed, last_ready, on_ready = (
            sem(n) for n in ("x_link", "r_link", "n_link", "sT_ready", "h1_ready", "rope_link", "roped", "scored", "maxed", "expd", "transposed",
                             "pt_ready", "summed", "last_ready", "on_ready"))
        sf = [sem("s_filled0"), sem("s_filled1")]
        sd = [sem("s_drained0"), sem("s_drained1")]
        s_high, s_link, h2_ready, shifted, s_expd, diag_ready, h3_ready, top_ready, e_ready, mask_ready, slot_ready = (
            sem(n) for n in ("s_high", "s_link", "h2_ready", "shifted", "s_expd", "diag_ready", "h3_ready", "top_ready",
                             "e_ready", "mask_ready", "slot_ready"))
        e_t, e_tc, e_gu, e_silu, e_h, e_dn, e_ye = (sem(n) for n in (
            "e_transposed", "e_xT_ready", "e_gate_up", "e_silu", "e_hidden", "e_down", "e_out_ready"))
        y_link, y_ready = sem("y_link"), sem("y_ready")

        passed = sem("passed")

        def alone(e):
            e.sem_inc(passed, 1)

        block = ctx.enter_context(nc.Block())
        XBANK = (bank[4], bank[5])
        SBANK = (bank[6], bank[7])

        def xpos(name, i, more=1):
            n, i = XS.index(name), i if name in XNEXT else i + 1
            return n % 2, i * (len(XS) // 2) + n // 2 + more

        def spos(name, j, more=1):
            name = name[:2] if name[:2] == "wo" else name
            n = SS.index(name)
            if name in BEFORE:
                j = j + 1
            return n % 2, j * (len(SS) // 2) + n // 2 + more

        def high_count(name, i):
            return (i if name in XNEXT else i + 1) * len(XSPLIT) + XSPLIT.index(name) + 1

        def wait_pos(e, sems, pos):
            e.wait_ge(sems[pos[0]], pos[1] + (FREE if sems in (xd, sd) else 0))

        def part_of(w, u):
            return w[:, u // 2, 1024 * (u % 2):1024 * (u % 2) + 1024]

        def q_halves(name, parity, half, src):
            a = 4 * (name == "qb")
            dst = q2[parity][DC * half:DC * half + DC, :, a:a + 4, :].rearrange("p b c s -> p c b s")
            return dst, src[DC * parity:DC * parity + DC, :].rearrange("p (c b s) -> p c b s", c=4, b=BT)

        @block.sync
        def _(e):
            def load_fold_first(g):
                half = g % 2
                hs = slice(g * GH, g * GH + GH)
                fs = slice(g * GH * HD, (g + 1) * GH * HD)
                if g >= 2:
                    e.wait_ge(f_a, g - 1)
                for c in range(2):
                    e.dma_start(fqr[half][:, :, c], Wqr[hs, c * QC:(c + 1) * QC, :].rearrange("h q r -> q h r")).then_inc(rope_in[half], 16)
                e.dma_start(fkr[half], Wkr[hs].rearrange("h d r -> d h r")).then_inc(rope_in[half], 16)
                if g >= 2:
                    e.wait_ge(f_b, g - 1)
                e.dma_start(fkq[half], kcq[hs].rearrange("h k q -> k h q")).then_inc(fold_in[half], 16)
                for c in range(DCH):
                    e.dma_start(fWo[half][:, c], Wo_x[c * P:(c + 1) * P, fs].rearrange("p (h k) -> p h k", h=GH)).then_inc(fold_in[half], 16)

            def load_fold_rest(g):
                half = g % 2
                hs = slice(g * GH, g * GH + GH)
                fs = slice(g * GH * HD, (g + 1) * GH * HD)
                if g >= 2:
                    e.wait_ge(f_m, g - 1)
                e.dma_start(fkv[half], kckv[hs].rearrange("h k d -> k h d")).then_inc(rest_in[half], 16)
                e.dma_start(fWq[half], Wq[fs, :].rearrange("(h k) d -> k h d", h=GH)).then_inc(rest_in[half], 16)

            def load_part(u):
                n = BUFFER[u]
                if n in BUFFER[:u]:
                    e.wait_ge(w_done, max(v for v in range(u) if BUFFER[v] == n) + 1)
                elif n >= 3:
                    e.wait_ge(f_m, GROUPS)
                w, c, o = u // 4, u % 4 // 2, 1024 * (u % 2)
                to, here = parts[n], w_in[n]
                if w < 3:
                    e.dma_start(to[:, 0], codes[w][c * P:(c + 1) * P, o:o + 1024]).then_inc(here, 16)
                    for q in range(4):
                        e.dma_start(to[32 * q:32 * q + 32, 1],
                                    scales[w][4 * c + q:4 * c + q + 1, o:o + 1024].to_broadcast([32, 1024])).then_inc(here, 16)
                else:
                    hs = slice(4 * (u % 4), 4 * (u % 4) + 4)
                    e.dma_start(to[:, 0].rearrange("p (h d) -> p h d", h=4),
                                codes[w].rearrange("(h p) d -> p h d", p=P)[:, hs]).then_inc(here, 16)
                    for q in range(4):
                        e.dma_start(to[32 * q:32 * q + 32, 1].rearrange("p (h d) -> p h d", h=4),
                                    scales[w].rearrange("(h q) d -> q h d", q=4)[q:q + 1, hs].to_broadcast([32, 4, D])
                                    ).then_inc(here, 16)

            def load_context(i):
                bs = bass.ds(i * BT, BT)
                for c in range(2):
                    e.dma_start(C[:, :, c, :], ctx_in[bs, c * P:(c + 1) * P, :].rearrange("b p d -> p b d")).then_inc(ctx_ld, 16)
                e.dma_start(C[:, :, 2, :], ctx_in[bs, 2 * P, :].unsqueeze(0).to_broadcast([P, BT, DC])).then_inc(ctx_ld, 16)

            load_fold_first(0)
            load_fold_rest(0)
            load_context(0)
            load_fold_first(1)
            load_fold_rest(1)
            load_fold_first(2)
            e.dma_start(X[:, :, :], x.rearrange("(t p) d -> p t d", p=P)).then_inc(x_in, 16)
            load_part(0)
            load_fold_rest(2)
            load_fold_first(3)
            load_part(1)
            load_fold_rest(3)
            load_part(2)
            for u in range(3, 6):
                load_part(u)
            e.wait_ge(roped, 2 * BT)
            load_context(1)
            for u in range(6, PARTS):
                load_part(u)
            e.wait_ge(w_done, PARTS)

            def load_expert(ex, n):
                e.dma_start(gu[:, n], gup[bass.ds(ex, 1)].rearrange("o (c p) f -> p (o c) f", p=P)).then_inc(ew_in[n], 16)
                e.dma_start(dn[:, n], dnp[bass.ds(ex, 1)].rearrange("o i d -> i (o d)")).then_inc(ew_in[n], 16)

            def load_rows(ex, n):
                e.dma_start(xe[:, n], XE[bass.ds(ex * CAP, CAP), :]).then_inc(xe_in[n], 16)

            for n in range(NB):
                load_expert(n, n)
            with e.Fori(2, T) as i:
                e.wait_ge(roped, i * (2 * BT))
                load_context(i)
            e.wait_ge(h3_free, T + FREE)
            for n in range(NB):
                load_rows(n, n)
            with e.Fori(1, E // NB) as j:
                for n in range(NB):
                    e.wait_ge(e_ye, j * NB + (n + 1 - NB))
                    load_expert(j * NB + n, n)
                    load_rows(j * NB + n, n)
            for n in range(4):
                e.wait_ge(ye_out[n], 16 * E // 4)
            for c in range(T // FC):
                for y in range(NY):
                    e.dma_start(ysum[:, y, FC * c:FC * c + FC, :],
                                Y[y][FC * c * P:FC * (c + 1) * P, :].rearrange("(t p) d -> p t d", p=P)).then_inc(sums_in[c], 16)
            for c in range(T // FC):
                e.wait_ge(y_ready, c + 1)
                e.dma_start(out[FC * c * P:FC * (c + 1) * P, :].rearrange("(t p) d -> p t d", p=P),
                            X[:, FC * c:FC * c + FC, :]).then_inc(stored, 16)
            e.wait_ge(stored, 16 * (T // FC))

        @block.gpsimd
        def _(e):
            links = [0]

            def link(ins):
                links[0] += 1
                ins.then_inc(pool_link, 1)
                e.wait_ge(pool_link, links[0])

            link(e.memset(ident[:, :], 0.0))
            e.affine_select(out=ident[:, :], in_=ident[:, :], compare_op=ALU.not_equal, fill=1.0, base=0,
                            pattern=[[-1, P]], channel_multiplier=1).then_inc(consts, 1)
            link(e.memset(ones16[:, :], 1.0))
            e.affine_select(out=before[:, :], in_=ones16[:, :], compare_op=ALU.is_gt, fill=0.0, base=0,
                            pattern=[[1, P]], channel_multiplier=-1).then_inc(consts, 1)
            link(e.iota(iota_i[:, :], pattern=[[1, E]], base=0, channel_multiplier=0))
            link(e.tensor_copy(iota_e[:, :], iota_i[:, :]))
            e.tensor_scalar(slot0[:, :], iota_e[:, :], float(CAP), float(-NOSLOT), ALU.mult, ALU.add).then_inc(iotas, 1)
            link(e.iota(spare_i[:, :], pattern=[[0, 1]], base=B * S, channel_multiplier=1))
            link(e.memset(h3[:, 0:D + E], 0.0))
            e.tensor_copy(h3[:, D + E:ROW], spare_i[:, :]).then_inc(iotas, 1)
            e.wait_ge(tab_in, 16 * 2)

            def rope_products(i):
                if not isinstance(i, int) or i > 0:
                    e.wait_ge(roped, i * (2 * BT))
                e.wait_ge(ctx_ld, i * 48 + 48)
                half = DC // 2
                e.tensor_tensor(Ct[:, :, :, 0:half], C[:, :, :, half:DC],
                                sinT[:, :, 0:half].unsqueeze(1).to_broadcast([P, BT, 3, half]), ALU.mult).then_inc(rope_link, 1)
                e.tensor_tensor(Ct[:, :, :, half:DC], C[:, :, :, 0:half],
                                sinT[:, :, half:DC].unsqueeze(1).to_broadcast([P, BT, 3, half]), ALU.mult).then_inc(rope_link, 1)
                e.wait_ge(rope_link, i * 3 + 2)
                e.tensor_tensor(C[:, :, :, :], C[:, :, :, :],
                                cosT[:, :, :].unsqueeze(1).to_broadcast([P, BT, 3, DC]), ALU.mult).then_inc(rope_link, 1)

            def rope_sums(i, b):
                e.wait_ge(rope_link, i * 3 + 3)
                if not isinstance(i, int) or i > 0:
                    e.wait_ge(summed, i * ROWS + (RB * (b + 1) - ROWS))
                    e.wait_ge(last_ready, i * BT + (b + 1 - BT))
                for d in range(2):
                    e.tensor_tensor(Cr[:, b, :, d, :], C[:, b], Ct[:, b], ALU.add).then_inc(roped, 1)

            def last_rows(i, b):
                e.wait_ge(expd, i * ROWS + RB * (b + 1))
                e.wait_ge(roped, i * (2 * BT) + 2 * b + 2)
                wait_pos(e, xf, xpos(f"cT{(b - 2) % BT}", i if b >= 2 else i - 1))
                e.tensor_tensor(On[:, b % 2], Cr[:, b, 2, 0, :].unsqueeze(1).to_broadcast([P, RB, DC]),
                                pr[:, RB * (b % 2):RB * (b % 2) + RB, NL - 1:NL].to_broadcast([P, RB, DC]),
                                ALU.mult).then_inc(last_ready, 1)

            def scatter(j):
                e.wait_ge(slot_ready, j + 1)
                alone(e)
                for k in range(TOPK):
                    e.indirect_dma_start(XE[:, :], bass.IndirectOffsetOnAxis(ap=slot[:, k:k + 1], axis=0), h3[:, :], None,
                                         bounds_check=E * CAP - 1, oob_is_err=False).then_inc(scat, 16)

            def scattered(j):
                e.wait_ge(scat, j * (16 * TOPK) + 16 * TOPK)
                e.sem_inc(h3_free, 1)

            rope_products(0)
            for b in range(BT):
                rope_sums(0, b)

            def part_low(u):
                e.wait_ge(w_high, u + 1)
                e.tensor_tensor(part_of(Wl, u), parts[BUFFER[u]][:, 0], part_of(Wh, u), ALU.subtract).then_inc(w_done, 1)

            for u in range(PART0[GROUPS]):
                part_low(u)

            def tile(i, m, last=False):
                if not last:
                    rope_products(i + 1)
                for b in range(BT):
                    last_rows(i, b)
                    if isinstance(i, int) and i == 0:
                        for r, u in TILE_PARTS.items():
                            if RB * b <= r < RB * (b + 1):
                                part_low(u)
                    if b == BT - 1 and m is not None:
                        scatter(m)
                    if not last:
                        rope_sums(i + 1, b)
                if m is not None:
                    scattered(m)

            tile(0, None)
            e.wait_ge(w_done, PARTS)
            e.memset(diag[:, :, :], 0.0).then_inc(zeroed, 1)
            tile(1, None)
            e.wait_ge(zero_out, 16 * (E // 8 + NY))
            with e.Fori(1, T - 2) as j:
                tile(j + 1, j - 1)
            tile(T - 1, T - 3, last=True)
            for m in (T - 2, T - 1):
                scatter(m)
                scattered(m)

            def add_out(j, first):
                for n in range(NB):
                    e.wait_ge(e_ye, j * NB + n + 1)
                    if not first or n >= NY:
                        e.wait_ge(ye_out[(n - NY) % 4], j * (16 * NB // 4) + 16 * ((n - NY) // 4 + 1))
                    alone(e)
                    e.indirect_dma_start(Y[n % NY][:, :], bass.IndirectOffsetOnAxis(ap=etok[:, n % 4:n % 4 + 1], axis=0), ye[:, n % 4], None,
                                         bounds_check=YROWS - 1, oob_is_err=False, compute_op=ALU.add).then_inc(ye_out[n % 4], 16)

            add_out(0, True)
            with e.Fori(1, E // NB) as j:
                add_out(j, False)

        @block.scalar
        def _(e):
            e.dma_start(rwr, rw).then_inc(rw_in, 16)
            e.dma_start(cosT[:, :, :], rope_cos).then_inc(tab_in, 16)
            e.dma_start(sinT[:, :, :], rope_sin).then_inc(tab_in, 16)

            def part_high(u):
                e.wait_ge(w_mul, u + 1)
                e.copy(part_of(Wh, u), parts[BUFFER[u]][:, 0]).then_inc(w_high, 1)

            for g in range(GROUPS):
                e.wait_ge(f_b, g + 1)
                for p in range(2):
                    e.copy(fkqT[:, 2 * p:2 * p + 2], bank[p][0:QC, :].rearrange("p (h c d) -> p h c d", h=2, c=2)).then_inc(f_ta, 1)
                for p in range(2):
                    e.copy(fWoT[:, 2 * p:2 * p + 2], bank[5 + p][:, :].rearrange("p (h d) -> p h d", h=2)).then_inc(f_ta, 1)
                e.wait_ge(f_n, g + 1)
                e.copy(N[:, 2 * g:2 * g + 2, :], bank[5][:, :].rearrange("p (c d) -> p c d", c=2)).then_inc(f_na, 1)
                for u in range(PART0[g], PART0[g + 1]):
                    part_high(u)
                if g == 1:
                    with nc.allow_non_contiguous_dma(reason="biases of 2048 elements"):
                        for n, bias in enumerate((bq, bk)):
                            e.dma_start(bqk[:, n, :], bias.rearrange("(h p) -> p h", p=P)).then_inc(bias_in, 16)
                        e.dma_start(bvT[:, :], bv.rearrange("(h p) -> p h", p=P)).then_inc(bias_in, 16)
                    e.dma_start(obias[:, :], bo.unsqueeze(0).to_broadcast([P, D])).then_inc(bias_in, 16)

            def blank(n):
                if n < E // 8:
                    e.dma_start(XE.rearrange("(e c) d -> c e d", c=CAP)[:, 8 * n:8 * n + 8],
                                h3[:, :].unsqueeze(1).to_broadcast([P, 8, ROW])).then_inc(zero_out, 16)
                else:
                    e.dma_start(Y[n - E // 8].rearrange("(a p) d -> p a d", p=P),
                                h3[:, 0:D].unsqueeze(1).to_broadcast([P, YROWS // P, D])).then_inc(zero_out, 16)

            def x_use(name, i):
                bk_, need = xpos(name, i)
                src = XBANK[bk_]
                e.wait_ge(xf[bk_], need)
                if name == "hT":
                    dst, s = h1T[:, :, :], src[:, 0:D].rearrange("p (c t) -> p c t", c=DCH)
                elif name in ("qa", "qb"):
                    for n in range(2):
                        dst, s = q_halves(name, n, n, src)
                        ins = e.copy(dst, s)
                    ins.then_inc(x_high, 1)
                    return
                elif name[:2] == "kt":
                    e.copy(KTh[:, int(name[2]) % 2, 0:NL], src[:, 0:NL]).then_inc(x_high, 1)
                    return
                else:
                    b = int(name[2])
                    dst, s = cT[:, :, S * b:S * b + S], src[:, 0:D].rearrange("p (c t) -> p c t", c=HP)
                e.copy(dst, s).then_inc(xd[bk_], 1)

            def exp_row(i, r):
                e.wait_ge(maxed, i * ROWS + r + 1)
                if r % RB == 0:
                    b = r // RB
                    if b >= 2:
                        e.wait_ge(on_ready, i * BT + b - 1)
                    elif not isinstance(i, int) or i > 0:
                        e.wait_ge(on_ready, i * BT + (b - 1))
                s = r % (2 * RB)
                e.activation(pr[:, s, :], bank[r % 2][:, 0:NL], ACT.Exp, bias=nmax[:, s:s + 1],
                             accum_out=rsum[:, s:s + 1]).then_inc(expd, 1)

            def copy_row(i, r):
                e.wait_ge(transposed, i * ROWS + r + 1)
                if r >= 2:
                    e.wait_ge(summed, i * ROWS + r - 1)
                e.copy(pT[:, r % 2], bank[2][:, 0:2 * P].rearrange("p (c t) -> p c t", c=2)).then_inc(pt_ready, 1)

            def s_use(name, j):
                bk_, need = spos(name, j)
                src = SBANK[bk_]
                if name == "rT":
                    e.wait_ge(sf[bk_], need)
                    e.copy(h3T, src[:, 0:D].rearrange("p (c t) -> p c t", c=DCH)).then_inc(sd[bk_], 1)
                elif name == "hT":
                    e.wait_ge(sf[bk_], need)
                    e.copy(h2h, src[:, 0:D].rearrange("p (c t) -> p c t", c=DCH)).then_inc(s_high, 1)
                elif name[0] == "v":
                    e.wait_ge(sf[bk_], need)
                    e.mul(V[:, 512 * int(name[1]):512 * int(name[1]) + 512], src[:, :], 1.0 / WS).then_inc(sd[bk_], 1)
                elif name[:2] == "pv":
                    e.wait_ge(sf[bk_], need)
                    g = int(name[2])
                    e.copy(oTh[:, 4 * g:4 * g + 4, :], src[:, :].rearrange("p (h t) -> p h t", h=4)).then_inc(s_high, 1)
                elif name == "sc":
                    e.wait_ge(shifted, j + 1)
                    e.activation(sS, sS, ACT.Exp, scale=float(HD) ** -0.5).then_inc(s_expd, 1)
                elif name == "log":
                    e.wait_ge(top_ready, j + 1)
                    e.activation(etop[:, :], top[:, :], ACT.Exp, bias=ntop[:, :], accum_out=esum[:, :]).then_inc(e_ready, 1)
                    e.activation(h3[:, D:D + E], lg[:, :], ACT.Exp, bias=ntop[:, :]).then_inc(e_ready, 1)

            def spread(j, q):
                e.wait_ge(sT_ready, j + 1)
                qs = slice(32 * q, 32 * q + 32)
                e.copy(diag[qs, :, qs], sT[qs]).then_inc(diag_ready, 1)

            def tile(i, j, m, last=False):

                def uses(names):
                    for name in names:
                        t = m if name in BEFORE else j
                        if t is not None:
                            s_use(name, t)

                for r in range(STEPS):
                    if i is not None:
                        if 2 <= r <= ROWS + 1:
                            copy_row(i, r - 2)
                        if r < ROWS:
                            exp_row(i, r)
                        for name in X_AT.get(r, ()):
                            if name in XNEXT and not last:
                                x_use(name, i + 1)
                            elif name not in XNEXT and name != "out":
                                x_use(name, i)
                        if isinstance(i, int) and i == 0 and r in TILE_PARTS:
                            part_high(TILE_PARTS[r])
                        if isinstance(i, int) and i == 1:
                            if r == 0:
                                e.wait_ge(iotas, 2)
                            if r < E // 8 + NY:
                                blank(r)
                    if j is not None and r in (13, 14):
                        for q in (0, 1) if r == 13 else (2, 3):
                            spread(j, q)
                    uses(BEHIND.get(r, ()))

            e.sem_inc(x_high, XSPLIT.index("qa"))
            for name in XNEXT:
                x_use(name, 0)

            tile(0, None, None)
            e.wait_ge(zeroed, 2)
            tile(1, 0, None)
            with e.Fori(1, T - 2) as j:
                tile(j + 1, j, j - 1)
            tile(T - 1, T - 2, T - 3, last=True)
            tile(None, T - 1, T - 2)
            tile(None, None, T - 1)

            def expert_copy(ex, n):
                e.wait_ge(e_t, ex + 1)
                e.copy(xeT[:, n % 2], bank[n % 2][:, 0:D].rearrange("p (c t) -> p c t", c=DCH)).then_inc(e_tc, 1)

            def experts(j, last):
                for n in range(NB):
                    if not (last and n == NB - 1):
                        expert_copy(j * NB + n + 1, n + 1)
                    e.wait_ge(e_gu, j * NB + n + 1)
                    e.activation(sg[:, n % 2], bank[2 + n % 2][0:I, 0:P], ACT.Silu).then_inc(e_silu, 1)

            expert_copy(0, 0)
            with e.Fori(0, E // NB - 1) as j:
                experts(j, False)
            experts(E // NB - 1, True)

        @block.vector
        def _(e):
            e.memset(count[:, :], 0.0).then_inc(zeroed, 1)
            e.wait_ge(rw_t, 1)
            e.tensor_copy(rwT[:, :, :], bank[7][:, 0:DCH * E].rearrange("p (c n) -> p c n", c=DCH)).then_inc(rwT_ready, 1)

            done = {}
            LINKS = {"x": (x_link, XLINKS), "s": (s_link, SLINKS), "r": (r_link, RLINKS), "n": (n_link, 0)}

            def link(ins, which, base):
                done[which] = done.get(which, 0) + 1
                s, n = LINKS[which]
                ins.then_inc(s, 1)
                e.wait_ge(s, base * n + done[which])

            def root_guess(var, y, t, which, base):
                link(e.tensor_scalar(var, var, 1e-5, None, ALU.add), which, base)
                link(e.tensor_scalar(t.bitcast(u32), var.bitcast(u32), 1, None, ALU.logical_shift_right), which, base)
                link(e.tensor_scalar(y.bitcast(u32), t.bitcast(u32), -1.0, float(0x5f3759df), ALU.mult, ALU.add), which, base)

            def root_steps(var, y, t, which, base, steps):
                c = 1.0
                for n in range(NEWTON):
                    if n in steps:
                        link(e.tensor_scalar(t, y, y, var, ALU.mult, ALU.mult), which, base)
                        if n < NEWTON - 1:
                            link(e.scalar_tensor_tensor(y, t, -3.0 * c * c, y, ALU.add, ALU.mult), which, base)
                        else:
                            link(e.tensor_scalar(t, t, -0.5 / c ** 3, 1.5 / c, ALU.mult, ALU.add), which, base)
                            link(e.tensor_tensor(y, t, y, ALU.mult), which, base)
                    c = -2.0 * c ** 3

            def all_stats(half):
                if half == 0:
                    e.wait_ge(x_in, 16)
                    for t in range(T):
                        e.bn_stats(st0[:, t, :], X[:, t, :]).then_inc(n_link, 1)
                    e.wait_ge(n_link, T)
                    for t in range(T):
                        e.bn_aggr(mv0[:, t, :], st0[:, t, :]).then_inc(n_link, 1)
                else:
                    e.wait_ge(n_link, 2 * T)
                    done["n"] = 2 * T
                    var, y, t = mv0[:, :, 1], rs0[:, 0, :], rs0[:, 1, :]
                    root_guess(var, y, t, "n", 0)
                    for _ in range(NEWTON):
                        link(e.tensor_tensor(t, y, y, ALU.mult), "n", 0)
                        link(e.scalar_tensor_tensor(t, t, -0.5, var, ALU.mult, ALU.mult), "n", 0)
                        link(e.scalar_tensor_tensor(y, t, 1.5, y, ALU.add, ALU.mult), "n", 0)

            def part_mul(u):
                e.wait_ge(w_in[BUFFER[u]], 80 * BUFFER[:u + 1].count(BUFFER[u]))
                e.scalar_tensor_tensor(parts[BUFFER[u]][:, 0], parts[BUFFER[u]][:, 0], WS, parts[BUFFER[u]][:, 1], ALU.mult, ALU.mult).then_inc(w_mul, 1)

            def rope_copies(g):
                e.wait_ge(f_a, g + 1)
                for p in range(2):
                    e.tensor_copy(fqrT[:, 2 * p:2 * p + 2], bank[2 + p][0:R, 0:4 * QC].rearrange("p (h c d) -> p h c d", h=2, c=2)).then_inc(f_td, 1)
                e.tensor_copy(fkrT, bank[4][0:R, 0:GH * DC].rearrange("p (h d) -> p h d", h=GH)).then_inc(f_td, 1)

            rope_copies(0)
            for g in range(GROUPS):
                left = list(range(PART0[g], PART0[g + 1]))
                e.wait_ge(f_g, g + 1)
                e.tensor_copy(fG, bank[7][0:QC, :].rearrange("p (h c d) -> p h c d", h=GH, c=2)).then_inc(f_gd, 1)
                if g < GROUPS - 1:
                    rope_copies(g + 1)
                if len(left) > 2:
                    part_mul(left.pop(0))
                e.wait_ge(f_q, g + 1)
                e.tensor_copy(fQ, bank[0][:, 0:GH * DC].rearrange("p (h d) -> p h d", h=GH)).then_inc(f_qd, 1)
                if len(left) > 1:
                    part_mul(left.pop(0))
                e.wait_ge(f_m, g + 1)
                e.tensor_copy(M[:, :, GH * DC * g:GH * DC * (g + 1)], bank[7][:, :].rearrange("p (c n) -> p c n", c=DCH)).then_inc(f_md, 1)
                for u in left:
                    part_mul(u)
                if g in (1, 2):
                    all_stats(g - 1)

            def norm_stats(t, which, base, st, mv):
                src = X[:, bass.ds(t, 1), :].rearrange("p o d -> p (o d)")
                alone(e)
                link(e.bn_stats(st[:, :], src), which, base)
                alone(e)
                link(e.bn_aggr(mv[:, :], st[:, :]), which, base)

            def norm_root(which, base, mv, rs):
                root_guess(mv[:, 1:2], rs[:, 0:1], rs[:, 1:2], which, base)
                root_steps(mv[:, 1:2], rs[:, 0:1], rs[:, 1:2], which, base, (0,))

            def norm_apply(dst, t, which, base, mv, rs, ready):
                src = X[:, bass.ds(t, 1), :].rearrange("p o d -> p (o d)")
                root_steps(mv[:, 1:2], rs[:, 0:1], rs[:, 1:2], which, base, range(1, NEWTON))
                e.tensor_scalar(dst[:, 0:D], src, mv[:, 0:1], rs[:, 0:1], ALU.subtract, ALU.mult).then_inc(ready, 1)

            def x_low(name, i):
                bk_, need = xpos(name, i)
                src = XBANK[bk_]
                e.wait_ge(x_high, high_count(name, i))
                if name[:2] == "kt":
                    b = int(name[2]) % 2
                    ins = e.tensor_tensor(KTl[:, b, 0:NL], src[:, 0:NL], KTh[:, b, 0:NL], ALU.subtract)
                else:
                    for n in range(2):
                        high, s = q_halves(name, n, n, src)
                        ins = e.tensor_tensor(q_halves(name, n, 1 - n, src)[0], s, high, ALU.subtract)
                ins.then_inc(xd[bk_], 1)

            def max_row(i, r):
                e.wait_ge(scored, i * ROWS + r + 1)
                s = r % (2 * RB)
                e.tensor_reduce(nmax[:, s:s + 1], bank[r % 2][:, 0:NL], AX.X, ALU.max, negate=True).then_inc(maxed, 1)

            def normalise(i, b):
                e.wait_ge(summed, i * ROWS + RB * (b + 1))
                e.wait_ge(last_ready, i * BT + b + 1)
                link(e.tensor_tensor(On[:, b % 2], bank[3][:, 0:RB * DC].rearrange("p (r d) -> p r d", r=RB),
                                     On[:, b % 2], ALU.add), "x", i)
                s = RB * (b % 2)
                link(e.reciprocal(rinv[:, s:s + RB], rsum[:, s:s + RB]), "x", i)
                e.tensor_tensor(On[:, b % 2], On[:, b % 2], rinv[:, s:s + RB].unsqueeze(2).to_broadcast([P, RB, DC]),
                                ALU.mult).then_inc(on_ready, 1)

            def x_out(i):
                bk_, need = xpos("out", i)
                e.wait_ge(xf[bk_], need)
                src = X[:, bass.ds(i, 1), :].rearrange("p o d -> p (o d)")
                e.tensor_tensor(src, src, XBANK[bk_][:, 0:D], ALU.add).then_inc(xd[bk_], 1)
                e.wait_ge(xd[bk_], need + FREE)
                norm_stats(i, "s", i, st1, mv1)

            def softmax_sum(j):
                e.wait_ge(s_expd, j + 1)
                link(e.tensor_reduce(ssum[:, :], sS, AX.X, ALU.add), "s", j)
                link(e.reciprocal(sinv[:, :], ssum[:, :]), "s", j)

            def softmax_end(j):
                link(e.tensor_tensor(sS, sS, sinv[:, :].unsqueeze(2).to_broadcast([P, H, S]), ALU.mult), "s", j)
                e.transpose(sT, sS).then_inc(sT_ready, 1)

            def s_use(name, j):
                bk_, need = spos(name, j)
                src = SBANK[bk_]
                if name[0] in "qk":
                    e.wait_ge(sf[bk_], need)
                    g, w = int(name[1]), int(name[0] == "k")
                    e.scalar_tensor_tensor((qS, kS)[w][:, 4 * g:4 * g + 4, :], src[:, :].rearrange("p (h t) -> p h t", h=4), 1.0 / WS,
                                           bqk[:, w, 4 * g:4 * g + 4].unsqueeze(2).to_broadcast([P, 4, P]), ALU.mult, ALU.add).then_inc(sd[bk_], 1)
                elif name == "sc":
                    e.wait_ge(sf[bk_], need)
                    s3 = src[:, :].rearrange("p (h t) -> p h t", h=H)
                    link(e.tensor_reduce(smax[:, :], s3, AX.X, ALU.max), "s", j)
                    e.tensor_tensor(sS, s3, smax[:, :].unsqueeze(2).to_broadcast([P, H, S]), ALU.subtract).then_inc(sd[bk_], 1)
                    e.wait_ge(sd[bk_], need + FREE)
                    e.nop().then_inc(shifted, 1)
                elif name == "hT":
                    e.wait_ge(s_high, j * 5 + 1)
                    e.tensor_tensor(h2l, src[:, 0:D].rearrange("p (c t) -> p c t", c=DCH), h2h, ALU.subtract).then_inc(sd[bk_], 1)
                elif name[:2] == "pv":
                    g = int(name[2])
                    e.wait_ge(s_high, j * 5 + g + 2)
                    e.tensor_tensor(oTl[:, 4 * g:4 * g + 4, :], src[:, :].rearrange("p (h t) -> p h t", h=4),
                                    oTh[:, 4 * g:4 * g + 4, :], ALU.subtract).then_inc(sd[bk_], 1)
                elif name == "log":
                    e.wait_ge(sf[bk_], need)
                    e.tensor_copy(lg[:, :], src[:, 0:E]).then_inc(sd[bk_], 1)
                    e.wait_ge(sd[bk_], need + FREE)
                    alone(e)
                    link(e.max(top[:, :], lg[:, :]), "r", j)
                    e.tensor_scalar(ntop[:, :], top[:, 0:1], -1.0, None, ALU.mult).then_inc(top_ready, 1)
                    link(e.max_index(topi[:, :], top[:, :], lg[:, :]), "r", j)
                elif name == "pos":
                    e.wait_ge(sf[bk_], need)
                    link(e.tensor_tensor(sv[:, :], src[:, 0:E], slot0[:, :], ALU.add), "r", j)
                    e.scalar_tensor_tensor(sv2[:, :], src[:, 0:E], float(CAP), sv[:, :], ALU.is_lt, ALU.mult).then_inc(sd[bk_], 1)
                    e.wait_ge(sd[bk_], need + FREE)
                    link(e.tensor_tensor(count[:, :], count[:, :], mask[:, :], ALU.add), "r", j)

            def chosen(j):
                link(e.tensor_copy(topf[:, :], topi[:, :]), "r", j)
                link(e.tensor_tensor(oh, iota_e[:, :].unsqueeze(1).to_broadcast([P, TOPK, E]),
                                     topf[:, :].unsqueeze(2).to_broadcast([P, TOPK, E]), ALU.is_equal), "r", j)
                with nc.allow_low_precision(reason="zeros and ones"):
                    e.tensor_reduce(mask[:, :], oh.rearrange("p k e -> p e k"), AX.X, ALU.add).then_inc(mask_ready, 1)
                e.wait_ge(mask_ready, j + 1)

            def weigh(j):
                e.wait_ge(e_ready, j * 2 + 2)
                link(e.reciprocal(einv[:, :], esum[:, :]), "r", j)
                link(e.tensor_scalar(h3[:, D:D + E], h3[:, D:D + E], einv[:, :], None, ALU.mult), "r", j)
                link(e.tensor_scalar(h3[:, D + E:ROW], h3[:, D + E:ROW], float(P), None, ALU.add), "r", j)

            def place(j):
                link(e.tensor_tensor(oh2, oh, sv2[:, :].unsqueeze(1).to_broadcast([P, TOPK, E]), ALU.mult), "r", j)
                link(e.tensor_reduce(slotf[:, :], oh2, AX.X, ALU.add), "r", j)
                e.tensor_scalar(slot[:, :], slotf[:, :], float(NOSLOT), None, ALU.add).then_inc(slot_ready, 1)

            def self_out(j):
                bk_, need = spos("wo", j)
                src = SBANK[bk_]
                e.wait_ge(sf[bk_], need)
                src2 = X[:, bass.ds(j, 1), :].rearrange("p o d -> p (o d)")
                e.scalar_tensor_tensor(src2, src[:, 0:D], 1.0 / WS, src2, ALU.mult, ALU.add).then_inc(sd[bk_], 1)
                e.wait_ge(sd[bk_], need + FREE)
                link(e.tensor_tensor(src2, src2, obias[:, :], ALU.add), "r", j)
                norm_stats(j, "r", j, st2, mv2)

            def self_out_norm(j):
                e.wait_ge(h3_free, j + FREE)
                norm_apply(h3, j, "r", j, mv2, rs2, h3_ready)

            def next_h1(i):
                e.tensor_scalar(h1[:, :], X[:, bass.ds(i, 1), :].rearrange("p o d -> p (o d)"),
                                mv0[:, bass.ds(i, 1), 0:1].rearrange("p o d -> p (o d)"), rs0[:, 0, bass.ds(i, 1)],
                                ALU.subtract, ALU.mult).then_inc(h1_ready, 1)

            def tile(i, j, m, last=False):
                done.clear()

                def uses(names):
                    for name in names:
                        t = m if name in BEFORE else j
                        if t is not None and name[:2] != "wo":
                            s_use(name, t)

                for r in range(STEPS):
                    if i is not None:
                        if r < ROWS:
                            max_row(i, r)
                        if r % RB == 2 and r > RB:
                            normalise(i, r // RB - 1)
                        for name in X_AT.get(r, ()):
                            if name in XSPLIT and name not in XNEXT:
                                x_low(name, i)
                            elif name in XSPLIT and not last:
                                x_low(name, i + 1)
                        if r == 8 and not last:
                            next_h1(i + 1)
                        if isinstance(i, int) and i == 0 and r in TILE_PARTS:
                            part_mul(TILE_PARTS[r])
                    if j is not None and r == 0:
                        x_out(j)
                        norm_root("s", j, mv1, rs1)
                    if j is not None and r == 1:
                        norm_apply(h2, j, "s", j, mv1, rs1, h2_ready)
                    if m is not None and r == 4:
                        self_out(m)
                    if m is not None and r == 5:
                        norm_root("r", m, mv2, rs2)
                    if m is not None and r == 6:
                        self_out_norm(m)
                    uses(BEHIND.get(r, ()))
                    if j is not None and r == 11:
                        softmax_sum(j)
                    if j is not None and r == 12:
                        softmax_end(j)
                    if m is not None and r == 9:
                        chosen(m)
                    if m is not None and r == 14:
                        weigh(m)
                    if m is not None and r == 15:
                        place(m)
                assert i is None or done["x"] == XLINKS, done
                assert j is None or done["s"] == SLINKS, done
                assert m is None or done["r"] == RLINKS, done

            e.sem_inc(h3_free, FREE)
            e.wait_ge(iotas, 2)
            e.wait_ge(bias_in, 64)
            e.tensor_copy(bvh[:, :], bvT[:, :]).then_inc(bv_split, 1)
            e.wait_ge(bv_split, 1)
            e.tensor_tensor(bvl[:, :], bvT[:, :], bvh[:, :], ALU.subtract).then_inc(bv_split, 1)
            next_h1(0)
            for name in ("qa", "qb", "kt0"):
                x_low(name, 0)
            tile(0, None, None)
            e.wait_ge(ob_mm, 1)
            e.scalar_tensor_tensor(obias[:, :], bank[7][:, 0:D], 1.0 / WS, obias[:, :], ALU.mult, ALU.add).then_inc(ob_ready, 1)
            e.wait_ge(ob_ready, 1)
            tile(1, 0, None)
            e.wait_ge(zero_out, 16 * (E // 8 + NY))
            e.tensor_scalar(h3[:, D + E:ROW], h3[:, D + E:ROW], float(-(B * S + P)), None, ALU.add).then_inc(zeroed, 1)
            e.wait_ge(zeroed, 3)
            with e.Fori(1, T - 2) as j:
                tile(j + 1, j, j - 1)
            tile(T - 1, T - 2, T - 3, last=True)
            tile(None, T - 1, T - 2)
            tile(None, None, T - 1)

            def experts(j, first):
                for n in range(NB):
                    e.wait_ge(e_silu, j * NB + n + 1)
                    e.tensor_tensor(hh[:, n % 2], sg[:, n % 2], bank[2 + n % 2][0:I, P:2 * P], ALU.mult).then_inc(e_h, 1)
                    if not (first and n == 0):
                        m = (n - 1) % NB
                        e.wait_ge(e_dn, j * NB + n)
                        if not first or m >= 4:
                            e.wait_ge(ye_out[m % 4], j * 32 + (16 * (m // 4) if n else -16))
                        weighted(m, j * NB + n - 1)

            def weighted(m, ex):
                e.tensor_copy(etok[:, m % 4:m % 4 + 1], xe[:, m, D + E:ROW])
                e.tensor_scalar(ye[:, m % 4], bank[4 + m % 2][:, 0:D], xe[:, m, bass.ds(ex + D, 1)], None, ALU.mult).then_inc(e_ye, 1)

            experts(0, True)
            with e.Fori(1, E // NB) as j:
                experts(j, False)
            e.wait_ge(e_dn, E)
            e.wait_ge(ye_out[3], 16 * (E // 4 - 1))
            weighted(NB - 1, E - 1)
            for c in range(T // FC):
                e.wait_ge(sums_in[c], 16 * NY)
                for y in range(NY):
                    ins = e.tensor_tensor(X[:, FC * c:FC * c + FC, :], X[:, FC * c:FC * c + FC, :], ysum[:, y, FC * c:FC * c + FC, :], ALU.add)
                    if y < NY - 1:
                        ins.then_inc(y_link, 1)
                        e.wait_ge(y_link, c * (NY - 1) + y + 1)
                ins.then_inc(y_ready, 1)

        @block.tensor
        def _(e):
            for s in (xd[0], xd[1], sd[0], sd[1]):
                e.sem_inc(s, FREE)
            e.wait_ge(consts, 2)
            e.wait_ge(rw_in, 16)
            for c in range(DCH):
                ins = e.transpose(bank[7][:, c * E:(c + 1) * E], rwr[:, c * P:(c + 1) * P], ident[0:E, 0:E])
            ins.then_inc(rw_t, 1)
            e.wait_ge(rwT_ready, 1)

            def rope_transposes(g):
                e.wait_ge(rope_in[g % 2], 48 * (g // 2) + 48)
                if g:
                    e.wait_ge(f_td, 3 * g)
                for h in range(GH):
                    for c in range(2):
                        e.transpose(bank[2 + h // 2][0:R, (2 * (h % 2) + c) * QC:(2 * (h % 2) + c + 1) * QC], fqr[g % 2][:, h, c, :], ident[0:QC, 0:QC])
                    ins = e.transpose(bank[4][0:R, h * DC:(h + 1) * DC], fkr[g % 2][:, h, :], ident[0:DC, 0:DC])
                ins.then_inc(f_a, 1)

            def transposes(g):
                e.wait_ge(fold_in[g % 2], 48 * (g // 2) + 48)
                if g:
                    e.wait_ge(f_qd, g)
                    e.wait_ge(f_na, g)
                for h in range(GH):
                    p, o = h // 2, 256 * (h % 2)
                    for c in range(2):
                        e.transpose(bank[p][0:QC, o + c * P:o + (c + 1) * P], fkq[g % 2][:, h, c * QC:(c + 1) * QC], ident[:, :])
                        ins = e.transpose(bank[5 + p][:, o + c * P:o + (c + 1) * P], fWo[g % 2][:, c, h, :], ident[:, :])
                ins.then_inc(f_b, 1)

            rope_transposes(0)
            transposes(0)
            for g in range(GROUPS):
                e.wait_ge(f_td, g * 3 + 3)
                if g:
                    e.wait_ge(f_md, g)
                for h in range(GH):
                    for c in range(2):
                        ins = e.matmul(bank[7][0:QC, (2 * h + c) * DC:(2 * h + c + 1) * DC], fqrT[:, h, c, :], fkrT[:, h, :], start=True, stop=True)
                ins.then_inc(f_g, 1)
                if g < GROUPS - 1:
                    rope_transposes(g + 1)
                e.wait_ge(f_gd, g + 1)
                e.wait_ge(f_ta, g * 4 + 4)
                for h in range(GH):
                    for c in range(2):
                        ins = e.matmul(bank[0][:, h * DC:(h + 1) * DC], fkqT[:, h, c, :], fG[:, h, c, :], start=c == 0, stop=c == 1)
                ins.then_inc(f_q, 1)
                e.wait_ge(rest_in[g % 2], 32 * (g // 2) + 32)
                for h in range(GH):
                    q = DC * (h % 2)
                    ins = e.matmul(bank[5][q:q + DC, (h // 2) * D:(h // 2 + 1) * D], fkv[g % 2][:, h, :], fWoT[:, h, :], start=True, stop=True)
                ins.then_inc(f_n, 1)
                e.wait_ge(f_qd, g + 1)
                for h in range(GH):
                    for c in range(DCH):
                        ins = e.matmul(bank[7][:, c * 256 + h * DC:c * 256 + (h + 1) * DC], fWq[g % 2][:, h, c * P:(c + 1) * P], fQ[:, h, :], start=True, stop=True)
                ins.then_inc(f_m, 1)
                if g < GROUPS - 1:
                    transposes(g + 1)
            e.wait_ge(f_md, GROUPS)
            e.wait_ge(f_na, GROUPS)

            def split(dst, terms, first=True, last=True):
                for n, (ah, al, bh, bl) in enumerate(terms):
                    e.matmul(dst, ah, bh, start=first and n == 0, stop=False)
                    e.matmul(dst, ah, bl, start=False, stop=False)
                    ins = e.matmul(dst, al, bh, start=False, stop=last and n == len(terms) - 1)
                return ins

            def x_use(name, i):
                bk_, need = xpos(name, i)
                dst = XBANK[bk_]
                e.wait_ge(xd[bk_], need - 1 + FREE)
                if name == "hT":
                    e.wait_ge(h1_ready, i + 1)
                    for c in range(DCH):
                        ins = e.transpose(dst[:, c * P:(c + 1) * P], h1[:, c * P:(c + 1) * P], ident[:, :])
                elif name in ("qa", "qb"):
                    wait_pos(e, xd, xpos("hT", i))
                    for n in range(4):
                        c = n + 4 * (name == "qb")
                        for k in range(DCH):
                            ins = e.matmul(dst[:, n * P:(n + 1) * P], M[:, k, c * P:(c + 1) * P], h1T[:, k, :], start=k == 0, stop=k == DCH - 1)
                elif name[:2] == "kt":
                    b = int(name[2])
                    e.wait_ge(roped, i * (2 * BT) + 2 * b + 2)
                    for c in range(2):
                        e.transpose(dst[:, c * P:(c + 1) * P], Cr[:, b, c].rearrange("p t d -> p (t d)"), ident[:, :])
                    ins = e.transpose(dst[:, 2 * P:NL], Cr[0:1, b, 2].rearrange("p t d -> p (t d)"), ident[0:1, 0:1])
                elif name[:2] == "cT":
                    b = int(name[2])
                    e.wait_ge(on_ready, i * BT + b + 1)
                    for g in range(2):
                        ins = e.transpose(dst[:, g * P:(g + 1) * P], On[:, b % 2, 2 * g:2 * g + 2, :].rearrange("p r d -> p (r d)"), ident[:, :])
                else:
                    wait_pos(e, xd, xpos("cT3", i))
                    for c in range(HP):
                        ins = e.matmul(dst[:, 0:D], cT[:, c, :], N[:, c, :], start=c == 0, stop=c == HP - 1)
                ins.then_inc(xf[bk_], 1)

            def score_row(i, r):
                b, g, q = r // RB, r % RB // 2, DC * (r % 2)
                if r % RB == 0:
                    wait_pos(e, xd, xpos(f"kt{b}", i))
                if r == 0:
                    wait_pos(e, xd, xpos("qb", i))
                e.wait_ge(expd, i * ROWS + r - 1 if r else i * ROWS)
                Q = q2[r % 2][:, b, 4 * g:4 * g + 4, :].rearrange("p c s -> p (c s)")
                e.matmul(bank[r % 2][:, 0:NL], Q, KTh[:, b % 2, 0:NL], start=True, stop=False)
                e.matmul(bank[r % 2][:, 0:NL], Q[q:q + DC], KTl[q:q + DC, b % 2, 0:NL], start=False, stop=True).then_inc(scored, 1)

            def transpose_row(i, r):
                e.wait_ge(expd, i * ROWS + r + 1)
                e.wait_ge(pt_ready, i * ROWS + r)
                for c in range(2):
                    ins = e.transpose(bank[2][:, c * P:(c + 1) * P], pr[:, r % (2 * RB), c * P:(c + 1) * P], ident[:, :])
                ins.then_inc(transposed, 1)

            def sum_row(i, r):
                b = r // RB
                e.wait_ge(pt_ready, i * ROWS + r + 1)
                if r % RB == 0:
                    e.wait_ge(on_ready, i * BT + b)
                o = DC * (r % RB)
                for c in range(2):
                    ins = e.matmul(bank[3][:, o:o + DC], pT[:, r % 2, c, :], Cr[:, b, c, 0, :], start=c == 0, stop=c == 1)
                ins.then_inc(summed, 1)

            def s_use(name, j):
                bk_, need = spos(name, j)
                dst = SBANK[bk_]
                if name not in ("wo1", "wo2", "wo3"):
                    e.wait_ge(sd[bk_], need - 1 + FREE)
                if name in ("hT", "rT"):
                    e.wait_ge(h2_ready if name == "hT" else h3_ready, j + 1)
                    src = h2 if name == "hT" else h3
                    for c in range(DCH):
                        ins = e.transpose(dst[:, c * P:(c + 1) * P], src[:, c * P:(c + 1) * P], ident[:, :])
                elif name[0] in "qk":
                    wait_pos(e, sd, spos("hT", j))
                    w = 2 * (name[0] == "k")
                    for n in range(4):
                        h = 4 * int(name[1]) + n
                        ins = split(dst[:, n * P:(n + 1) * P], [(Wh[:, w + k, h * HD:(h + 1) * HD], Wl[:, w + k, h * HD:(h + 1) * HD],
                                                                 h2h[:, k, :], h2l[:, k, :]) for k in range(DCH)])
                elif name == "sc":
                    wait_pos(e, sd, spos("k3", j))
                    for h in range(H):
                        for q in range(4):
                            qs = slice(32 * q, 32 * q + 32)
                            ins = e.matmul(dst[qs, h * S:(h + 1) * S], qS[:, h, qs], kS[:, h, qs], start=True, stop=True, tile_position=(0, 32 * q))
                elif name[0] == "v":
                    o = 512 * int(name[1])
                    ins = split(dst[:, :], [(h2h[:, k, :], h2l[:, k, :], Wh[:, 4 + k, o:o + 512], Wl[:, 4 + k, o:o + 512])
                                            for k in range(DCH)])
                elif name[:2] == "pv":
                    e.wait_ge(diag_ready, j * 4 + 4)
                    wait_pos(e, sd, spos("v3", j))
                    for n in range(4):
                        h = 4 * int(name[2]) + n
                        ins = e.matmul(dst[:, n * P:(n + 1) * P], V[:, h * HD:(h + 1) * HD], diag[:, h, :], start=True, stop=True)
                elif name[:2] == "wo":
                    if name == "wo0":
                        wait_pos(e, sd, spos("pv3", j))
                    a = 4 * int(name[2])
                    ins = split(dst[:, 0:D], [(oTh[:, h, :], oTl[:, h, :], Wh[:, 6 + h // 8, (h % 8) * D:(h % 8 + 1) * D],
                                               Wl[:, 6 + h // 8, (h % 8) * D:(h % 8 + 1) * D]) for h in range(a, a + 4)],
                                first=a == 0, last=a == 12)
                elif name == "log":
                    wait_pos(e, sd, spos("rT", j))
                    for k in range(DCH):
                        ins = e.matmul(dst[:, 0:E], h3T[:, k, :], rwT[:, k, :], start=k == 0, stop=k == DCH - 1)
                elif name == "pos":
                    e.wait_ge(mask_ready, j + 1)
                    e.matmul(dst[:, 0:E], before[:, :], mask[:, :], start=True, stop=False)
                    ins = e.matmul(dst[:, 0:E], ones16[:, :], count[:, :], start=False, stop=True)
                if name not in ("wo0", "wo1", "wo2"):
                    ins.then_inc(sf[bk_], 1)

            def skip(name, j):
                bk_, need = spos(name, j)
                e.wait_ge(sd[bk_], need - 1 + FREE)
                e.sem_inc(sf[bk_], 1)
                e.sem_inc(sd[bk_], 1)

            def x_skip(name, i):
                bk_, need = xpos(name, i)
                e.wait_ge(xd[bk_], need - 1 + FREE)
                e.sem_inc(xf[bk_], 1)
                e.sem_inc(xd[bk_], 1)

            def tile(i, j, m, last=False):

                def uses(names):
                    for name in names:
                        t = m if name[:2] == "wo" or name in BEFORE else j
                        if t is not None:
                            s_use(name, t)
                        elif name not in ("wo0", "wo1", "wo2") and (j is not None or m is not None):
                            skip(name, m + 1 if j is None else j - 1)

                for r in range(STEPS):
                    if i is not None:
                        if r < ROWS:
                            score_row(i, r)
                        if 2 <= r <= ROWS + 1:
                            transpose_row(i, r - 2)
                        if 3 <= r <= ROWS + 2:
                            sum_row(i, r - 3)
                        for name in X_AT.get(r, ()):
                            if name not in XNEXT:
                                x_use(name, i)
                            elif not last:
                                x_use(name, i + 1)
                            else:
                                x_skip(name, i + 1)
                    uses(BEHIND.get(r, ()))

            for name in XS:
                (x_use(name, 0) if name in XNEXT else x_skip(name, -1))
            tile(0, None, None)
            e.wait_ge(w_done, PARTS)
            e.wait_ge(bv_split, 2)
            ins = split(bank[7][:, 0:D], [(bvh[:, h:h + 1].to_broadcast([P, P]), bvl[:, h:h + 1].to_broadcast([P, P]),
                                           Wh[:, 6 + h // 8, (h % 8) * D:(h % 8 + 1) * D],
                                           Wl[:, 6 + h // 8, (h % 8) * D:(h % 8 + 1) * D]) for h in range(H)])
            ins.then_inc(ob_mm, 1)
            e.wait_ge(ob_ready, 1)
            tile(1, 0, None)
            with e.Fori(1, T - 2) as j:
                tile(j + 1, j, j - 1)
            tile(T - 1, T - 2, T - 3, last=True)
            tile(None, T - 1, T - 2)
            tile(None, None, T - 1)

            def expert_t(j, n):
                e.wait_ge(xe_in[n], j * 16 + 16)
                for c in range(DCH):
                    ins = e.transpose(bank[n % 2][:, c * P:(c + 1) * P], xe[:, n, c * P:(c + 1) * P], ident[:, :])
                ins.then_inc(e_t, 1)

            def expert_gate_up(j, n):
                e.wait_ge(ew_in[n], j * 32 + 32)
                e.wait_ge(e_tc, j * NB + n + 1)
                for half in range(2):
                    for c in range(DCH):
                        ins = e.matmul(bank[2 + n % 2][0:I, half * P:(half + 1) * P], gu[:, n, c, half * I:(half + 1) * I], xeT[:, n % 2, c, :],
                                       start=c == 0, stop=c == DCH - 1)
                ins.then_inc(e_gu, 1)

            def expert_down(j, n, before_that):
                e.wait_ge(e_h, before_that + 1)
                if not isinstance(before_that, int) or before_that >= 2:
                    e.wait_ge(e_ye, before_that - 1)
                e.matmul(bank[4 + n % 2][:, 0:D], hh[:, n % 2], dn[:, n], start=True, stop=True).then_inc(e_dn, 1)

            def experts(j, first, last):
                for n in range(NB):
                    if n < NB - 1:
                        expert_t(j, n + 1)
                    elif not last:
                        expert_t(j + 1, 0)
                    expert_gate_up(j, n)
                    if not (first and n == 0):
                        expert_down(j, (n - 1) % NB, j * NB + n - 1)

            expert_t(0, 0)
            experts(0, True, False)
            with e.Fori(1, E // NB - 1) as j:
                experts(j, False, False)
            experts(E // NB - 1, False, True)
            expert_down(E // NB - 1, NB - 1, E - 1)


_NAMES = ["x", "ctx_512", "L0_xattn_Wq", "L0_xattn_w_kc_q", "L0_xattn_w_kc_kv", "L0_xattn_W_qr", "L0_xattn_W_kr",
          "L0_xattn_Wo", "L0_attn_wq_codes", "L0_attn_wk_codes", "L0_attn_wv_codes", "L0_attn_wo_codes",
          "L0_attn_wq_scales", "L0_attn_wk_scales", "L0_attn_wv_scales", "L0_attn_wo_scales", "L0_attn_bq",
          "L0_attn_bk", "L0_attn_bv", "L0_attn_bo", "L0_ffn_router_weight", "L0_ffn_gate_up_proj", "L0_ffn_down_proj"]


def rope_tables():
    import numpy as np
    inv = (np.float32(1.0) / np.float32(10000.0) ** (np.arange(0, DC, 2, dtype=np.float32) / np.float32(DC))).astype(np.float32)
    f = np.arange(NL, dtype=np.float32)[:, None] * inv[None, :]
    sin, cos = (np.repeat(t.astype(np.float32), 2, axis=-1) for t in (np.sin(f), np.cos(f)))
    sin = np.concatenate([-sin[:, :DC // 2], sin[:, DC // 2:]], axis=-1)
    lay = lambda t: np.ascontiguousarray(np.stack([t[:P], t[P:2 * P], np.repeat(t[2 * P:], P, axis=0)], axis=1))
    return lay(cos), lay(sin)


def kernel(**inputs):
    import numpy as np
    import concourse.bacc as bacc
    from concourse.bass_utils import run_bass_kernel_spmd

    nc = bacc.Bacc("TRN2", target_bir_lowering=False, num_devices=1)
    arrays, aps = {}, {}

    def give(name, a):
        arrays[name + "_dram"] = a
        aps[name] = nc.dram_tensor(name + "_dram", a.shape, mybir.dt.from_np(a.dtype), kind="ExternalInput").ap()

    for name in _NAMES:
        a = np.ascontiguousarray(inputs[name])
        give(name, a.reshape(B * S, D) if name == "x" else a)
    cos, sin = rope_tables()
    give("rope_cos", cos)
    give("rope_sin", sin)
    out = nc.dram_tensor("out_dram", [B * S, D], mybir.dt.float32, kind="ExternalOutput").ap()
    v = [aps[n] for n in _NAMES]
    build(nc, *v[:8], v[8:12], v[12:16], *v[16:], aps["rope_cos"], aps["rope_sin"], out)
    r = run_bass_kernel_spmd(nc, [arrays], core_ids=[0])
    return r.results[0]["out_dram"].reshape(B, S, D)
```
